# Optimizing a Trainium2 kernel written in Bass

```python
import numpy as np
import jax
import jax.numpy as jnp

def _softmax(x, axis=-1):
    return jax.nn.softmax(x, axis=axis)

def _gelu(x):
    return jax.nn.gelu(x, approximate=True)

def _silu(x):
    return jax.nn.silu(x)

def _sigmoid(x):
    return jax.nn.sigmoid(x)

def _layernorm(x, axis=-1, eps=1e-05):
    m = jnp.mean(x, axis=axis, keepdims=True)
    v = jnp.var(x, axis=axis, keepdims=True)
    return (x - m) / jnp.sqrt(v + eps)

def _scatter_add(tgt, idx, src, axis=0):
    return tgt.at[idx].add(src)

def _segment_sum(src, seg, n):
    return jax.ops.segment_sum(src, seg, n)
kernel_name = 'mk_xattn_ffn_d2_seqx_r8_6bc5bf'

def setup_inputs(seed: int=0):
    np.random.seed(seed)
    _w = jnp.asarray

    def _rec_inputs():
        import jax
        import jax.numpy as jnp
        _rk = jax.random.key(seed)
        x = 0.0002417 + 0.9998 * jax.random.normal(jax.random.fold_in(_rk, 1), (16, 56, 128), jnp.float32)
        _lenS = 56 - jax.random.randint(jax.random.fold_in(_rk, 7), (16,), 0, max(1, 56 // 4) + 1, jnp.int32)
        _lenS2 = 1500 - jax.random.randint(jax.random.fold_in(_rk, 8), (16,), 0, max(1, 1500 // 4) + 1, jnp.int32)
        _ctx_1024P = jax.random.normal(jax.random.fold_in(_rk, 11), (16, 16, 128), jnp.float32)
        _ctx_1024c = jax.random.dirichlet(jax.random.fold_in(_rk, 511), 0.3 * jnp.ones((16,), jnp.float32), (16, 1500))
        _ctx_1024t = jnp.einsum('bsk,bkd->bsd', _ctx_1024c, _ctx_1024P)
        _ctx_1024t = _ctx_1024t * jax.lax.rsqrt(jnp.mean(jnp.square(_ctx_1024t)) + 1e-12) * 0.953939
        ctx_1024 = 7.22013e-05 + 1.00017 * (_ctx_1024t + 0.3 * jax.random.normal(jax.random.fold_in(_rk, 611), (16, 1500, 128), jnp.float32))
        return (x, ctx_1024)
    x, ctx_1024 = _rec_inputs()

    def _L0_xattn_setup():
        import jax, jax.numpy as jnp
        import numpy as np
        EMBED = 128
        HEADS = 16
        HEAD_DIM = EMBED // HEADS
        key = jax.random.key(seed)
        ks = jax.random.split(key, 8)
        N, S = (4, 256)
        inp = {'values': jax.random.normal(ks[0], (N, S, EMBED), dtype=jnp.float32), 'keys': jax.random.normal(ks[1], (N, S, EMBED), dtype=jnp.float32), 'queries': jax.random.normal(ks[2], (N, S, EMBED), dtype=jnp.float32), 'W_v': jax.random.normal(ks[3], (EMBED, EMBED), dtype=jnp.float32) / np.sqrt(EMBED), 'W_k': jax.random.normal(ks[4], (EMBED, EMBED), dtype=jnp.float32) / np.sqrt(EMBED), 'W_q': jax.random.normal(ks[5], (EMBED, EMBED), dtype=jnp.float32) / np.sqrt(EMBED), 'W_o': jax.random.normal(ks[6], (EMBED, EMBED), dtype=jnp.float32) / np.sqrt(EMBED), 'b_o': jax.random.normal(ks[7], (EMBED,), dtype=jnp.float32) * 0.01}
        return inp
    _L0_xattn_all = _L0_xattn_setup()
    _L0_xattn_in = {k: v for k, v in _L0_xattn_all.items() if k in ('W_v', 'W_k', 'W_q', 'W_o', 'b_o')}
    del _L0_xattn_all

    def _L0_ffn_setup():
        import jax, jax.numpy as jnp
        import numpy as np
        BEST_K = 2

        def _expert(xf, w1, w3, w2):
            return jax.nn.silu(xf @ w1) * (xf @ w3) @ w2
        key = jax.random.key(seed)
        ks = jax.random.split(key, 9)
        E, S_sh, D, H = (8, 2, 128, 64)
        B, S = (2, 256)
        w = lambda k, shape: jax.random.normal(k, shape, dtype=jnp.float32) * 0.02
        return {'x': jax.random.normal(ks[0], (B, S, D), dtype=jnp.float32), 'router_w': w(ks[1], (D, E)), 'router_b': jnp.zeros((E,), dtype=jnp.float32), 'routed_w1': w(ks[2], (E, D, H)), 'routed_w3': w(ks[3], (E, D, H)), 'routed_w2': w(ks[4], (E, H, D)), 'shared_w1': w(ks[5], (S_sh, D, H)), 'shared_w3': w(ks[6], (S_sh, D, H)), 'shared_w2': w(ks[7], (S_sh, H, D))}
    _L0_ffn_all = _L0_ffn_setup()
    _L0_ffn_in = {k: v for k, v in _L0_ffn_all.items() if k in ('router_w', 'router_b', 'routed_w1', 'routed_w3', 'routed_w2', 'shared_w1', 'shared_w3', 'shared_w2')}
    del _L0_ffn_all

    def _L1_xattn_setup():
        import jax, jax.numpy as jnp
        import numpy as np
        EPS = 1e-05

        def layer_norm(x, g, b):
            mu = jnp.mean(x, axis=-1, keepdims=True)
            var = jnp.var(x, axis=-1, keepdims=True)
            return (x - mu) * jax.lax.rsqrt(var + EPS) * g + b
        key = jax.random.key(seed)
        ks = jax.random.split(key, 8)
        dim, heads, dim_head = (128, 16, 64)
        inner = heads * dim_head
        b, n, m = (8, 512, 64)
        s = dim ** (-0.5)
        return {'x': jax.random.normal(ks[0], (b, n, dim), jnp.float32), 'latents': jax.random.normal(ks[1], (b, m, dim), jnp.float32), 'ln_m_g': jnp.ones((dim,), jnp.float32), 'ln_m_b': jnp.zeros((dim,), jnp.float32), 'ln_l_g': jnp.ones((dim,), jnp.float32), 'ln_l_b': jnp.zeros((dim,), jnp.float32), 'Wq': jax.random.normal(ks[2], (dim, inner), jnp.float32) * s, 'Wkv': jax.random.normal(ks[3], (dim, 2 * inner), jnp.float32) * s, 'Wout': jax.random.normal(ks[4], (inner, dim), jnp.float32) * s}
    _L1_xattn_all = _L1_xattn_setup()
    _L1_xattn_in = {k: v for k, v in _L1_xattn_all.items() if k in ('ln_m_g', 'ln_m_b', 'ln_l_g', 'ln_l_b', 'Wq', 'Wkv', 'Wout')}
    del _L1_xattn_all

    def _L1_ffn_setup():
        import jax, jax.numpy as jnp
        import numpy as np
        B, S, H, E, K, I = (4, 256, 128, 8, 2, 512)
        GATE_EPS = 1e-06
        LN_EPS = 1e-05
        key = jax.random.key(seed)
        k0, k1, k2, k3 = jax.random.split(key, 4)
        x = jax.random.normal(k0, (B, S, H), jnp.float32)
        gate_w = jax.random.normal(k1, (E, H), jnp.float32) * np.float32(np.sqrt(2.0 / (H + E)))
        expert_bias = jnp.zeros((E,), jnp.float32)
        w_up = jax.random.normal(k2, (E, I, H), jnp.float32) * np.float32(np.sqrt(2.0 / (H + I)))
        w_down = jax.random.normal(k3, (E, H, I), jnp.float32) * np.float32(np.sqrt(2.0 / (H + I)))
        return {'x': x, 'gate_w': gate_w, 'expert_bias': expert_bias, 'w_up': w_up, 'w_down': w_down}
    _L1_ffn_all = _L1_ffn_setup()
    _L1_ffn_in = {k: v for k, v in _L1_ffn_all.items() if k in ('gate_w', 'expert_bias', 'w_up', 'w_down')}
    del _L1_ffn_all
    return {'x': x, 'ctx_1024': ctx_1024, 'L0_xattn_W_v': _L0_xattn_in['W_v'], 'L0_xattn_W_k': _L0_xattn_in['W_k'], 'L0_xattn_W_q': _L0_xattn_in['W_q'], 'L0_xattn_W_o': _L0_xattn_in['W_o'], 'L0_xattn_b_o': _L0_xattn_in['b_o'], 'L0_ffn_router_w': _L0_ffn_in['router_w'], 'L0_ffn_router_b': _L0_ffn_in['router_b'], 'L0_ffn_routed_w1': _L0_ffn_in['routed_w1'], 'L0_ffn_routed_w3': _L0_ffn_in['routed_w3'], 'L0_ffn_routed_w2': _L0_ffn_in['routed_w2'], 'L0_ffn_shared_w1': _L0_ffn_in['shared_w1'], 'L0_ffn_shared_w3': _L0_ffn_in['shared_w3'], 'L0_ffn_shared_w2': _L0_ffn_in['shared_w2'], 'L1_xattn_ln_m_g': _L1_xattn_in['ln_m_g'], 'L1_xattn_ln_m_b': _L1_xattn_in['ln_m_b'], 'L1_xattn_ln_l_g': _L1_xattn_in['ln_l_g'], 'L1_xattn_ln_l_b': _L1_xattn_in['ln_l_b'], 'L1_xattn_Wq': _L1_xattn_in['Wq'], 'L1_xattn_Wkv': _L1_xattn_in['Wkv'], 'L1_xattn_Wout': _L1_xattn_in['Wout'], 'L1_ffn_gate_w': _L1_ffn_in['gate_w'], 'L1_ffn_expert_bias': _L1_ffn_in['expert_bias'], 'L1_ffn_w_up': _L1_ffn_in['w_up'], 'L1_ffn_w_down': _L1_ffn_in['w_down']}

def reference(x, ctx_1024, L0_xattn_W_v, L0_xattn_W_k, L0_xattn_W_q, L0_xattn_W_o, L0_xattn_b_o, L0_ffn_router_w, L0_ffn_router_b, L0_ffn_routed_w1, L0_ffn_routed_w3, L0_ffn_routed_w2, L0_ffn_shared_w1, L0_ffn_shared_w3, L0_ffn_shared_w2, L1_xattn_ln_m_g, L1_xattn_ln_m_b, L1_xattn_ln_l_g, L1_xattn_ln_l_b, L1_xattn_Wq, L1_xattn_Wkv, L1_xattn_Wout, L1_ffn_gate_w, L1_ffn_expert_bias, L1_ffn_w_up, L1_ffn_w_down):
    import jax
    import jax.numpy as jnp

    def _L0_xattn_ref(values, keys, queries, W_v, W_k, W_q, W_o, b_o):
        import jax, jax.numpy as jnp
        import numpy as np
        EMBED = 128
        HEADS = 16
        HEAD_DIM = EMBED // HEADS
        N, q_len, _ = queries.shape
        v = (values @ W_v).reshape(N, -1, HEADS, HEAD_DIM)
        k = (keys @ W_k).reshape(N, -1, HEADS, HEAD_DIM)
        q = (queries @ W_q).reshape(N, -1, HEADS, HEAD_DIM)
        energy = jnp.einsum('nqhd,nkhd->nhqk', q, k) / jnp.sqrt(jnp.float32(EMBED))
        attn = jax.nn.softmax(energy, axis=-1)
        out = jnp.einsum('nhqk,nkhd->nqhd', attn, v).reshape(N, q_len, EMBED)
        return out @ W_o + b_o

    def _L0_ffn_ref(x, router_w, router_b, routed_w1, routed_w3, routed_w2, shared_w1, shared_w3, shared_w2):
        import jax, jax.numpy as jnp
        import numpy as np
        BEST_K = 2

        def _expert(xf, w1, w3, w2):
            return jax.nn.silu(xf @ w1) * (xf @ w3) @ w2
        B, S, D = x.shape
        T = B * S
        xf = x.reshape(T, D)
        logits = xf @ router_w + router_b
        topk_vals, topk_idx = jax.lax.top_k(logits, BEST_K)
        sparse = jnp.full_like(logits, -jnp.inf)
        sparse = sparse.at[jnp.arange(T)[:, None], topk_idx].set(topk_vals)
        gates = jax.nn.softmax(sparse, axis=-1)
        routed = jax.vmap(_expert, in_axes=(None, 0, 0, 0))(xf, routed_w1, routed_w3, routed_w2)
        routed_out = jnp.einsum('etd,te->td', routed, gates)
        shared_out = jax.vmap(_expert, in_axes=(None, 0, 0, 0))(xf, shared_w1, shared_w3, shared_w2).sum(axis=0)
        return (routed_out + shared_out).reshape(B, S, D)

    def _L1_xattn_ref(x, latents, ln_m_g, ln_m_b, ln_l_g, ln_l_b, Wq, Wkv, Wout):
        import jax, jax.numpy as jnp
        import numpy as np
        EPS = 1e-05

        def layer_norm(x, g, b):
            mu = jnp.mean(x, axis=-1, keepdims=True)
            var = jnp.var(x, axis=-1, keepdims=True)
            return (x - mu) * jax.lax.rsqrt(var + EPS) * g + b
        heads, dim_head = (16, 64)
        scale = dim_head ** (-0.5)
        x = layer_norm(x, ln_m_g, ln_m_b)
        lat = layer_norm(latents, ln_l_g, ln_l_b)
        b, m, _ = lat.shape
        q = lat @ Wq
        kv_input = jnp.concatenate([x, lat], axis=1)
        kv = kv_input @ Wkv
        k, v = jnp.split(kv, 2, axis=-1)

        def split_heads(t):
            return t.reshape(t.shape[0], t.shape[1], heads, dim_head).transpose(0, 2, 1, 3)
        q, k, v = (split_heads(q), split_heads(k), split_heads(v))
        dots = jnp.einsum('bhid,bhjd->bhij', q, k) * scale
        attn = jax.nn.softmax(dots, axis=-1)
        out = jnp.einsum('bhij,bhjd->bhid', attn, v)
        out = out.transpose(0, 2, 1, 3).reshape(b, m, heads * dim_head)
        return out @ Wout

    def _L1_ffn_ref(x, gate_w, expert_bias, w_up, w_down):
        import jax, jax.numpy as jnp
        import numpy as np
        B, S, H, E, K, I = (4, 256, 128, 8, 2, 512)
        GATE_EPS = 1e-06
        LN_EPS = 1e-05
        logits = jnp.einsum('bsh,eh->bse', x, gate_w) + expert_bias
        weights = jax.nn.softmax(logits, axis=-1)
        top_w, top_i = jax.lax.top_k(weights, K)
        top_w = top_w / (jnp.sum(top_w, axis=-1, keepdims=True) + GATE_EPS)
        sparse_w = jnp.sum(jax.nn.one_hot(top_i, E, dtype=weights.dtype) * top_w[..., None], axis=-2)
        out = jnp.zeros_like(x)
        for e in range(E):
            h = jax.nn.gelu(jnp.einsum('bsh,ih->bsi', x, w_up[e]), approximate=False)
            y = jnp.einsum('bsi,hi->bsh', h, w_down[e])
            out = out + sparse_w[..., e:e + 1] * y
        mu = jnp.mean(out, axis=-1, keepdims=True)
        var = jnp.mean(jnp.square(out - mu), axis=-1, keepdims=True)
        out = (out - mu) * jax.lax.rsqrt(var + LN_EPS)
        return out + x
    x = x + _L0_xattn_ref(ctx_1024, ctx_1024, _layernorm(x, axis=-1), L0_xattn_W_v, L0_xattn_W_k, L0_xattn_W_q, L0_xattn_W_o, L0_xattn_b_o)
    x = x + _L0_ffn_ref(_layernorm(x, axis=-1), L0_ffn_router_w, L0_ffn_router_b, L0_ffn_routed_w1, L0_ffn_routed_w3, L0_ffn_routed_w2, L0_ffn_shared_w1, L0_ffn_shared_w3, L0_ffn_shared_w2)
    x = x + _L1_xattn_ref(ctx_1024, _layernorm(x, axis=-1), L1_xattn_ln_m_g, L1_xattn_ln_m_b, L1_xattn_ln_l_g, L1_xattn_ln_l_b, L1_xattn_Wq, L1_xattn_Wkv, L1_xattn_Wout)
    x = x + _L1_ffn_ref(_layernorm(x, axis=-1), L1_ffn_gate_w, L1_ffn_expert_bias, L1_ffn_w_up, L1_ffn_w_down)
    return x

_drawn_inputs = setup_inputs


def setup_inputs(seed=0):
    import zlib

    import numpy as np

    out = dict(_drawn_inputs(seed))
    spreads = {'L0_ffn_router_b': (0.0, 0.8),
     'L1_xattn_ln_m_g': (1.0, 0.2),
     'L1_xattn_ln_m_b': (0.0, 0.1),
     'L1_xattn_ln_l_g': (1.0, 0.2),
     'L1_xattn_ln_l_b': (0.0, 0.1),
     'L1_ffn_expert_bias': (0.0, 0.1)}
    factors = {'L0_xattn_b_o': 3.204,
     'L0_ffn_router_w': 5.128,
     'L0_ffn_routed_w1': 8.0,
     'L0_ffn_routed_w3': 8.0,
     'L0_ffn_routed_w2': 6.46,
     'L0_ffn_shared_w1': 3.686,
     'L0_ffn_shared_w3': 3.543,
     'L0_ffn_shared_w2': 2.893}
    for name, (base, spread) in spreads.items():
        noise = np.random.default_rng([zlib.crc32(name.encode()), seed]).standard_normal(out[name].shape)
        drawn = base * np.exp(spread * noise) if base else spread * noise
        out[name] = jnp.asarray(drawn.astype(out[name].dtype))
    for name, factor in factors.items():
        out[name] = (out[name] * factor).astype(out[name].dtype)
    return out
```

```python
from contextlib import ExitStack

import concourse.bass as bass
from concourse import mybir

F32 = mybir.dt.float32
F32R = mybir.dt.float32r
BF16 = mybir.dt.bfloat16
U32 = mybir.dt.uint32
ALU = mybir.AluOpType
ACT = mybir.ActivationFunctionType
AX = mybir.AxisListType

B, NQ, D = 16, 56, 128
NCTX = 1500
KT, KP = 12, 125
HEADS = 16
NTOK = B * NQ
TT = NTOK // 128
HALF = NTOK // 2
HQ = HEADS * NQ
PAIR = 2 * NQ
NJ = HEADS // 2
CH = 500
NC = NCTX // CH
HD0, HD1 = 8, 64
GQ = 4 * NQ
VW = 2 * HD0 + 1
E0, HID0 = 8, 64
E1, I1 = 8, 512
LN_EPS = 1e-5
GATE_EPS = 1e-6
CONSTS = 128 + 4 + 2 + 8


def at_least(eng, sem, count):
    if isinstance(count, int) and count <= 0:
        return
    eng.wait_ge(sem, count)


class Chain:

    def __init__(self, eng, sem):
        self.eng, self.sem, self.n, self.offset = eng, sem, 0, 0

    def link(self, ins):
        self.n += 1
        ins.then_inc(self.sem, 1)
        self.eng.wait_ge(self.sem, self.offset + self.n)


class Ring:

    def __init__(self, banks, names, full, free):
        self.banks, self.full, self.free = banks, full, free
        self.place = {name: k for k, name in enumerate(names)}
        n = len(banks)
        self.uses = [len(range(k, len(names), n)) for k in range(n)]

    def __call__(self, name, rounds=0):
        k = self.place[name]
        slot = k % len(self.banks)
        return self.banks[slot], self.full[slot], self.free[slot], rounds * self.uses[slot] + k // len(self.banks)


def batch_loop(eng, chain, step):
    step(0, 0)
    before = chain.n
    step(1, 1)
    start, stride = chain.n, 2 * (chain.n - before)
    with eng.Fori(1, B // 2 - 1) as i:
        chain.n, chain.offset = start, (i - 1) * stride
        step(2 * i, 0)
        step(2 * i + 1, 1)
    chain.n, chain.offset = start + (B // 2 - 2) * stride, 0
    step(B - 2, 0)
    step(B - 1, 1)


def spread(groups, pieces):
    out, n = [], len(groups)
    for k, g in enumerate(groups):
        out += g
        out += pieces[k * len(pieces) // n:(k + 1) * len(pieces) // n]
    return out


def build(nc, A, out):
    x_tok = A["x"].rearrange("b q d -> (b q) d").rearrange("(t p) d -> p t d", p=128)
    out_tok = out.rearrange("b q d -> (b q) d").rearrange("(t p) d -> p t d", p=128)
    ctx_rows = A["ctx_1024"].rearrange("b (p t) d -> b p t d", p=KP)

    with ExitStack() as outer:
        def tensor(stack, name, shape, dt=F32):
            return stack.enter_context(nc.sbuf_tensor(name, shape, dt))

        def sem(name):
            return outer.enter_context(nc.semaphore(name))

        def sems(name, n):
            return [sem(f"{name}{i}") for i in range(n)]

        ps = outer.enter_context(nc.psum_tensor("ps", [128, 8, 512], F32))

        cst = tensor(outer, "cst", [128, CONSTS])
        ident = cst[:, 0:128]
        group_mask = cst[:, 128:132]
        pair_mask = cst[:, 132:134]
        iota8 = cst[:, 134:142]
        ident_bf = tensor(outer, "ident_bf", [128, 128], BF16)
        x_nat = tensor(outer, "x_nat", [128, TT, D])
        h_nat = tensor(outer, "h_nat", [128, TT, D])
        hT = tensor(outer, "hT", [128, NTOK])
        stats = tensor(outer, "stats", [128, TT, 6])
        mv = tensor(outer, "mv", [128, TT, 2])
        rstd = tensor(outer, "rstd", [128, TT])
        ctx_mv = tensor(outer, "ctx_mv", [KP, B * KT, 2])

        with ExitStack() as l0:
            wq0 = tensor(l0, "wq0", [128, 128])
            wk0 = tensor(l0, "wk0", [128, 128])
            wv0 = tensor(l0, "wv0", [128, 128])
            qT = tensor(l0, "qT", [128, NTOK])
            AT0 = tensor(l0, "AT0", [64, 2, NTOK])
            phase_queries(nc, A, sem, sems, ps, locals())
            phase_attention0(nc, A, sem, sems, ps, locals(), ctx_rows)
            phase_ffn0(nc, A, sem, sems, ps, locals())
        with ExitStack() as l1:
            AT1 = tensor(l1, "AT1", [128, NJ, NTOK])
            phase_attention1(nc, A, sem, sems, ps, locals(), ctx_rows)
            phase_ffn1(nc, A, sem, sems, ps, locals(), out_tok)


def layer_norm(v, chain, act_ready, act_done, round_, src, dst, stats, mv, rstd):
    for t in range(TT):
        last = v.bn_stats(stats[:, t, :], src[:, t, :])
    chain.link(last)
    for t in range(TT):
        last = v.bn_aggr(mv[:, t, :], stats[:, t, :])
    chain.link(last)
    v.tensor_scalar(rstd[:], mv[:, :, 1], LN_EPS, None, ALU.add).then_inc(act_ready, 1)
    v.wait_ge(act_done, round_)
    chain.link(v.reciprocal(rstd[:], rstd[:]))
    for t in range(TT):
        last = v.tensor_scalar(dst[:, t, :], src[:, t, :], mv[:, t, 0:1], rstd[:, t:t + 1], ALU.subtract, ALU.mult)
    chain.link(last)


def transposed_tiles(h):
    return range(0, 4) if h == 0 else range(4, TT)


def phase_queries(nc, A, sem, sems, ps, T):
    cst, ident, ident_bf, x_nat, h_nat, hT, qT = (T[k] for k in "cst ident ident_bf x_nat h_nat hT qT".split())
    const_in, x_in, w0_in = sem("const_in"), sem("x_in"), sem("w0_in")
    var_ready, root_done, norm_ready = sem("q_var_ready"), sem("q_root_done"), sem("q_norm_ready")
    hT_ready, own = sem("q_hT_ready"), sem("q_own")
    q_full, q_used = sem("q_full"), sem("q_used")
    with nc.Block() as block:
        @block.sync
        def _(sp):
            sp.dma_start(cst[:], A["consts"]).then_inc(const_in, 16)
            sp.dma_start(x_nat[:], T["x_tok"]).then_inc(x_in, 16)
            sp.dma_start(T["wq0"][:], A["L0_xattn_W_q"]).then_inc(w0_in, 16)
            sp.dma_start(T["wk0"][:], A["L0_xattn_W_k"]).then_inc(w0_in, 16)
            sp.dma_start(T["wv0"][:], A["L0_xattn_W_v"]).then_inc(w0_in, 16)

        @block.vector
        def _(v):
            chain = Chain(v, own)
            v.wait_ge(const_in, 16)
            v.wait_ge(x_in, 16)
            nc.vector.tensor_copy(ident_bf[:], ident)
            layer_norm(v, chain, var_ready, root_done, 1, x_nat, h_nat, T["stats"], T["mv"], T["rstd"])
            v.sem_inc(norm_ready, 1)
            for h in range(2):
                v.wait_ge(q_full, h + 1)
                n = 128 * len(transposed_tiles(h))
                nc.vector.tensor_copy(hT[:, 512 * h:512 * h + n], ps[:, h, 0:n]).then_inc(hT_ready, 1)

        @block.scalar
        def _(act):
            act.wait_ge(var_ready, 1)
            nc.scalar.activation(T["rstd"][:], T["rstd"][:], ACT.Sqrt).then_inc(root_done, 1)
            for h in range(2):
                act.wait_ge(q_full, h + 3)
                nc.scalar.activation(qT[:, HALF * h:HALF * (h + 1)], ps[:, 2 + h, 0:HALF], ACT.Copy).then_inc(q_used, 1)

        @block.tensor
        def _(pe):
            pe.wait_ge(const_in, 16)
            pe.wait_ge(norm_ready, 1)
            for h in range(2):
                for k, t in enumerate(transposed_tiles(h)):
                    last = nc.tensor.transpose(ps[:, h, 128 * k:128 * (k + 1)], h_nat[:, t, :], ident)
                last.then_inc(q_full, 1)
            pe.wait_ge(w0_in, 48)
            pe.wait_ge(hT_ready, 2)
            for h in range(2):
                nc.tensor.matmul(ps[:, 2 + h, 0:HALF], T["wq0"][:], hT[:, HALF * h:HALF * (h + 1)],
                                 start=True, stop=True).then_inc(q_full, 1)
            pe.wait_ge(q_used, 2)


def phase_attention0(nc, A, sem, sems, ps, T, ctx_rows):
    ident, ident_bf, qT, AT0, ctx_mv = (T[k] for k in "ident ident_bf qT AT0 ctx_mv".split())
    SCALE = 1.0 / float(D) ** 0.5
    NP = KT // 2
    with ExitStack() as st:
        def sb(name, shape, dt=F32):
            return st.enter_context(nc.sbuf_tensor(name, shape, dt))
        ctx = [sb(f"a_ctx{s}", [KP, KT, D]) for s in range(2)]
        ctxT = sb("a_ctxT", [128, NCTX])
        kT_hi = [sb(f"a_kT_hi{s}", [128, NCTX], F32R) for s in range(2)]
        kT_lo = [sb(f"a_kT_lo{s}", [128, NCTX], F32R) for s in range(2)]
        kT_bf = sb("a_kT_bf", [128, NCTX], BF16)
        vals = [sb(f"a_vals{s}", [KP, KT, NJ, VW]) for s in range(2)]
        q_f = sb("a_q_f", [128, 4, NQ])
        q_hi = [sb(f"a_q_hi{s}", [128, 4, NQ], F32R) for s in range(2)]
        q_lo = [sb(f"a_q_lo{s}", [128, 4, NQ], F32R) for s in range(2)]
        q_bf = sb("a_q_bf", [128, 4 * NQ], BF16)
        mx = sb("a_mx", [PAIR, NJ, NC])
        negm = sb("a_negm", [PAIR, NJ], BF16)
        negm_rep = sb("a_negm_rep", [PAIR, NJ, 32], BF16)
        mrow = [sb(f"a_mrow{s}", [128, GQ], BF16) for s in range(2)]
        ones = sb("a_ones", [128, KP], BF16)
        P = [sb(f"a_P{s}", [KP, 4, 2, GQ]) for s in range(2)]
        c_st = sb("a_c_st", [KP, KT, 6])
        c_mv = sb("a_c_mv", [KP, KT, 2])
        rden = sb("a_rden", [PAIR, NJ])
        o_sel = sb("a_o_sel", [PAIR, NJ, HD0])
        o_nat = sb("a_o_nat", [PAIR, 2 * NJ, HD0])

        ctx_in = sems("a_ctx_in", 2)
        ctx_measured = sem("a_ctx_measured")
        load_turn, pool_turn = sem("a_load_turn"), sem("a_pool_turn")
        aux_full, aux_free = sems("a_aux_full", 3), sems("a_aux_free", 3)
        k_hi_ready, k_bf_ready, q_ready, negm_ready = (sem("a_" + n) for n in
                                                       "k_hi_ready k_bf_ready q_ready negm_ready".split())
        ones_ready = sem("a_ones_ready")
        s_full, exp_done = sems("a_s_full", 2), sems("a_exp_done", 2)
        pv_done, o_ready, oT_full, o_free = (sem("a_" + n) for n in "pv_done o_ready oT_full o_free".split())
        own_v = sem("a_own_v")

        names = [("ctxT", c) for c in range(NC)] + [("k", c) for c in range(NC)] + [("v", c) for c in range(NC)] \
            + [("max", c, j) for c in range(NC) for j in range(NJ)] + [("row",)]
        ring = Ring([5, 6, 7], names, aux_full, aux_free)

        def order(b):
            groups = [[("scores", u)] + ([("finish",)] if u == 1 and not (isinstance(b, int) and b == 0) else [])
                      + ([("weigh", u - 1)] if u else []) for u in range(NP)] + [[("weigh", NP - 1)]]
            last = isinstance(b, int) and b == B - 1
            return spread(groups, [] if last else [("prepare", n) for n in names])

        with nc.Block() as block:
            @block.sync
            def _(sp):
                def load(b, s):
                    if not (isinstance(b, int) and b < 2):
                        bank, full, free, u = ring(("ctxT", NC - 1), b - 2)
                        sp.wait_ge(free, u + 1)
                        sp.sem_inc(load_turn, 1)
                        sp.wait_ge(ctx_measured, b - 1)
                    sp.dma_start(ctx[s][:], ctx_rows[b]).then_inc(ctx_in[s], 16)
                load(0, 0)
                load(1, 1)
                with sp.Fori(1, B // 2) as i:
                    load(2 * i, 0)
                    load(2 * i + 1, 1)

            @block.gpsimd
            def _(pool):
                for s in range(2):
                    nc.gpsimd.memset(vals[s][:, :, :, VW - 1:VW], 1.0)
                nc.gpsimd.memset(o_nat[:, NJ:, :], 0.0)
                nc.gpsimd.memset(ones[:], 1.0).then_inc(ones_ready, 1)

                def step(b, s):
                    for c in range(NC):
                        pool.wait_ge(k_hi_ready, b * NC + c + 1)
                        pool.sem_inc(pool_turn, 1)
                        nc.gpsimd.tensor_copy(kT_bf[:, c * CH:(c + 1) * CH],
                                              kT_hi[s][:, c * CH:(c + 1) * CH].bitcast(F32)).then_inc(k_bf_ready, 1)
                step(0, 0)
                step(1, 1)
                with pool.Fori(1, B // 2) as i:
                    step(2 * i, 0)
                    step(2 * i + 1, 1)

            @block.vector
            def _(v):
                chain = Chain(v, own_v)

                def prepare(b, s):
                    at_least(v, pv_done, NP * (b - 1))
                    chain.link(nc.vector.tensor_tensor(
                        q_f[:], T["group_mask"].unsqueeze(2).broadcast_to((128, 4, NQ)),
                        qT[:, bass.ds(b * NQ, NQ)].unsqueeze(1).broadcast_to((128, 4, NQ)), ALU.mult))
                    chain.link(nc.vector.tensor_copy(q_hi[s][:], q_f[:]))
                    nc.vector.tensor_copy(q_bf[:].rearrange("p (h q) -> p h q", h=4), q_f[:])
                    nc.vector.tensor_tensor(q_lo[s][:], q_f[:], q_hi[s][:].bitcast(F32), ALU.subtract).then_inc(q_ready, 1)
                    v.wait_ge(ctx_in[s], 8 * (b - s) + 16)
                    for t in range(KT):
                        last = nc.vector.bn_stats(c_st[:, t, :], ctx[s][:, t, :])
                    last.then_inc(ctx_measured, 1)
                    v.wait_ge(ctx_measured, b + 1)
                    for c in range(NC):
                        bank, full, free, u = ring(("k", c), b)
                        v.wait_ge(k_hi_ready, b * NC + c + 1)
                        nc.vector.tensor_tensor(kT_lo[s][:, c * CH:(c + 1) * CH], ps[:, bank, 0:CH],
                                                kT_hi[s][:, c * CH:(c + 1) * CH].bitcast(F32),
                                                ALU.subtract).then_inc(free, 1)
                    for t in range(KT):
                        last = nc.vector.bn_aggr(c_mv[:, t, :], c_st[:, t, :])
                    chain.link(last)
                    nc.vector.tensor_copy(ctx_mv[:, bass.ds(b * KT, KT), :], c_mv[:])
                    for c in range(NC):
                        for j in range(NJ):
                            bank, full, free, u = ring(("max", c, j), b)
                            v.wait_ge(full, u + 1)
                            nc.vector.tensor_reduce(mx[:, j, c:c + 1], ps[0:PAIR, bank, 0:CH], AX.X,
                                                    ALU.max).then_inc(free, 1)
                            if c == NC - 1 and j == NJ - 1:
                                v.wait_ge(free, u + 1)
                    chain.link(nc.vector.tensor_reduce(negm[:], mx[:], AX.X, ALU.max, negate=True))
                    nc.vector.tensor_copy(negm_rep[:], negm[:].unsqueeze(2).broadcast_to((PAIR, NJ, 32))).then_inc(negm_ready, 1)
                    bank, full, free, u = ring(("row",), b)
                    v.wait_ge(full, u + 1)
                    nc.vector.tensor_copy(mrow[s][:], ps[:, bank, 0:GQ]).then_inc(free, 1)

                def finish(b, s):
                    v.wait_ge(pv_done, NP * (b + 1))
                    o = ps[0:PAIR, 4, 0:NJ * VW].rearrange("p (j w) -> p j w", j=NJ)
                    nc.vector.tensor_scalar(o_sel[:], o[:, :, 0:HD0], T["pair_mask"][0:PAIR, 0:1], None, ALU.mult)
                    chain.link(nc.vector.reciprocal(rden[:], o[:, :, VW - 1]))
                    chain.link(nc.vector.scalar_tensor_tensor(o_sel[:], o[:, :, HD0:2 * HD0], T["pair_mask"][0:PAIR, 1:2],
                                                              o_sel[:], ALU.mult, ALU.add))
                    nc.vector.tensor_tensor(o_nat[:, 0:NJ, :], o_sel[:], rden[:].unsqueeze(2).broadcast_to((PAIR, NJ, HD0)),
                                            ALU.mult).then_inc(o_ready, 1)

                def step(b, s):
                    if not (isinstance(b, int) and b == 0):
                        finish(b - 1, 1 - s)
                    if not (isinstance(b, int) and b == B - 1):
                        prepare(b + 1, 1 - s)
                prepare(0, 0)
                batch_loop(v, chain, step)
                finish(B - 1, 1)

            @block.scalar
            def _(act):
                def prepare(b, s, name):
                    kind = name[0]
                    if kind not in ("ctxT", "k", "v"):
                        return
                    c = name[1]
                    bank, full, free, u = ring(name, b)
                    act.wait_ge(full, u + 1)
                    cols = slice(c * CH, (c + 1) * CH)
                    if kind == "ctxT":
                        nc.scalar.activation(ctxT[:, cols], ps[:, bank, 0:CH], ACT.Copy).then_inc(free, 1)
                    elif kind == "k":
                        nc.scalar.activation(kT_hi[s][:, cols], ps[:, bank, 0:CH], ACT.Copy).then_inc(k_hi_ready, 1)
                    else:
                        nc.scalar.activation(
                            vals[s][:, 4 * c:4 * c + 4, :, 0:2 * HD0],
                            ps[0:KP, bank, :].rearrange("p (t j w) -> p t j w", t=4, j=NJ), ACT.Copy).then_inc(free, 1)

                def finish(b):
                    act.wait_ge(oT_full, b + 1)
                    nc.scalar.activation(AT0[:, :, bass.ds(b * NQ, NQ)],
                                         ps[0:64, 4, 256:256 + PAIR].rearrange("p (a q) -> p a q", a=2),
                                         ACT.Copy).then_inc(o_free, 1)

                def step(b, s):
                    for item in order(b):
                        if item[0] == "scores":
                            n = b * NP + item[1]
                            at_least(act, pv_done, n - 1)
                            for h in range(2):
                                act.wait_ge(s_full[h], n + 1)
                                nc.scalar.activation(P[item[1] % 2][:, 2 * h:2 * h + 2].rearrange("p g a c -> p g (a c)"),
                                                     ps[0:KP, 2 * h:2 * h + 2, 0:2 * GQ], ACT.Exp,
                                                     scale=SCALE).then_inc(exp_done[h], 1)
                        elif item[0] == "finish":
                            finish(b - 1)
                        elif item[0] == "prepare":
                            prepare(b + 1, 1 - s, item[1])
                for n in names:
                    prepare(0, 0, n)
                batch_loop(act, Chain(act, None), step)
                finish(B - 1)

            @block.tensor
            def _(pe):
                def prepare(b, s, name):
                    kind = name[0]
                    bank, full, free, u = ring(name, b)
                    at_least(pe, free, u)
                    if kind == "ctxT":
                        c = name[1]
                        if c == 0:
                            pe.wait_ge(ctx_in[s], 8 * (b - s) + 16)
                        for k in range(4):
                            last = nc.tensor.transpose(ps[:, bank, KP * k:KP * (k + 1)], ctx[s][:, 4 * c + k, :],
                                                       ident[0:KP, 0:KP])
                        last.then_inc(full, 1)
                    elif kind == "k":
                        c = name[1]
                        _, _, free_t, ut = ring(("ctxT", c), b)
                        pe.wait_ge(free_t, ut + 1)
                        nc.tensor.matmul(ps[:, bank, 0:CH], T["wk0"][:], ctxT[:, c * CH:(c + 1) * CH],
                                         start=True, stop=True).then_inc(full, 1)
                    elif kind == "v":
                        c = name[1]
                        for k in range(4):
                            last = nc.tensor.matmul(ps[0:KP, bank, 128 * k:128 * (k + 1)],
                                                    ctxT[:, (4 * c + k) * KP:(4 * c + k + 1) * KP], T["wv0"][:],
                                                    start=True, stop=True)
                        last.then_inc(full, 1)
                    elif kind == "max":
                        c, j = name[1:]
                        if j == 0:
                            pe.wait_ge(k_bf_ready, b * NC + c + 1)
                            pe.wait_ge(q_ready, b + 1)
                        g = j // 2
                        nc.tensor.matmul(ps[0:PAIR, bank, 0:CH], q_bf[32 * g:32 * g + 32, (j % 2) * PAIR:(j % 2 + 1) * PAIR],
                                         kT_bf[32 * g:32 * g + 32, c * CH:(c + 1) * CH],
                                         start=True, stop=True).then_inc(full, 1)
                    elif kind == "row":
                        pe.wait_ge(negm_ready, b + 1)
                        for j in range(NJ):
                            g = j // 2
                            last = nc.tensor.matmul(ps[32 * g:32 * g + 32, bank, (j % 2) * PAIR:(j % 2 + 1) * PAIR],
                                                    negm_rep[:, j, :], ident_bf[0:PAIR, 0:PAIR], start=True, stop=True)
                        last.then_inc(full, 1)

                def step(b, s):
                    for item in order(b):
                        if item[0] == "scores":
                            u = item[1]
                            n = b * NP + u
                            if u == 0:
                                _, _, free, ur = ring(("row",), b)
                                pe.wait_ge(free, ur + 1)
                                pe.wait_ge(q_ready, b + 1)
                            for g in range(4):
                                if g % 2 == 0:
                                    at_least(pe, exp_done[g // 2], n)
                                rows = slice(32 * g, 32 * g + 32)
                                for a in range(2):
                                    o = ps[0:KP, g, a * GQ:(a + 1) * GQ]
                                    keys = slice((2 * u + a) * KP, (2 * u + a + 1) * KP)
                                    hi, lo = kT_hi[s][rows, keys], kT_lo[s][rows, keys]
                                    qh = q_hi[s][rows].rearrange("p h q -> p (h q)")
                                    ql = q_lo[s][rows].rearrange("p h q -> p (h q)")
                                    nc.tensor.matmul(o, ones[32 * g:32 * g + 1, :], mrow[s][32 * g:32 * g + 1, :],
                                                     start=True, stop=False)
                                    nc.tensor.matmul(o, hi, qh, start=False, stop=False)
                                    nc.tensor.matmul(o, hi, ql, start=False, stop=False)
                                    last = nc.tensor.matmul(o, lo, qh, start=False, stop=True)
                                if g % 2:
                                    last.then_inc(s_full[g // 2], 1)
                        elif item[0] == "weigh":
                            u = item[1]
                            n = b * NP + u
                            if u == 0:
                                at_least(pe, o_free, b)
                            pe.wait_ge(exp_done[0], n + 1)
                            pe.wait_ge(exp_done[1], n + 1)
                            for a in range(2):
                                t = 2 * u + a
                                for j in range(NJ):
                                    last = nc.tensor.matmul(
                                        ps[0:PAIR, 4, j * VW:(j + 1) * VW],
                                        P[u % 2][:, j // 2, a, (j % 2) * PAIR:(j % 2 + 1) * PAIR], vals[s][:, t, j, :],
                                        start=(t == 0 and j == 0), stop=(t == KT - 1), skip_group_check=True)
                            last.then_inc(pv_done, 1)
                        elif item[0] == "finish":
                            finish(b - 1)
                        else:
                            prepare(b + 1, 1 - s, item[1])

                def finish(b):
                    pe.wait_ge(o_ready, b + 1)
                    nc.tensor.transpose(ps[:, 4, 256:256 + PAIR], o_nat[:].rearrange("p j d -> p (j d)"),
                                        ident[0:PAIR, 0:PAIR]).then_inc(oT_full, 1)

                pe.wait_ge(ones_ready, 1)
                for n in names:
                    prepare(0, 0, n)
                batch_loop(pe, Chain(pe, None), step)
                finish(B - 1)


def phase_ffn0(nc, A, sem, sems, ps, T):
    ident, x_nat, h_nat, hT, AT0 = (T[k] for k in "ident x_nat h_nat hT AT0".split())
    EP = E0 // 2 + 1
    with ExitStack() as st:
        def sb(name, shape, dt=F32):
            return st.enter_context(nc.sbuf_tensor(name, shape, dt))
        wo = sb("f_wo", [64, 2, D])
        bo = sb("f_bo", [128, D])
        rw = sb("f_rw", [128, E0])
        rb = sb("f_rb", [128, E0])
        w1 = sb("f_w1", [128, 2 * EP, HID0])
        w3 = sb("f_w3", [128, 2 * EP, HID0])
        w2 = sb("f_w2", [128, EP, D])
        act_sb = sb("f_act", [128, 2, HALF])
        H = sb("f_H", [128, EP, NTOK])
        lg = sb("f_lg", [128, TT, E0])
        top = sb("f_top", [128, TT, 8])
        idx = sb("f_idx", [128, TT, 8], U32)
        idxf = sb("f_idxf", [128, TT, 8])
        hit = sb("f_hit", [128, TT, 2, E0])
        gate = sb("f_gate", [128, TT, E0])
        gsum = sb("f_gsum", [128, TT])

        w_in, small_in = sem("f_w_in"), sem("f_small_in")
        var_ready, root_done, own = sem("f_var_ready"), sem("f_root_done"), sem("f_own")
        norm_ready, hT_ready, exp_ready, exp_done, act_ready, H_ready = (
            sem("f_" + n) for n in "norm_ready hT_ready exp_ready exp_done act_ready H_ready".split())
        full, free = sems("f_full", 8), sems("f_free", 8)
        names = [("o", t) for t in range(TT)] + [("T", h) for h in range(2)] + [("lg",)] \
            + [(w, e, h) for e in range(EP) for h in range(2) for w in "ab"] \
            + [("y", t, k) for t in range(TT) for k in range(3)]
        ring = Ring(list(range(8)), names, full, free)

        with nc.Block() as block:
            @block.sync
            def _(sp):
                wo_rows = A["L0_xattn_W_o"].rearrange("(j a d) n -> a j d n", a=2, d=HD0)
                for a in range(2):
                    for j in range(NJ):
                        sp.dma_start(wo[HD0 * j:HD0 * (j + 1), a, :], wo_rows[a, j]).then_inc(small_in, 16)
                sp.dma_start(bo[:], A["L0_xattn_b_o"].rearrange("(a n) -> a n", a=1).broadcast_to((128, D))).then_inc(small_in, 16)
                sp.dma_start(rb[:], A["L0_ffn_router_b"].rearrange("(a n) -> a n", a=1).broadcast_to((128, E0))).then_inc(small_in, 16)
                sp.dma_start(rw[:], A["L0_ffn_router_w"]).then_inc(small_in, 16)
                for w, name in ((w1, "w1"), (w3, "w3")):
                    sp.dma_start(w[:, 0:E0, :], A["L0_ffn_routed_" + name].rearrange("e d h -> d e h")).then_inc(w_in, 16)
                    sp.dma_start(w[:, E0:, :], A["L0_ffn_shared_" + name].rearrange("e d h -> d e h")).then_inc(w_in, 16)
                sp.dma_start(w2[:, 0:EP - 1, :], A["L0_ffn_routed_w2"].rearrange("(k e) h d -> (e h) k d", e=2)).then_inc(w_in, 16)
                sp.dma_start(w2[:, EP - 1, :], A["L0_ffn_shared_w2"].rearrange("e h d -> (e h) d")).then_inc(w_in, 16)

            @block.vector
            def _(v):
                chain = Chain(v, own)
                v.wait_ge(small_in, 16 * (2 * NJ + 3))
                for t in range(TT):
                    bank, fu, fr, u = ring(("o", t))
                    v.wait_ge(fu, u + 1)
                    last = nc.vector.tensor_tensor(x_nat[:, t, :], x_nat[:, t, :], ps[:, bank, 0:D], ALU.add)
                    last.then_inc(fr, 1)
                    v.wait_ge(fr, u + 1)
                    last = nc.vector.tensor_tensor(x_nat[:, t, :], x_nat[:, t, :], bo[:], ALU.add)
                chain.link(last)
                layer_norm(v, chain, var_ready, root_done, 1, x_nat, h_nat, T["stats"], T["mv"], T["rstd"])
                v.sem_inc(norm_ready, 1)
                for h in range(2):
                    bank, fu, fr, u = ring(("T", h))
                    v.wait_ge(fu, u + 1)
                    n = 128 * len(transposed_tiles(h))
                    nc.vector.tensor_copy(hT[:, 512 * h:512 * h + n], ps[:, bank, 0:n]).then_inc(fr, 1)
                bank, fu, fr, u = ring(("lg",))
                v.wait_ge(fu, u + 1)
                nc.vector.tensor_tensor(lg[:], ps[:, bank, 0:TT * E0].rearrange("p (t e) -> p t e", t=TT),
                                        rb[:].unsqueeze(1).broadcast_to((128, TT, E0)), ALU.add).then_inc(fr, 1)
                v.wait_ge(fr, u + 1)
                top2(nc, chain, T["iota8"], lg, top, idx, idxf, hit)
                chain.link(nc.vector.tensor_tensor(lg[:], lg[:], top[:, :, 0:1].broadcast_to((128, TT, E0)), ALU.subtract))
                v.sem_inc(exp_ready, 1)
                v.wait_ge(exp_done, 1)
                chain.link(nc.vector.tensor_tensor(gate[:], lg[:], hit[:, :, 0, :], ALU.mult))
                chain.link(nc.vector.tensor_reduce(gsum[:], gate[:], AX.X, ALU.add))
                chain.link(nc.vector.reciprocal(gsum[:], gsum[:]))
                chain.link(nc.vector.tensor_tensor(gate[:], gate[:], gsum[:].unsqueeze(2).broadcast_to((128, TT, E0)), ALU.mult))
                for e in range(EP):
                    for h in range(2):
                        bank, fu, fr, u = ring(("b", e, h))
                        v.wait_ge(act_ready, 2 * e + h + 1)
                        v.wait_ge(fu, u + 1)
                        nc.vector.tensor_tensor(H[:, e, h * HALF:(h + 1) * HALF], act_sb[:, h, :], ps[:, bank, 0:HALF],
                                                ALU.mult).then_inc(fr, 1)
                        v.wait_ge(fr, u + 1)
                        v.sem_inc(H_ready, 1)
                for t in range(TT):
                    bank, fu, fr, u = ring(("y", t, 2))
                    v.wait_ge(fu, u + 1)
                    nc.vector.tensor_tensor(x_nat[:, t, :], x_nat[:, t, :], ps[:, bank, 0:D], ALU.add).then_inc(fr, 1)
                    v.wait_ge(fr, u + 1)
                    for k in range(2):
                        bank, fu, fr, u = ring(("y", t, k))
                        v.wait_ge(fu, u + 1)
                        for e in range(4):
                            i = nc.vector.scalar_tensor_tensor(x_nat[:, t, :], ps[:, bank, D * e:D * (e + 1)],
                                                               gate[:, t, 2 * e + k:2 * e + k + 1], x_nat[:, t, :],
                                                               ALU.mult, ALU.add)
                            if e < 3:
                                chain.link(i)
                        i.then_inc(fr, 1)
                        v.wait_ge(fr, u + 1)

            @block.scalar
            def _(act):
                act.wait_ge(var_ready, 1)
                nc.scalar.activation(T["rstd"][:], T["rstd"][:], ACT.Sqrt).then_inc(root_done, 1)
                act.wait_ge(exp_ready, 1)
                nc.scalar.activation(lg[:], lg[:], ACT.Exp).then_inc(exp_done, 1)
                for e in range(EP):
                    for h in range(2):
                        bank, fu, fr, u = ring(("a", e, h))
                        act.wait_ge(fu, u + 1)
                        at_least(act, H_ready, 2 * e + h - 1)
                        nc.scalar.activation(act_sb[:, h, :], ps[:, bank, 0:HALF], ACT.Silu).then_inc(fr, 1)
                        act.wait_ge(fr, u + 1)
                        act.sem_inc(act_ready, 1)

            @block.tensor
            def _(pe):
                def claim(name):
                    bank, fu, fr, u = ring(name)
                    at_least(pe, fr, u)
                    return bank, fu
                pe.wait_ge(small_in, 16 * (2 * NJ + 3))
                for t in range(TT):
                    bank, fu = claim(("o", t))
                    for a in range(2):
                        last = nc.tensor.matmul(ps[:, bank, 0:D], AT0[:, a, 128 * t:128 * (t + 1)], wo[:, a, :],
                                                start=(a == 0), stop=(a == 1))
                    last.then_inc(fu, 1)
                pe.wait_ge(norm_ready, 1)
                for h in range(2):
                    bank, fu = claim(("T", h))
                    for k, t in enumerate(transposed_tiles(h)):
                        last = nc.tensor.transpose(ps[:, bank, 128 * k:128 * (k + 1)], h_nat[:, t, :], ident)
                    last.then_inc(fu, 1)
                for h in range(2):
                    _, _, fr, u = ring(("T", h))
                    pe.wait_ge(fr, u + 1)
                bank, fu = claim(("lg",))
                for t in range(TT):
                    last = nc.tensor.matmul(ps[:, bank, E0 * t:E0 * (t + 1)], hT[:, 128 * t:128 * (t + 1)], rw[:],
                                            start=True, stop=True)
                last.then_inc(fu, 1)
                pe.wait_ge(w_in, 16 * 6)
                for e in range(EP):
                    for h in range(2):
                        for w, wt in (("a", w1), ("b", w3)):
                            bank, fu = claim((w, e, h))
                            nc.tensor.matmul(ps[:, bank, 0:HALF], wt[:, 2 * e:2 * e + 2, :].rearrange("p e h -> p (e h)"),
                                             hT[:, h * HALF:(h + 1) * HALF], start=True, stop=True).then_inc(fu, 1)
                pe.wait_ge(H_ready, 2 * EP)
                for t in range(TT):
                    tok = slice(128 * t, 128 * (t + 1))
                    for k in range(3):
                        bank, fu = claim(("y", t, k))
                        if k < 2:
                            for e in range(4):
                                last = nc.tensor.matmul(ps[:, bank, D * e:D * (e + 1)], H[64 * k:64 * k + 64, e, tok],
                                                        w2[64 * k:64 * k + 64, e, :], start=True, stop=True)
                        else:
                            last = nc.tensor.matmul(ps[:, bank, 0:D], H[:, EP - 1, tok], w2[:, EP - 1, :],
                                                    start=True, stop=True)
                        last.then_inc(fu, 1)


def phase_attention1(nc, A, sem, sems, ps, T, ctx_rows):
    ident, ident_bf, x_nat, h_nat, ctx_mv, AT1 = (T[k] for k in "ident ident_bf x_nat h_nat ctx_mv AT1".split())
    SCALE = float(HD1) ** -0.5
    INNER = HEADS * HD1
    NT = KT + 1
    with ExitStack() as st:
        def sb(name, shape, dt=F32, stack=st):
            return stack.enter_context(nc.sbuf_tensor(name, shape, dt))
        wkT = [sb(f"b_wkT{i}", [128, NJ, 128]) for i in range(2)]
        wv = [sb(f"b_wv{i}", [128, HEADS, HD1 + 1]) for i in range(2)]
        wq = sb("b_wq", [128, INNER])
        lT = sb("b_lT", [128, NTOK])
        ctx_r = sb("b_ctx_r", [KP, B * KT])

        with ExitStack() as pre:
            wq_raw = sb("b_wq_raw", [128, INNER], stack=pre)
            wkv_raw = sb("b_wkv_raw", [128, 2 * INNER], stack=pre)
            gb = sb("b_gb", [128, 4], stack=pre)
            M = [sb(f"b_M{i}", [128, 128], stack=pre) for i in range(2)]
            ones = sb("b_ones", [1, 128], stack=pre)
            w_in, gb_in, own = sem("w_w_in"), sem("w_gb_in"), sem("w_own")
            var_ready, root_done, M_ready, l_ready = (sem("w_" + n) for n in "var_ready root_done M_ready l_ready".split())
            full, free = sems("w_full", 8), sems("w_free", 8)
            names = [("wkT", i, h) for i in range(2) for h in range(2)] + [("wv", i, h) for i in range(2) for h in range(2)] \
                + [("wq", h) for h in range(2)] + [("T", h) for h in range(2)]
            ring = Ring(list(range(8)), names, full, free)
            with nc.Block() as block:
                @block.sync
                def _(sp):
                    for k, n in enumerate(("ln_m_g", "ln_m_b", "ln_l_g", "ln_l_b")):
                        sp.dma_start(gb[:, k:k + 1], A["L1_xattn_" + n].rearrange("(p a) -> p a", a=1)).then_inc(gb_in, 16)
                    sp.dma_start(wkv_raw[:], A["L1_xattn_Wkv"]).then_inc(w_in, 16)
                    sp.dma_start(wq_raw[:], A["L1_xattn_Wq"]).then_inc(w_in, 16)

                @block.vector
                def _(v):
                    chain = Chain(v, own)
                    nc.vector.memset(ones[:], 1.0)
                    for i in range(2):
                        last = nc.vector.memset(wv[i][:, :, HD1:], 0.0)
                    chain.link(last)
                    for i in range(2):
                        last = nc.vector.memset(wv[i][0:1, :, HD1:], 1.0)
                    v.wait_ge(gb_in, 64)
                    for i in range(2):
                        last = nc.vector.tensor_scalar(M[i][:], ident, gb[:, 2 * i:2 * i + 1], None, ALU.mult)
                    chain.link(last)
                    for i in range(2):
                        nc.vector.tensor_scalar(M[i][0:1, 1:128], ones[:, 1:128], gb[0:1, 2 * i:2 * i + 1], -1.0,
                                                ALU.mult, ALU.mult)
                        last = nc.vector.tensor_copy(M[i][:, 0:1], gb[:, 2 * i + 1:2 * i + 2])
                    last.then_inc(M_ready, 1)
                    chain.link(nc.vector.tensor_scalar(ctx_r[:], ctx_mv[:, :, 1], LN_EPS, None, ALU.add))
                    layer_norm(v, chain, var_ready, root_done, 1, x_nat, h_nat, T["stats"], T["mv"], T["rstd"])
                    layer_norm(v, chain, var_ready, root_done, 2, h_nat, h_nat, T["stats"], T["mv"], T["rstd"])
                    nc.vector.memset(h_nat[:, :, 0:1], 1.0).then_inc(l_ready, 1)
                    v.wait_ge(root_done, 3)
                    nc.vector.reciprocal(ctx_r[:], ctx_r[:])
                    for h in range(2):
                        bank, fu, fr, u = ring(("T", h))
                        v.wait_ge(fu, u + 1)
                        n = 128 * len(transposed_tiles(h))
                        nc.vector.tensor_copy(lT[:, 512 * h:512 * h + n], ps[:, bank, 0:n]).then_inc(fr, 1)

                @block.scalar
                def _(act):
                    for r in range(2):
                        act.wait_ge(var_ready, r + 1)
                        nc.scalar.activation(T["rstd"][:], T["rstd"][:], ACT.Sqrt).then_inc(root_done, 1)
                    nc.scalar.activation(ctx_r[:], ctx_r[:], ACT.Sqrt).then_inc(root_done, 1)
                    for name in names:
                        bank, fu, fr, u = ring(name)
                        if name[0] == "T":
                            continue
                        act.wait_ge(fu, u + 1)
                        h = name[-1]
                        if name[0] == "wkT":
                            dst = wkT[name[1]][:, 4 * h:4 * h + 4, :].rearrange("p j f -> p (j f)")
                            src = ps[:, bank, :]
                        elif name[0] == "wv":
                            dst = wv[name[1]][:, 8 * h:8 * h + 8, 0:HD1]
                            src = ps[:, bank, :].rearrange("p (j d) -> p j d", j=8)
                        else:
                            dst, src = wq[:, 512 * h:512 * (h + 1)], ps[:, bank, :]
                        nc.scalar.activation(dst, src, ACT.Copy).then_inc(fr, 1)

                @block.tensor
                def _(pe):
                    pe.wait_ge(w_in, 32)
                    pe.wait_ge(M_ready, 1)
                    for name in names:
                        bank, fu, fr, u = ring(name)
                        at_least(pe, fr, u)
                        h = name[-1]
                        if name[0] == "wkT":
                            for k in range(4):
                                j = 4 * h + k
                                last = nc.tensor.matmul(ps[:, bank, 128 * k:128 * (k + 1)],
                                                        wkv_raw[:, 128 * j:128 * (j + 1)], M[name[1]][:], start=True, stop=True)
                        elif name[0] == "wv":
                            last = nc.tensor.matmul(ps[:, bank, :], M[name[1]][:],
                                                    wkv_raw[:, INNER + 512 * h:INNER + 512 * (h + 1)], start=True, stop=True)
                        elif name[0] == "wq":
                            last = nc.tensor.matmul(ps[:, bank, :], M[1][:], wq_raw[:, 512 * h:512 * (h + 1)],
                                                    start=True, stop=True)
                        else:
                            if h == 0:
                                pe.wait_ge(l_ready, 1)
                            for k, t in enumerate(transposed_tiles(h)):
                                last = nc.tensor.transpose(ps[:, bank, 128 * k:128 * (k + 1)], h_nat[:, t, :], ident)
                        last.then_inc(fu, 1)

        ctx = [sb(f"b_ctx{s}", [KP, KT, D]) for s in range(2)]
        c_mv = sb("b_c_mv", [KP, KT, 2])
        y = [sb(f"b_y{s}", [KP, KT, D]) for s in range(2)]
        yT_hi = [sb(f"b_yT_hi{s}", [128, NCTX], F32R) for s in range(2)]
        yT_lo = [sb(f"b_yT_lo{s}", [128, NCTX], F32R) for s in range(2)]
        yT_bf = sb("b_yT_bf", [128, NCTX], BF16)
        l_f = sb("b_l_f", [128, NQ])
        l_hi = [sb(f"b_l_hi{s}", [128, 128], F32R) for s in range(2)]
        l_lo = [sb(f"b_l_lo{s}", [128, 128], F32R) for s in range(2)]
        l_bf = sb("b_l_bf", [128, NQ], BF16)
        l_nat = [sb(f"b_l_nat{s}", [NQ, D]) for s in range(2)]
        q_f = sb("b_q_f", [128, NJ, NQ])
        Q_f = [sb(f"b_Q_f{i}", [128, NJ, 2, NQ]) for i in range(2)]
        Q_bf = [sb(f"b_Q_bf{i}", [128, HQ], BF16) for i in range(2)]
        Q_hi = [[sb(f"b_Q_hi{s}{i}", [128, HQ], F32R) for i in range(2)] for s in range(2)]
        Q_lo = [[sb(f"b_Q_lo{s}{i}", [128, HQ], F32R) for i in range(2)] for s in range(2)]
        mx = sb("b_mx", [PAIR, NC + 1, NJ])
        negm = sb("b_negm", [PAIR, NJ], BF16)
        P = [sb(f"b_P{k}", [KP, 2, HALF]) for k in range(2)]
        U = [sb(f"b_U{i}", [128, HEADS, NQ]) for i in range(2)]
        rden = sb("b_rden", [NQ, HEADS])
        o_nat = sb("b_o_nat", [NQ, HEADS, HD1])

        ctx_in = sems("b_ctx_in", 2)
        aux_full, aux_free = sems("b_aux_full", 2), sems("b_aux_free", 2)
        s_full, exp_done, p_used = sems("b_s_full", 2), sems("b_exp_done", 2), sems("b_p_used", 2)
        (y_ready, hi_ready, bf_ready, l_ready, Q_bf_ready, mx_ready, Q_ready, u_free, own_v, own_p, pool_turn,
         pe_turn) = (sem("b_" + n) for n in
            "y_ready hi_ready bf_ready l_ready Q_bf_ready mx_ready Q_ready u_free own_v own_p pool_turn pe_turn".split())

        prep = [("l_nat",), ("q",)] + [("Q", i, a) for i in range(2) for a in range(2)] + [("T", c) for c in range(NC)] \
            + [("max", c, j) for c in range(NC) for j in range(NJ)] + [("max_l",)] + [("row", h) for h in range(2)]
        fin = [("Ul", h) for h in range(2)] + [("out", k) for k in range(4)] + [("oT", h) for h in range(2)]
        assert len(prep) % 2 == 0 and len(fin) % 2 == 0
        P2, F2 = len(prep) // 2, len(fin) // 2
        prep_at = {n: k for k, n in enumerate(prep)}
        fin_at = {n: k for k, n in enumerate(fin)}

        def aux_prep(name, b):
            k = prep_at[name]
            ends = max(b - 1, 0) if isinstance(b, int) else b - 1
            return 6 + k % 2, aux_full[k % 2], aux_free[k % 2], b * P2 + ends * F2 + k // 2

        def aux_fin(name, b):
            k = fin_at[name]
            prepared = min(b + 2, B) if isinstance(b, int) else b + 2
            return 6 + k % 2, aux_full[k % 2], aux_free[k % 2], prepared * P2 + b * F2 + k // 2

        def order(b):
            first, last = isinstance(b, int) and b == 0, isinstance(b, int) and b == B - 1
            groups = []
            for t in range(NT):
                g = [("scores", t)]
                if t == 0 and not first:
                    g += [("fin", n) for n in fin if n[0] == "Ul"]
                if t:
                    g.append(("weigh", t - 1))
                if t in (2, 3) and not first:
                    g += [("fin", n) for n in fin if n[0] == "out" and n[1] // 2 == t - 2]
                if t == 4 and not first:
                    g += [("fin", n) for n in fin if n[0] == "oT"]
                groups.append(g)
            if last:
                return sum(groups, [])
            early, late = groups[:5], groups[5:]
            return sum(early, []) + spread(late, [("prepare", n) for n in prep])

        def s_use(b, t):
            return t % 2, b * (NT // 2 + 1 if t % 2 == 0 else NT // 2) + t // 2

        with nc.Block() as block:
            @block.sync
            def _(sp):
                def load(b, s):
                    if not (isinstance(b, int) and b < 2):
                        sp.wait_ge(y_ready, b - 1)
                    sp.dma_start(ctx[s][:], ctx_rows[b]).then_inc(ctx_in[s], 16)
                load(0, 0)
                load(1, 1)
                with sp.Fori(1, B // 2) as i:
                    load(2 * i, 0)
                    load(2 * i + 1, 1)

            @block.gpsimd
            def _(pool):
                def step(b, s):
                    if not (isinstance(b, int) and b < 2):
                        pool.wait_ge(p_used[1], 6 * (b - 1))
                        pool.sem_inc(pool_turn, 1)
                    nc.gpsimd.tensor_copy(c_mv[:, :, 0], ctx_mv[:, bass.ds(b * KT, KT), 0])
                    nc.gpsimd.tensor_copy(c_mv[:, :, 1], ctx_r[:, bass.ds(b * KT, KT)]).then_inc(own_p, 1)
                    pool.wait_ge(own_p, 2 * b + 1)
                    pool.sem_inc(pool_turn, 1)
                    pool.wait_ge(ctx_in[s], 8 * (b - s) + 16)
                    pool.sem_inc(pool_turn, 1)
                    for t in range(KT):
                        last = nc.gpsimd.tensor_scalar(y[s][:, t, :], ctx[s][:, t, :], c_mv[:, t, 0:1], c_mv[:, t, 1:2],
                                                       ALU.subtract, ALU.mult)
                    last.then_inc(own_p, 1)
                    pool.wait_ge(own_p, 2 * b + 2)
                    pool.sem_inc(pool_turn, 1)
                    nc.gpsimd.memset(y[s][:, :, 0:1], 1.0).then_inc(y_ready, 1)
                    for c in range(NC):
                        pool.wait_ge(hi_ready, b * NC + c + 1)
                        pool.sem_inc(pool_turn, 1)
                        nc.gpsimd.tensor_copy(yT_bf[:, c * CH:(c + 1) * CH],
                                              yT_hi[s][:, c * CH:(c + 1) * CH].bitcast(F32)).then_inc(bf_ready, 1)
                step(0, 0)
                step(1, 1)
                with pool.Fori(1, B // 2) as i:
                    step(2 * i, 0)
                    step(2 * i + 1, 1)

            @block.vector
            def _(v):
                chain = Chain(v, own_v)

                def prepare(b, s):
                    at_least(v, p_used[1], 6 * (b - 1))
                    chain.link(nc.vector.tensor_copy(l_f[:], lT[:, bass.ds(b * NQ, NQ)]))
                    nc.vector.tensor_copy(l_bf[:], l_f[:])
                    chain.link(nc.vector.tensor_copy(l_hi[s][:, 0:NQ], l_f[:]))
                    nc.vector.tensor_tensor(l_lo[s][:, 0:NQ], l_f[:], l_hi[s][:, 0:NQ].bitcast(F32), ALU.subtract).then_inc(l_ready, 1)
                    bank, fu, fr, u = aux_prep(("q",), b)
                    v.wait_ge(fu, u + 1)
                    nc.vector.tensor_copy(q_f[:].rearrange("p j q -> p (j q)"), ps[:, bank, 0:HALF]).then_inc(fr, 1)
                    for i in range(2):
                        for a in range(2):
                            bank, fu, fr, u = aux_prep(("Q", i, a), b)
                            v.wait_ge(fu, u + 1)
                            nc.vector.tensor_copy(Q_f[i][:, :, a, :],
                                                  ps[:, bank, 0:HALF].rearrange("p (j q) -> p j q", j=NJ)).then_inc(fr, 1)
                            v.wait_ge(fr, u + 1)
                        nc.vector.tensor_copy(Q_bf[i][:], Q_f[i][:].rearrange("p j a q -> p (j a q)")).then_inc(Q_bf_ready, 1)
                    for c in range(NC):
                        bank, fu, fr, u = aux_prep(("T", c), b)
                        v.wait_ge(hi_ready, b * NC + c + 1)
                        nc.vector.tensor_tensor(yT_lo[s][:, c * CH:(c + 1) * CH], ps[:, bank, 0:CH],
                                                yT_hi[s][:, c * CH:(c + 1) * CH].bitcast(F32), ALU.subtract).then_inc(fr, 1)
                    for c in range(NC):
                        for j in range(NJ):
                            bank, fu, fr, u = aux_prep(("max", c, j), b)
                            v.wait_ge(fu, u + 1)
                            nc.vector.tensor_reduce(mx[:, c, j:j + 1], ps[0:PAIR, bank, 0:CH], AX.X, ALU.max).then_inc(fr, 1)
                    bank, fu, fr, u = aux_prep(("max_l",), b)
                    v.wait_ge(fu, u + 1)
                    nc.vector.tensor_reduce(mx[:, NC, :], ps[0:PAIR, bank, 0:HALF].rearrange("p (j k) -> p j k", j=NJ), AX.X,
                                            ALU.max).then_inc(fr, 1)
                    v.wait_ge(fr, u + 1)
                    nc.vector.tensor_reduce(negm[:], mx[:].rearrange("p c j -> p j c"), AX.X, ALU.max,
                                            negate=True).then_inc(mx_ready, 1)
                    for h in range(2):
                        bank, fu, fr, u = aux_prep(("row", h), b)
                        v.wait_ge(fu, u + 1)
                        for i in range(2):
                            row = Q_f[i][0:1].rearrange("p j a q -> p (j a q)")[:, h * HALF:(h + 1) * HALF]
                            last = nc.vector.tensor_tensor(row, row, ps[0:1, bank, 0:HALF], ALU.add)
                        last.then_inc(fr, 1)
                    v.wait_ge(fr, u + 1)
                    for i in range(2):
                        last = nc.vector.tensor_copy(Q_hi[s][i][:], Q_f[i][:].rearrange("p j a q -> p (j a q)"))
                    chain.link(last)
                    for i in range(2):
                        last = nc.vector.tensor_tensor(Q_lo[s][i][:], Q_f[i][:].rearrange("p j a q -> p (j a q)"),
                                                       Q_hi[s][i][:].bitcast(F32), ALU.subtract)
                    last.then_inc(Q_ready, 1)

                def finish(b):
                    for k in range(4):
                        bank, fu, fr, u = aux_fin(("out", k), b)
                        v.wait_ge(fu, u + 1)
                        o = ps[0:NQ, bank, 0:4 * (HD1 + 1)].rearrange("p (h w) -> p h w", h=4)
                        chain.link(nc.vector.reciprocal(rden[:, 4 * k:4 * k + 4], o[:, :, HD1]))
                        last = nc.vector.tensor_tensor(o_nat[:, 4 * k:4 * k + 4, :], o[:, :, 0:HD1],
                                                       rden[:, 4 * k:4 * k + 4].unsqueeze(2).broadcast_to((NQ, 4, HD1)), ALU.mult)
                        last.then_inc(fr, 1)

                def step(b, s):
                    if not (isinstance(b, int) and b == 0):
                        finish(b - 1)
                    if not (isinstance(b, int) and b == B - 1):
                        prepare(b + 1, 1 - s)
                for buf in l_hi + l_lo:
                    last = nc.vector.memset(buf[:, NQ:].bitcast(F32), 0.0)
                chain.link(last)
                prepare(0, 0)
                batch_loop(v, chain, step)
                finish(B - 1)

            @block.scalar
            def _(act):
                def prepare(b, s, name):
                    kind = name[0]
                    if kind not in ("T", "l_nat"):
                        return
                    bank, fu, fr, u = aux_prep(name, b)
                    act.wait_ge(fu, u + 1)
                    if kind == "T":
                        c = name[1]
                        nc.scalar.activation(yT_hi[s][:, c * CH:(c + 1) * CH], ps[:, bank, 0:CH], ACT.Copy).then_inc(hi_ready, 1)
                    else:
                        nc.scalar.activation(l_nat[s][:], ps[0:NQ, bank, 0:D], ACT.Copy).then_inc(fr, 1)

                def finish(b, name):
                    kind, k = name
                    if kind == "out":
                        return
                    bank, fu, fr, u = aux_fin(name, b)
                    act.wait_ge(fu, u + 1)
                    if kind == "Ul":
                        nc.scalar.activation(U[1][:, 8 * k:8 * k + 8, :].rearrange("p h q -> p (h q)"), ps[:, bank, 0:HALF],
                                             ACT.Copy).then_inc(fr, 1)
                    else:
                        nc.scalar.activation(AT1[:, 4 * k:4 * k + 4, bass.ds(b * NQ, NQ)],
                                             ps[:, bank, 0:4 * NQ].rearrange("p (j q) -> p j q", j=4), ACT.Copy).then_inc(fr, 1)

                def step(b, s):
                    items = order(b)
                    if items[1][0] == "fin":
                        items = items[1:3] + items[0:1] + items[3:]
                    for kind, what in items:
                        if kind == "scores":
                            k, u = s_use(b, what)
                            rows = KP if what < KT else NQ
                            act.wait_ge(s_full[k], u + 1)
                            at_least(act, p_used[k], 6 * b + what // 2)
                            nc.scalar.activation(P[k][0:rows], ps[0:rows, 2 * k:2 * k + 2, 0:HALF], ACT.Exp,
                                                 scale=SCALE).then_inc(exp_done[k], 1)
                        elif kind == "weigh":
                            if what == KT - 1:
                                act.wait_ge(p_used[1], 6 * (b + 1))
                                nc.scalar.activation(U[0][:].rearrange("p (a h) q -> p a (h q)", a=2), ps[:, 4:6, 0:HALF],
                                                     ACT.Copy).then_inc(u_free, 1)
                        elif kind == "fin":
                            finish(b - 1, what)
                        else:
                            prepare(b + 1, 1 - s, what)
                for n in prep:
                    prepare(0, 0, n)
                batch_loop(act, Chain(act, None), step)
                for n in fin:
                    finish(B - 1, n)

            @block.tensor
            def _(pe):
                def prepare(b, s, name):
                    kind = name[0]
                    bank, fu, fr, u = aux_prep(name, b)
                    at_least(pe, fr, u)
                    if kind == "l_nat":
                        pe.wait_ge(l_ready, b + 1)
                        pe.sem_inc(pe_turn, 1)
                        last = nc.tensor.transpose(ps[0:NQ, bank, 0:D], l_f[:], ident)
                    elif kind == "q":
                        for j in range(NJ):
                            last = nc.tensor.matmul(ps[:, bank, NQ * j:NQ * (j + 1)], wq[:, 128 * j:128 * (j + 1)], l_f[:],
                                                    start=True, stop=True)
                    elif kind == "Q":
                        i, a = name[1:]
                        if (i, a) == (0, 0):
                            _, _, fq, uq = aux_prep(("q",), b)
                            pe.wait_ge(fq, uq + 1)
                        rows = slice(64 * a, 64 * a + 64)
                        for j in range(NJ):
                            last = nc.tensor.matmul(ps[:, bank, NQ * j:NQ * (j + 1)], wkT[i][rows, j, :], q_f[rows, j, :],
                                                    start=True, stop=True)
                    elif kind == "T":
                        c = name[1]
                        if c == 0:
                            pe.wait_ge(y_ready, b + 1)
                        for k in range(4):
                            last = nc.tensor.transpose(ps[:, bank, KP * k:KP * (k + 1)], y[s][:, 4 * c + k, :],
                                                       ident[0:KP, 0:KP])
                    elif kind == "max":
                        c, j = name[1:]
                        if j == 0:
                            pe.wait_ge(bf_ready, b * NC + c + 1)
                            pe.wait_ge(Q_bf_ready, 2 * b + 2)
                        last = nc.tensor.matmul(ps[0:PAIR, bank, 0:CH], Q_bf[0][:, PAIR * j:PAIR * (j + 1)],
                                                yT_bf[:, c * CH:(c + 1) * CH], start=True, stop=True)
                    elif kind == "max_l":
                        for j in range(NJ):
                            last = nc.tensor.matmul(ps[0:PAIR, bank, NQ * j:NQ * (j + 1)], Q_bf[1][:, PAIR * j:PAIR * (j + 1)],
                                                    l_bf[:], start=True, stop=True)
                    else:
                        h = name[1]
                        if h == 0:
                            pe.wait_ge(mx_ready, b + 1)
                        for k in range(4):
                            last = nc.tensor.matmul(ps[0:1, bank, PAIR * k:PAIR * (k + 1)], negm[:, 4 * h + k:4 * h + k + 1],
                                                    ident_bf[0:PAIR, 0:PAIR], start=True, stop=True)
                    last.then_inc(fu, 1)

                def finish(b, s, name):
                    kind, k = name
                    bank, fu, fr, u = aux_fin(name, b)
                    at_least(pe, fr, u)
                    if kind == "Ul":
                        kk, us = s_use(b, KT)
                        if k == 0:
                            pe.wait_ge(exp_done[kk], us + 1)
                        last = nc.tensor.matmul(ps[:, bank, 0:HALF], l_nat[s][:], P[kk][0:NQ, k, :], start=True, stop=True)
                    elif kind == "out":
                        if k == 0:
                            pe.wait_ge(u_free, b + 1)
                            for h in range(2):
                                _, _, fl, ul = aux_fin(("Ul", h), b)
                                pe.wait_ge(fl, ul + 1)
                        pe.sem_inc(pe_turn, 1)
                        for n in range(4):
                            h = 4 * k + n
                            o = ps[0:NQ, bank, (HD1 + 1) * n:(HD1 + 1) * (n + 1)]
                            nc.tensor.matmul(o, U[0][:, h, :], wv[0][:, h, :], start=True, stop=False)
                            last = nc.tensor.matmul(o, U[1][:, h, :], wv[1][:, h, :], start=False, stop=True)
                    else:
                        if k == 0:
                            for m in (2, 3):
                                _, _, fo, uo = aux_fin(("out", m), b)
                                pe.wait_ge(fo, uo + 1)
                        pe.sem_inc(pe_turn, 1)
                        for n in range(4):
                            j = 4 * k + n
                            last = nc.tensor.transpose(ps[:, bank, NQ * n:NQ * (n + 1)],
                                                       o_nat[:, 2 * j:2 * j + 2, :].rearrange("p h d -> p (h d)"),
                                                       ident[0:NQ, 0:NQ])
                    last.then_inc(fu, 1)

                def step(b, s):
                    for kind, what in order(b):
                        if kind == "scores":
                            t = what
                            k, u = s_use(b, t)
                            if t == 0:
                                pe.wait_ge(Q_ready, b + 1)
                            at_least(pe, exp_done[k], u)
                            i = int(t == KT)
                            if i:
                                hi, lo, rows = l_hi[s][:], l_lo[s][:], 128
                            else:
                                hi, lo, rows = yT_hi[s][:, KP * t:KP * (t + 1)], yT_lo[s][:, KP * t:KP * (t + 1)], KP
                            for h in range(2):
                                o = ps[0:rows, 2 * k + h, 0:HALF]
                                cols = slice(HALF * h, HALF * (h + 1))
                                nc.tensor.matmul(o, hi, Q_hi[s][i][:, cols], start=True, stop=False)
                                nc.tensor.matmul(o, hi, Q_lo[s][i][:, cols], start=False, stop=False)
                                last = nc.tensor.matmul(o, lo, Q_hi[s][i][:, cols], start=False, stop=True)
                            last.then_inc(s_full[k], 1)
                        elif kind == "weigh":
                            t = what
                            k, u = s_use(b, t)
                            if t == 0:
                                at_least(pe, u_free, b)
                            pe.wait_ge(exp_done[k], u + 1)
                            for h in range(2):
                                last = nc.tensor.matmul(ps[:, 4 + h, 0:HALF], y[s][:, t, :], P[k][:, h, :],
                                                        start=(t == 0), stop=(t == KT - 1))
                            last.then_inc(p_used[k], 1)
                        elif kind == "fin":
                            finish(b - 1, 1 - s, what)
                        else:
                            prepare(b + 1, 1 - s, what)

                for n in prep:
                    prepare(0, 0, n)
                batch_loop(pe, Chain(pe, None), step)
                for n in fin:
                    finish(B - 1, 1, n)


def top2(nc, chain, iota8, lg, top, idx, idxf, hit):
    for t in range(TT):
        last = nc.vector.max(top[:, t, :], lg[:, t, :])
    chain.link(last)
    for t in range(TT):
        last = nc.vector.max_index(idx[:, t, :], top[:, t, :], lg[:, t, :])
    chain.link(last)
    chain.link(nc.vector.tensor_copy(idxf[:], idx[:]))
    for k in range(2):
        last = nc.vector.tensor_tensor(hit[:, :, k, :], idxf[:, :, k:k + 1].broadcast_to((128, TT, 8)),
                                       iota8.unsqueeze(1).broadcast_to((128, TT, 8)), ALU.is_equal)
    chain.link(last)
    chain.link(nc.vector.tensor_tensor(hit[:, :, 0, :], hit[:, :, 0, :], hit[:, :, 1, :], ALU.add))


def phase_ffn1(nc, A, sem, sems, ps, T, out_tok):
    ident, x_nat, h_nat, hT, AT1 = (T[k] for k in "ident x_nat h_nat hT AT1".split())
    KI = I1 // 128
    with ExitStack() as st:
        def sb(name, shape, dt=F32):
            return st.enter_context(nc.sbuf_tensor(name, shape, dt))
        wout = sb("g_wout", [128, NJ, D])
        gw = sb("g_gw", [E1, D])
        gwT = sb("g_gwT", [128, E1])
        eb = sb("g_eb", [128, E1])
        up = sb("g_up", [128, E1, KI, D])
        down = sb("g_down", [128, E1, I1])
        upT = [sb(f"g_upT{k}", [128, I1]) for k in range(2)]
        downT = [sb(f"g_downT{k}", [128, I1]) for k in range(2)]
        H = [sb(f"g_H{k}", [128, KI, NTOK]) for k in range(2)]
        acc = sb("g_acc", [128, TT, D])
        lg = sb("g_lg", [128, TT, E1])
        top = sb("g_top", [128, TT, 8])
        idx = sb("g_idx", [128, TT, 8], U32)
        idxf = sb("g_idxf", [128, TT, 8])
        hit = sb("g_hit", [128, TT, 2, E1])
        gate = sb("g_gate", [128, TT, E1])
        gsum = sb("g_gsum", [128, TT])

        w_in, small_in, out_done = sem("g_w_in"), sem("g_small_in"), sem("g_out_done")
        var_ready, root_done, own, norm_ready, exp_ready, exp_done, result_ready = (
            sem("g_" + n) for n in "var_ready root_done own norm_ready exp_ready exp_done result_ready".split())
        full, free = sems("g_full", 8), sems("g_free", 8)
        names = [("gT",)] + [("o", t) for t in range(TT)] + [("T", h) for h in range(2)] + [("lg",)]
        for e in range(E1 + 1):
            if e < E1:
                names += [("upT", e), ("downT", e)] + [("h", e, k, h) for k in range(KI) for h in range(2)]
            if e:
                names += [("y", e - 1, h) for h in range(2)]
        ring = Ring(list(range(8)), names, full, free)

        with nc.Block() as block:
            @block.sync
            def _(sp):
                sp.dma_start(gw[:], A["L1_ffn_gate_w"]).then_inc(small_in, 16)
                sp.dma_start(eb[:], A["L1_ffn_expert_bias"].rearrange("(a n) -> a n", a=1).broadcast_to((128, E1))).then_inc(small_in, 16)
                sp.dma_start(wout[:], A["L1_xattn_Wout"].rearrange("(j p) n -> p j n", p=128)).then_inc(small_in, 16)
                sp.dma_start(up[:], A["L1_ffn_w_up"].rearrange("e (k p) d -> p e k d", p=128)).then_inc(w_in, 16)
                sp.dma_start(down[:], A["L1_ffn_w_down"].rearrange("e p i -> p e i")).then_inc(w_in, 16)
                sp.wait_ge(result_ready, 1)
                sp.dma_start(out_tok, acc[:]).then_inc(out_done, 16)
                sp.wait_ge(out_done, 16)

            @block.vector
            def _(v):
                chain = Chain(v, own)

                def take(name):
                    bank, fu, fr, u = ring(name)
                    v.wait_ge(fu, u + 1)
                    return bank, fr, u
                bank, fr, u = take(("gT",))
                nc.vector.tensor_copy(gwT[:], ps[:, bank, 0:E1]).then_inc(fr, 1)
                for t in range(TT):
                    bank, fr, u = take(("o", t))
                    nc.vector.tensor_tensor(x_nat[:, t, :], x_nat[:, t, :], ps[:, bank, 0:D], ALU.add).then_inc(fr, 1)
                v.wait_ge(fr, u + 1)
                layer_norm(v, chain, var_ready, root_done, 1, x_nat, h_nat, T["stats"], T["mv"], T["rstd"])
                v.sem_inc(norm_ready, 1)
                for h in range(2):
                    bank, fr, u = take(("T", h))
                    n = 128 * len(transposed_tiles(h))
                    nc.vector.tensor_copy(hT[:, 512 * h:512 * h + n], ps[:, bank, 0:n]).then_inc(fr, 1)
                bank, fr, u = take(("lg",))
                v.wait_ge(small_in, 48)
                nc.vector.tensor_tensor(lg[:], ps[:, bank, 0:TT * E1].rearrange("p (t e) -> p t e", t=TT),
                                        eb[:].unsqueeze(1).broadcast_to((128, TT, E1)), ALU.add).then_inc(fr, 1)
                v.wait_ge(fr, u + 1)
                top2(nc, chain, T["iota8"], lg, top, idx, idxf, hit)
                chain.link(nc.vector.tensor_tensor(lg[:], lg[:], top[:, :, 0:1].broadcast_to((128, TT, E1)), ALU.subtract))
                v.sem_inc(exp_ready, 1)
                v.wait_ge(exp_done, 1)

                def divide(a, s):
                    chain.link(nc.vector.reciprocal(s, s))
                    chain.link(nc.vector.tensor_tensor(a, a, s.unsqueeze(2).broadcast_to((128, TT, E1)), ALU.mult))
                chain.link(nc.vector.tensor_reduce(gsum[:], lg[:], AX.X, ALU.add))
                divide(lg[:], gsum[:])
                chain.link(nc.vector.tensor_tensor(gate[:], lg[:], hit[:, :, 0, :], ALU.mult))
                chain.link(nc.vector.tensor_reduce(gsum[:], gate[:], AX.X, ALU.add))
                chain.link(nc.vector.tensor_scalar(gsum[:], gsum[:], GATE_EPS, None, ALU.add))
                divide(gate[:], gsum[:])

                def weights(e):
                    bank, fr, u = take(("upT", e))
                    nc.vector.tensor_copy(upT[e % 2][:], ps[:, bank, :]).then_inc(fr, 1)
                    bank, fr, u = take(("downT", e))
                    nc.vector.tensor_copy(downT[e % 2][:], ps[:, bank, :]).then_inc(fr, 1)
                for e in range(E1 + 1):
                    if e < E1:
                        weights(e)
                    if e == 0:
                        continue
                    for h in range(2):
                        bank, fr, u = take(("y", e - 1, h))
                        for k, t in enumerate(transposed_tiles(h)):
                            y = ps[:, bank, D * k:D * (k + 1)]
                            g = gate[:, t, e - 1:e]
                            if e == 1:
                                last = nc.vector.tensor_scalar(acc[:, t, :], y, g, None, ALU.mult)
                            else:
                                last = nc.vector.scalar_tensor_tensor(acc[:, t, :], y, g, acc[:, t, :], ALU.mult, ALU.add)
                        last.then_inc(fr, 1)
                        v.wait_ge(fr, u + 1)
                chain.link(nc.vector.tensor_tensor(x_nat[:], x_nat[:], h_nat[:], ALU.add))
                layer_norm(v, chain, var_ready, root_done, 2, acc, acc, T["stats"], T["mv"], T["rstd"])
                nc.vector.tensor_tensor(acc[:], acc[:], x_nat[:], ALU.add).then_inc(result_ready, 1)

            @block.scalar
            def _(act):
                act.wait_ge(var_ready, 1)
                nc.scalar.activation(T["rstd"][:], T["rstd"][:], ACT.Sqrt).then_inc(root_done, 1)
                act.wait_ge(exp_ready, 1)
                nc.scalar.activation(lg[:], lg[:], ACT.Exp).then_inc(exp_done, 1)
                for e in range(E1):
                    for k in range(KI):
                        for h in range(2):
                            bank, fu, fr, u = ring(("h", e, k, h))
                            act.wait_ge(fu, u + 1)
                            nc.scalar.activation(H[e % 2][:, k, h * HALF:(h + 1) * HALF], ps[:, bank, 0:HALF],
                                                 ACT.Gelu).then_inc(fr, 1)
                act.wait_ge(var_ready, 2)
                nc.scalar.activation(T["rstd"][:], T["rstd"][:], ACT.Sqrt).then_inc(root_done, 1)

            @block.tensor
            def _(pe):
                def claim(name):
                    bank, fu, fr, u = ring(name)
                    at_least(pe, fr, u)
                    return bank, fu

                def copied(name):
                    bank, fu, fr, u = ring(name)
                    pe.wait_ge(fr, u + 1)
                pe.wait_ge(small_in, 48)
                bank, fu = claim(("gT",))
                nc.tensor.transpose(ps[:, bank, 0:E1], gw[:], ident[0:E1, 0:E1]).then_inc(fu, 1)
                for t in range(TT):
                    bank, fu = claim(("o", t))
                    for j in range(NJ):
                        last = nc.tensor.matmul(ps[:, bank, 0:D], AT1[:, j, 128 * t:128 * (t + 1)], wout[:, j, :],
                                                start=(j == 0), stop=(j == NJ - 1))
                    last.then_inc(fu, 1)
                pe.wait_ge(norm_ready, 1)
                for h in range(2):
                    bank, fu = claim(("T", h))
                    for k, t in enumerate(transposed_tiles(h)):
                        last = nc.tensor.transpose(ps[:, bank, 128 * k:128 * (k + 1)], h_nat[:, t, :], ident)
                    last.then_inc(fu, 1)
                for h in range(2):
                    copied(("T", h))
                bank, fu = claim(("lg",))
                for t in range(TT):
                    last = nc.tensor.matmul(ps[:, bank, E1 * t:E1 * (t + 1)], hT[:, 128 * t:128 * (t + 1)], gwT[:],
                                            start=True, stop=True)
                last.then_inc(fu, 1)
                pe.wait_ge(w_in, 32)

                def outputs(e):
                    for k in range(KI):
                        for h in range(2):
                            copied(("h", e, k, h))
                    for h in range(2):
                        bank, fu = claim(("y", e, h))
                        for n, t in enumerate(transposed_tiles(h)):
                            for k in range(KI):
                                last = nc.tensor.matmul(ps[:, bank, D * n:D * (n + 1)], H[e % 2][:, k, 128 * t:128 * (t + 1)],
                                                        downT[e % 2][:, 128 * k:128 * (k + 1)],
                                                        start=(k == 0), stop=(k == KI - 1))
                        last.then_inc(fu, 1)
                for e in range(E1):
                    bank, fu = claim(("upT", e))
                    for k in range(KI):
                        last = nc.tensor.transpose(ps[:, bank, 128 * k:128 * (k + 1)], up[:, e, k, :], ident)
                    last.then_inc(fu, 1)
                    bank, fu = claim(("downT", e))
                    for k in range(KI):
                        last = nc.tensor.transpose(ps[:, bank, 128 * k:128 * (k + 1)], down[:, e, 128 * k:128 * (k + 1)], ident)
                    last.then_inc(fu, 1)
                    copied(("upT", e))
                    copied(("downT", e))
                    for k in range(KI):
                        for h in range(2):
                            bank, fu = claim(("h", e, k, h))
                            nc.tensor.matmul(ps[:, bank, 0:HALF], upT[e % 2][:, 128 * k:128 * (k + 1)],
                                             hT[:, h * HALF:(h + 1) * HALF], start=True, stop=True).then_inc(fu, 1)
                    if e:
                        outputs(e - 1)
                outputs(E1 - 1)


_INS = ["x", "ctx_1024", "L0_xattn_W_v", "L0_xattn_W_k", "L0_xattn_W_q", "L0_xattn_W_o", "L0_xattn_b_o",
        "L0_ffn_router_w", "L0_ffn_router_b", "L0_ffn_routed_w1", "L0_ffn_routed_w3", "L0_ffn_routed_w2",
        "L0_ffn_shared_w1", "L0_ffn_shared_w3", "L0_ffn_shared_w2", "L1_xattn_ln_m_g", "L1_xattn_ln_m_b",
        "L1_xattn_ln_l_g", "L1_xattn_ln_l_b", "L1_xattn_Wq", "L1_xattn_Wkv", "L1_xattn_Wout",
        "L1_ffn_gate_w", "L1_ffn_expert_bias", "L1_ffn_w_up", "L1_ffn_w_down"]


def constants():
    import numpy as np
    p = np.arange(128)
    c = np.zeros((128, CONSTS), np.float32)
    c[:, 0:128] = np.eye(128)
    c[:, 128:132] = (p[:, None] % 32) // HD0 == np.arange(4)[None, :]
    c[:, 132] = p < NQ
    c[:, 133] = p >= NQ
    c[:, 134:142] = np.arange(8)
    return c


def kernel(**inputs):
    import numpy as np
    import concourse.bacc as bacc
    from concourse.bass_utils import run_bass_kernel_spmd as run

    nc = bacc.Bacc("TRN2", target_bir_lowering=False, num_devices=1)
    arrays, aps = {}, {}
    for name, a in [(n, inputs[n]) for n in _INS] + [("consts", constants())]:
        a = np.ascontiguousarray(a)
        arrays[f"in_{name}_dram"] = a
        aps[name] = nc.dram_tensor(f"in_{name}_dram", a.shape, mybir.dt.from_np(a.dtype), kind="ExternalInput").ap()
    out = nc.dram_tensor("out_0_dram", (B, NQ, D), F32, kind="ExternalOutput").ap()
    build(nc, aps, out)
    r = run(nc, [arrays], core_ids=[0])
    return r.results[0]["out_0_dram"]
```

```python
from contextlib import ExitStack

import concourse.bass as bass
from concourse import mybir

F32 = mybir.dt.float32
F32R = mybir.dt.float32r
BF16 = mybir.dt.bfloat16
U32 = mybir.dt.uint32
ALU = mybir.AluOpType
ACT = mybir.ActivationFunctionType
AX = mybir.AxisListType

B, NQ, D = 16, 56, 128
NCTX = 1500
KT, KP = 12, 125
HEADS = 16
NTOK = B * NQ
TT = NTOK // 128
HALF = NTOK // 2
HQ = HEADS * NQ
PAIR = 2 * NQ
NJ = HEADS // 2
CH = 500
NC = NCTX // CH
HD0, HD1 = 8, 64
GQ = 4 * NQ
VW = 4 * HD0 + 1
VPAD = 66
E0, HID0 = 8, 64
E1, I1 = 8, 512
LN_EPS = 1e-5
GATE_EPS = 1e-6
CONSTS = 128 + 4 + 2 + 8 + HEADS


def at_least(eng, sem, count):
    if isinstance(count, int) and count <= 0:
        return
    eng.wait_ge(sem, count)


class Chain:

    def __init__(self, eng, sem):
        self.eng, self.sem, self.n, self.offset = eng, sem, 0, 0

    def link(self, ins):
        self.n += 1
        ins.then_inc(self.sem, 1)
        self.eng.wait_ge(self.sem, self.offset + self.n)


class Ring:

    def __init__(self, banks, names, full, free):
        self.banks, self.full, self.free = banks, full, free
        self.place = {name: k for k, name in enumerate(names)}
        n = len(banks)
        self.uses = [len(range(k, len(names), n)) for k in range(n)]

    def __call__(self, name, rounds=0):
        k = self.place[name]
        slot = k % len(self.banks)
        return self.banks[slot], self.full[slot], self.free[slot], rounds * self.uses[slot] + k // len(self.banks)


class TwoStageRing:

    def __init__(self, banks, prep, fin, full, free):
        assert len(prep) % 2 == 0 and len(fin) % 2 == 0
        self.banks, self.full, self.free = banks, full, free
        self.prep_at = {n: k for k, n in enumerate(prep)}
        self.fin_at = {n: k for k, n in enumerate(fin)}
        self.p, self.f = len(prep) // 2, len(fin) // 2

    def use(self, k, before):
        return self.banks[k % 2], self.full[k % 2], self.free[k % 2], before + k // 2

    def prep(self, name, b):
        ends = max(b - 1, 0) if isinstance(b, int) else b - 1
        return self.use(self.prep_at[name], b * self.p + ends * self.f)

    def fin(self, name, b):
        prepared = min(b + 2, B) if isinstance(b, int) else b + 2
        return self.use(self.fin_at[name], prepared * self.p + b * self.f)


def batch_loop(eng, chain, step):
    step(0, 0)
    before = chain.n
    step(1, 1)
    start, stride = chain.n, 2 * (chain.n - before)
    with eng.Fori(1, B // 2 - 1) as i:
        chain.n, chain.offset = start, (i - 1) * stride
        step(2 * i, 0)
        step(2 * i + 1, 1)
    chain.n, chain.offset = start + (B // 2 - 2) * stride, 0
    step(B - 2, 0)
    step(B - 1, 1)


def spread(groups, pieces):
    out, n = [], len(groups)
    for k, g in enumerate(groups):
        out += g
        out += pieces[k * len(pieces) // n:(k + 1) * len(pieces) // n]
    return out


def build(nc, A, out):
    x_tok = A["x"].rearrange("b q d -> (b q) d").rearrange("(t p) d -> p t d", p=128)
    out_tok = out.rearrange("b q d -> (b q) d").rearrange("(t p) d -> p t d", p=128)
    ctx_rows = A["ctx_1024"].rearrange("b (p t) d -> b p t d", p=KP)

    with ExitStack() as outer:
        def tensor(stack, name, shape, dt=F32):
            return stack.enter_context(nc.sbuf_tensor(name, shape, dt))

        def sem(name):
            return outer.enter_context(nc.semaphore(name))

        def sems(name, n):
            return [sem(f"{name}{i}") for i in range(n)]

        ps = outer.enter_context(nc.psum_tensor("ps", [128, 8, 512], F32))

        cst = tensor(outer, "cst", [128, CONSTS])
        ident = cst[:, 0:128]
        group_mask = cst[:, 128:132]
        pair_mask = cst[:, 132:134]
        iota8 = cst[:, 134:142]
        head_mask = cst[:, 142:142 + HEADS]
        ident_bf = tensor(outer, "ident_bf", [128, 128], BF16)
        x_nat = tensor(outer, "x_nat", [128, TT, D])
        h_nat = tensor(outer, "h_nat", [128, TT, D])
        hT = tensor(outer, "hT", [128, NTOK])
        stats = tensor(outer, "stats", [128, TT, 6])
        mv = tensor(outer, "mv", [128, TT, 2])
        rstd = tensor(outer, "rstd", [128, TT])
        ctx_mv = tensor(outer, "ctx_mv", [KP, B * KT, 2])

        with ExitStack() as l0:
            wq0 = tensor(l0, "wq0", [128, 128])
            qT = tensor(l0, "qT", [128, NTOK])
            wk0 = tensor(l0, "wk0", [128, 128])
            wv0 = tensor(l0, "wv0", [128, 128])
            q_parts = tensor(l0, "q_parts", [96, 4, NTOK], F32R)
            AT0 = tensor(l0, "AT0", [64, 2, NTOK])
            phase_queries(nc, A, sem, sems, ps, locals())
            phase_attention0(nc, A, sem, sems, ps, locals(), ctx_rows)
            phase_ffn0(nc, A, sem, sems, ps, locals())
        with ExitStack() as l1:
            AT1 = tensor(l1, "AT1", [128, NJ, NTOK])
            phase_attention1(nc, A, sem, sems, ps, locals(), ctx_rows)
            phase_ffn1(nc, A, sem, sems, ps, locals(), out_tok)


def layer_norm(v, chain, act_ready, act_done, round_, src, dst, stats, mv, rstd):
    for t in range(TT):
        last = v.bn_stats(stats[:, t, :], src[:, t, :])
    chain.link(last)
    for t in range(TT):
        last = v.bn_aggr(mv[:, t, :], stats[:, t, :])
    chain.link(last)
    v.tensor_scalar(rstd[:], mv[:, :, 1], LN_EPS, None, ALU.add).then_inc(act_ready, 1)
    v.wait_ge(act_done, round_)
    chain.link(v.reciprocal(rstd[:], rstd[:]))
    for t in range(TT):
        last = v.tensor_scalar(dst[:, t, :], src[:, t, :], mv[:, t, 0:1], rstd[:, t:t + 1], ALU.subtract, ALU.mult)
    chain.link(last)


def transposed_tiles(h):
    return range(0, 4) if h == 0 else range(4, TT)


def phase_queries(nc, A, sem, sems, ps, T):
    cst, ident, ident_bf, x_nat, h_nat, hT, q_parts = (
        T[k] for k in "cst ident ident_bf x_nat h_nat hT q_parts".split())
    const_in, x_in, w0_in = sem("const_in"), sem("x_in"), sem("w0_in")
    var_ready, root_done, norm_ready = sem("q_var_ready"), sem("q_root_done"), sem("q_norm_ready")
    hT_ready, own = sem("q_hT_ready"), sem("q_own")
    q_full, w_ready, q_hi_ready, q_lo_ready = (sem("q_" + n) for n in "full w_ready hi_ready lo_ready".split())
    wq3 = T["l0"].enter_context(nc.sbuf_tensor("wq3", [128, 4, 3, 32], F32))
    with nc.Block() as block:
        @block.sync
        def _(sp):
            sp.dma_start(cst[:], A["consts"]).then_inc(const_in, 16)
            sp.dma_start(x_nat[:], T["x_tok"]).then_inc(x_in, 16)
            sp.dma_start(T["wq0"][:], A["L0_xattn_W_q"]).then_inc(w0_in, 16)
            sp.dma_start(T["wk0"][:], A["L0_xattn_W_k"]).then_inc(w0_in, 16)
            sp.dma_start(T["wv0"][:], A["L0_xattn_W_v"]).then_inc(w0_in, 16)

        @block.vector
        def _(v):
            chain = Chain(v, own)
            v.wait_ge(const_in, 16)
            v.wait_ge(x_in, 16)
            nc.vector.tensor_copy(ident_bf[:], ident)
            layer_norm(v, chain, var_ready, root_done, 1, x_nat, h_nat, T["stats"], T["mv"], T["rstd"])
            v.sem_inc(norm_ready, 1)
            v.wait_ge(w0_in, 48)
            nc.vector.tensor_copy(wq3[:], T["wq0"][:].rearrange("p (g c) -> p g c", g=4).unsqueeze(2)
                                  .broadcast_to((128, 4, 3, 32))).then_inc(w_ready, 1)
            for h in range(2):
                v.wait_ge(q_full, h + 1)
                n = 128 * len(transposed_tiles(h))
                nc.vector.tensor_copy(hT[:, 512 * h:512 * h + n], ps[:, h, 0:n]).then_inc(hT_ready, 1)
            for k in range(8):
                g, h = k // 2, k % 2
                lo = q_parts[32:64, g, HALF * h:HALF * (h + 1)]
                v.wait_ge(q_hi_ready, k + 1)
                nc.vector.tensor_tensor(lo, ps[32:64, (2 + k) % 8, 0:HALF], lo.bitcast(F32),
                                        ALU.subtract).then_inc(q_lo_ready, 1)

        @block.scalar
        def _(act):
            act.wait_ge(var_ready, 1)
            nc.scalar.activation(T["rstd"][:], T["rstd"][:], ACT.Sqrt).then_inc(root_done, 1)
            for k in range(8):
                g, h = k // 2, k % 2
                act.wait_ge(q_full, k + 3)
                nc.scalar.activation(q_parts[:, g, HALF * h:HALF * (h + 1)], ps[0:96, (2 + k) % 8, 0:HALF],
                                     ACT.Copy).then_inc(q_hi_ready, 1)
            for h in range(2):
                act.wait_ge(q_full, h + 11)
                nc.scalar.activation(T["qT"][:, HALF * h:HALF * (h + 1)], ps[:, 2 + h, 0:HALF], ACT.Copy)

        @block.tensor
        def _(pe):
            pe.wait_ge(const_in, 16)
            pe.wait_ge(norm_ready, 1)
            for h in range(2):
                for k, t in enumerate(transposed_tiles(h)):
                    last = nc.tensor.transpose(ps[:, h, 128 * k:128 * (k + 1)], h_nat[:, t, :], ident)
                last.then_inc(q_full, 1)
            pe.wait_ge(w_ready, 1)
            pe.wait_ge(hT_ready, 2)
            for k in range(8):
                g, h = k // 2, k % 2
                nc.tensor.matmul(ps[0:96, (2 + k) % 8, 0:HALF], wq3[:, g, :, :].rearrange("p r c -> p (r c)"),
                                 hT[:, HALF * h:HALF * (h + 1)], start=True, stop=True).then_inc(q_full, 1)
            for h in range(2):
                pe.wait_ge(q_lo_ready, h + 1)
                nc.tensor.matmul(ps[:, 2 + h, 0:HALF], T["wq0"][:], hT[:, HALF * h:HALF * (h + 1)],
                                 start=True, stop=True).then_inc(q_full, 1)


def phase_attention0(nc, A, sem, sems, ps, T, ctx_rows):
    ident, ident_bf, q_parts, AT0, ctx_mv = (T[k] for k in "ident ident_bf q_parts AT0 ctx_mv".split())
    SCALE = 1.0 / float(D) ** 0.5
    STACK = 12 * 16
    with ExitStack() as st:
        def sb(name, shape, dt=F32):
            return st.enter_context(nc.sbuf_tensor(name, shape, dt))
        ctx = [sb(f"a_ctx{s}", [KP, KT, D]) for s in range(2)]
        ctxT = sb("a_ctxT", [128, NCTX])
        k_hi = sb("a_k_hi", [128, NCTX], F32R)
        k_lo = sb("a_k_lo", [128, NCTX], F32R)
        k_bf = sb("a_k_bf", [128, NCTX], BF16)
        k_parts = [sb(f"a_k_parts{s}", [97, 4, NCTX], F32R) for s in range(2)]
        vals = [sb(f"a_vals{s}", [KP, KT, 4, VPAD]) for s in range(2)]
        q_rows = [sb(f"a_q_rows{s}", [97, 4, 4, NQ], F32R) for s in range(2)]
        q_bf = sb("a_q_bf", [128, HQ], BF16)
        qT = T["qT"]
        mx = sb("a_mx", [PAIR, NJ, NC])
        negm = sb("a_negm", [PAIR, NJ], BF16)
        P = [sb(f"a_P{s}", [KP, 4, GQ]) for s in range(2)]
        c_st = sb("a_c_st", [KP, KT, 6])
        c_mv = sb("a_c_mv", [KP, KT, 2])
        rden = sb("a_rden", [PAIR, NJ])
        o_T = sb("a_o_T", [VW, HQ])
        o_sel = sb("a_o_sel", [PAIR, 4, 2, HD0])
        o_nat = sb("a_o_nat", [PAIR, 2 * NJ, HD0])

        ctx_in, k_stacked = sems("a_ctx_in", 2), sems("a_k_stacked", 2)
        ctx_measured = sem("a_ctx_measured")
        sp_turn = sem("a_sp_turn")
        pe_turn = sem("a_pe_turn")
        aux_full, aux_free = sems("a_aux_full", 2), sems("a_aux_free", 2)
        k_bf_ready, q_ready, negm_ready, const_ready = (sem("a_" + n) for n in
                                                        "k_bf_ready q_ready negm_ready const_ready".split())
        s_full, exp_done = sems("a_s_full", 2), sems("a_exp_done", 2)
        pv_done, o_ready, o_free = (sem("a_" + n) for n in "pv_done o_ready o_free".split())
        own_v = sem("a_own_v")

        names = [("ctxT", c) for c in range(NC)] + [("k", c) for c in range(NC)] + [("v", c) for c in range(4)] \
            + [("max", c, j) for c in range(NC) for j in range(NJ)] + [("row", h) for h in range(2)]
        fin = ["o_nat", "oT"]
        aux = TwoStageRing([6, 7], names, fin, aux_full, aux_free)
        ring = aux.prep

        def order(b):
            first, last = isinstance(b, int) and b == 0, isinstance(b, int) and b == B - 1
            groups = []
            for t in range(KT + 1):
                if t < KT:
                    groups.append([("scores", t)])
                if t:
                    groups += [[("weigh", (t - 1, h))] for h in range(2)]
            rest = [] if first else [("fin", n) for n in fin]
            rest += [] if last else [("prepare", n) for n in names]
            return sum(groups[:3], []) + spread(groups[3:-3], rest) + sum(groups[-3:], [])

        with nc.Block() as block:
            @block.sync
            def _(sp):
                def load(b, s):
                    if not (isinstance(b, int) and b < 2):
                        bank, full, free, u = ring(("ctxT", NC - 1), b - 2)
                        sp.wait_ge(free, u + 1)
                        sp.sem_inc(sp_turn, 1)
                        sp.wait_ge(ctx_measured, b - 1)
                    sp.dma_start(ctx[s][:], ctx_rows[b]).then_inc(ctx_in[s], 16)

                def stack(b, s):
                    if not (isinstance(b, int) and b < 2):
                        sp.wait_ge(pv_done, KT * (b - 1))
                        sp.sem_inc(sp_turn, 1)
                    bank, full, free, u = ring(("k", NC - 1), b)
                    sp.wait_ge(free, u + 1)
                    for g in range(4):
                        for r, part in enumerate((k_hi, k_hi, k_lo)):
                            sp.dma_start(k_parts[s][32 * r:32 * r + 32, g, :].bitcast(F32),
                                         part[32 * g:32 * g + 32, :].bitcast(F32)).then_inc(k_stacked[s], 16)
                load(0, 0)
                load(1, 1)
                for b in range(2):
                    stack(b, b)
                    load(b + 2, b)
                with sp.Fori(1, B // 2 - 1) as i:
                    for s in range(2):
                        stack(2 * i + s, s)
                        load(2 * i + s + 2, s)
                for b in (B - 2, B - 1):
                    stack(b, b % 2)

            @block.gpsimd
            def _(pool):
                for s in range(2):
                    nc.gpsimd.memset(vals[s][:, :, :, VW - 1:], 1.0)
                nc.gpsimd.memset(o_nat[:, NJ:, :], 0.0).then_inc(const_ready, 1)

            @block.vector
            def _(v):
                chain = Chain(v, own_v)

                def prepare(b, s):
                    at_least(v, pv_done, KT * (b - 1))
                    nc.vector.tensor_tensor(
                        q_bf[:].rearrange("p (h q) -> p h q", h=HEADS),
                        T["head_mask"].unsqueeze(2).broadcast_to((128, HEADS, NQ)),
                        qT[:, bass.ds(b * NQ, NQ)].unsqueeze(1).broadcast_to((128, HEADS, NQ)), ALU.mult)
                    for g in range(4):
                        last = nc.vector.tensor_tensor(
                            q_rows[s][0:96, g], T["group_mask"][0:96].unsqueeze(2).broadcast_to((96, 4, NQ)),
                            q_parts[:, g, bass.ds(b * NQ, NQ)].bitcast(F32).unsqueeze(1).broadcast_to((96, 4, NQ)), ALU.mult)
                    last.then_inc(q_ready, 1)
                    v.wait_ge(ctx_in[s], 8 * (b - s) + 16)
                    for t in range(KT):
                        last = nc.vector.bn_stats(c_st[:, t, :], ctx[s][:, t, :])
                    last.then_inc(ctx_measured, 1)
                    v.wait_ge(ctx_measured, b + 1)
                    for c in range(NC):
                        bank, full, free, u = ring(("k", c), b)
                        cols = slice(c * CH, (c + 1) * CH)
                        v.wait_ge(k_bf_ready, b * NC + c + 1)
                        nc.vector.tensor_tensor(k_lo[:, cols], ps[:, bank, 0:CH], k_hi[:, cols].bitcast(F32),
                                                ALU.subtract).then_inc(free, 1)
                    for t in range(KT):
                        last = nc.vector.bn_aggr(c_mv[:, t, :], c_st[:, t, :])
                    chain.link(last)
                    nc.vector.tensor_copy(ctx_mv[:, bass.ds(b * KT, KT), :], c_mv[:])
                    for c in range(NC):
                        for j in range(NJ):
                            bank, full, free, u = ring(("max", c, j), b)
                            v.wait_ge(full, u + 1)
                            nc.vector.tensor_reduce(mx[:, j, c:c + 1], ps[0:PAIR, bank, 0:CH], AX.X,
                                                    ALU.max).then_inc(free, 1)
                    v.wait_ge(free, u + 1)
                    nc.vector.tensor_reduce(negm[:], mx[:], AX.X, ALU.max, negate=True).then_inc(negm_ready, 1)
                    for h in range(2):
                        bank, full, free, u = ring(("row", h), b)
                        v.wait_ge(full, u + 1)
                        nc.vector.tensor_copy(q_rows[s][96:97, 2 * h:2 * h + 2].rearrange("p g h q -> p (g h q)"),
                                              ps[96:97, bank, 0:HALF]).then_inc(free, 1)

                def finish(b, s):
                    bank, full, free, u = aux.fin("o_nat", b)
                    v.wait_ge(full, u + 1)
                    o = ps[0:PAIR, bank, 0:NJ * VW].rearrange("p (g a w) -> p g a w", g=4, a=2)
                    for a in range(2):
                        nc.vector.tensor_scalar(o_sel[:, :, a, :], o[:, :, a, 16 * a:16 * a + 8],
                                                T["pair_mask"][0:PAIR, 0:1], None, ALU.mult)
                    chain.link(nc.vector.reciprocal(rden[:].rearrange("p (g a) -> p g a", g=4), o[:, :, :, VW - 1]))
                    for a in range(2):
                        last = nc.vector.scalar_tensor_tensor(o_sel[:, :, a, :], o[:, :, a, 16 * a + 8:16 * a + 16],
                                                              T["pair_mask"][0:PAIR, 1:2], o_sel[:, :, a, :], ALU.mult, ALU.add)
                    last.then_inc(free, 1)
                    v.wait_ge(free, u + 1)
                    nc.vector.tensor_tensor(o_nat[:, 0:NJ, :], o_sel[:].rearrange("p g a d -> p (g a) d"),
                                            rden[:].unsqueeze(2).broadcast_to((PAIR, NJ, HD0)), ALU.mult).then_inc(o_ready, 1)

                def step(b, s):
                    if not (isinstance(b, int) and b == 0):
                        finish(b - 1, 1 - s)
                    if not (isinstance(b, int) and b == B - 1):
                        prepare(b + 1, 1 - s)
                for s in range(2):
                    nc.vector.memset(k_parts[s][96:97].bitcast(F32), 1.0).then_inc(const_ready, 1)
                prepare(0, 0)
                batch_loop(v, chain, step)
                finish(B - 1, 1)

            @block.scalar
            def _(act):
                def prepare(b, s, name):
                    kind = name[0]
                    if kind not in ("ctxT", "k", "v"):
                        return
                    c = name[1]
                    bank, full, free, u = ring(name, b)
                    act.wait_ge(full, u + 1)
                    cols = slice(c * CH, (c + 1) * CH)
                    if kind == "ctxT":
                        nc.scalar.activation(ctxT[:, cols], ps[:, bank, 0:CH], ACT.Copy).then_inc(free, 1)
                    elif kind == "k":
                        if c == 0 and not (isinstance(b, int) and b == 0):
                            act.wait_ge(k_stacked[1 - s], STACK // 2 * (b - 2 + s) + STACK)
                        nc.scalar.activation(k_hi[:, cols], ps[:, bank, 0:CH], ACT.Copy)
                        nc.scalar.activation(k_bf[:, cols], ps[:, bank, 0:CH], ACT.Copy).then_inc(k_bf_ready, 1)
                    else:
                        nc.scalar.activation(
                            vals[s][:, 3 * c:3 * c + 3, :, 0:4 * HD0],
                            ps[0:KP, bank, 0:384].rearrange("p (t g w) -> p t g w", t=3, g=4), ACT.Copy).then_inc(free, 1)

                def copy_out(b):
                    act.wait_ge(pv_done, KT * (b + 1))
                    nc.scalar.activation(o_T[:].rearrange("p (h c) -> p h c", h=2), ps[0:VW, 4:6, 0:HALF],
                                         ACT.Copy).then_inc(o_free, 1)

                def finish(b):
                    bank, full, free, u = aux.fin("oT", b)
                    act.wait_ge(full, u + 1)
                    nc.scalar.activation(AT0[:, :, bass.ds(b * NQ, NQ)],
                                         ps[0:64, bank, 0:PAIR].rearrange("p (a q) -> p a q", a=2), ACT.Copy).then_inc(free, 1)

                def step(b, s):
                    if not (isinstance(b, int) and b == 0):
                        copy_out(b - 1)
                    for kind, what in order(b):
                        if kind == "scores":
                            t = what
                            at_least(act, pv_done, KT * b + t - 1)
                            act.wait_ge(s_full[t % 2], KT // 2 * b + t // 2 + 1)
                            nc.scalar.activation(P[t % 2][:].rearrange("p (a g) c -> p a (g c)", a=2),
                                                 ps[0:KP, 2 * (t % 2):2 * (t % 2) + 2, 0:HALF], ACT.Exp,
                                                 scale=SCALE).then_inc(exp_done[t % 2], 1)
                        elif kind == "fin":
                            if what == "oT":
                                finish(b - 1)
                        elif kind == "prepare":
                            prepare(b + 1, 1 - s, what)
                for n in names:
                    prepare(0, 0, n)
                batch_loop(act, Chain(act, None), step)
                copy_out(B - 1)
                finish(B - 1)

            @block.tensor
            def _(pe):
                def prepare(b, s, name):
                    kind = name[0]
                    bank, full, free, u = ring(name, b)
                    at_least(pe, free, u)
                    if kind == "ctxT":
                        c = name[1]
                        if c == 0:
                            pe.wait_ge(ctx_in[s], 8 * (b - s) + 16)
                        for k in range(4):
                            last = nc.tensor.transpose(ps[:, bank, KP * k:KP * (k + 1)], ctx[s][:, 4 * c + k, :],
                                                       ident[0:KP, 0:KP])
                    elif kind == "k":
                        c = name[1]
                        _, _, free_t, ut = ring(("ctxT", c), b)
                        pe.wait_ge(free_t, ut + 1)
                        last = nc.tensor.matmul(ps[:, bank, 0:CH], T["wk0"][:], ctxT[:, c * CH:(c + 1) * CH],
                                                start=True, stop=True)
                    elif kind == "v":
                        c = name[1]
                        for k in range(3):
                            last = nc.tensor.matmul(ps[0:KP, bank, 128 * k:128 * (k + 1)],
                                                    ctxT[:, (3 * c + k) * KP:(3 * c + k + 1) * KP], T["wv0"][:],
                                                    start=True, stop=True)
                    elif kind == "max":
                        c, j = name[1:]
                        if j == 0:
                            pe.wait_ge(k_bf_ready, b * NC + c + 1)
                            pe.wait_ge(q_ready, b + 1)
                        last = nc.tensor.matmul(ps[0:PAIR, bank, 0:CH], q_bf[:, PAIR * j:PAIR * (j + 1)],
                                                k_bf[:, c * CH:(c + 1) * CH], start=True, stop=True)
                    else:
                        h = name[1]
                        if h == 0:
                            pe.wait_ge(negm_ready, b + 1)
                        for k in range(4):
                            last = nc.tensor.matmul(ps[96:97, bank, PAIR * k:PAIR * (k + 1)], negm[:, 4 * h + k:4 * h + k + 1],
                                                    ident_bf[0:PAIR, 0:PAIR], start=True, stop=True)
                    last.then_inc(full, 1)

                def finish(b, name):
                    bank, full, free, u = aux.fin(name, b)
                    pe.wait_ge(free, u)
                    if name == "o_nat":
                        pe.wait_ge(o_free, b + 1)
                        pe.sem_inc(pe_turn, 1)
                        for j in range(NJ):
                            last = nc.tensor.transpose(ps[0:PAIR, bank, VW * j:VW * (j + 1)], o_T[:, PAIR * j:PAIR * (j + 1)],
                                                       ident[0:VW, 0:VW])
                    else:
                        pe.wait_ge(o_ready, b + 1)
                        last = nc.tensor.transpose(ps[:, bank, 0:PAIR], o_nat[:].rearrange("p j d -> p (j d)"),
                                                   ident[0:PAIR, 0:PAIR])
                    last.then_inc(full, 1)

                def step(b, s):
                    for kind, what in order(b):
                        if kind == "scores":
                            t = what
                            if t == 0:
                                _, _, free, ur = ring(("row", 1), b)
                                pe.wait_ge(free, ur + 1)
                                pe.wait_ge(k_stacked[s], STACK // 2 * (b - s) + STACK)
                            at_least(pe, exp_done[t % 2], KT // 2 * b + t // 2)
                            for g in range(4):
                                last = nc.tensor.matmul(ps[0:KP, 2 * (t % 2) + g // 2, (g % 2) * GQ:(g % 2 + 1) * GQ],
                                                        k_parts[s][:, g, KP * t:KP * (t + 1)],
                                                        q_rows[s][:, g].rearrange("p h q -> p (h q)"), start=True, stop=True)
                            last.then_inc(s_full[t % 2], 1)
                        elif kind == "weigh":
                            t, h = what
                            if t == 0 and h == 0:
                                at_least(pe, o_free, b)
                            if h == 0:
                                pe.wait_ge(exp_done[t % 2], KT // 2 * b + t // 2 + 1)
                            for a in range(2):
                                g = 2 * h + a
                                last = nc.tensor.matmul(ps[0:VPAD, 4 + h, GQ * a:GQ * (a + 1)], vals[s][:, t, g, :],
                                                        P[t % 2][:, g, :], start=(t == 0 and a == 0), stop=(t == KT - 1),
                                                        skip_group_check=True)
                            if h:
                                last.then_inc(pv_done, 1)
                        elif kind == "fin":
                            finish(b - 1, what)
                        else:
                            prepare(b + 1, 1 - s, what)

                pe.wait_ge(const_ready, 3)
                for n in names:
                    prepare(0, 0, n)
                batch_loop(pe, Chain(pe, None), step)
                for n in fin:
                    finish(B - 1, n)


def phase_ffn0(nc, A, sem, sems, ps, T):
    ident, x_nat, h_nat, hT, AT0 = (T[k] for k in "ident x_nat h_nat hT AT0".split())
    EP = E0 // 2 + 1
    with ExitStack() as st:
        def sb(name, shape, dt=F32):
            return st.enter_context(nc.sbuf_tensor(name, shape, dt))
        wo = sb("f_wo", [64, 2, D])
        bo = sb("f_bo", [128, D])
        rw = sb("f_rw", [128, E0])
        rb = sb("f_rb", [128, E0])
        w1 = sb("f_w1", [128, 2 * EP, HID0])
        w3 = sb("f_w3", [128, 2 * EP, HID0])
        w2 = sb("f_w2", [128, EP, D])
        act_sb = sb("f_act", [128, 2, HALF])
        H = sb("f_H", [128, EP, NTOK])
        lg = sb("f_lg", [128, TT, E0])
        top = sb("f_top", [128, TT, 8])
        idx = sb("f_idx", [128, TT, 8], U32)
        idxf = sb("f_idxf", [128, TT, 8])
        hit = sb("f_hit", [128, TT, 2, E0])
        gate = sb("f_gate", [128, TT, E0])
        gsum = sb("f_gsum", [128, TT])

        w_in, small_in = sem("f_w_in"), sem("f_small_in")
        var_ready, root_done, own = sem("f_var_ready"), sem("f_root_done"), sem("f_own")
        norm_ready, hT_ready, exp_ready, exp_done, act_ready, H_ready = (
            sem("f_" + n) for n in "norm_ready hT_ready exp_ready exp_done act_ready H_ready".split())
        full, free = sems("f_full", 8), sems("f_free", 8)
        names = [("o", t) for t in range(TT)] + [("T", h) for h in range(2)] + [("lg",)] \
            + [(w, e, h) for e in range(EP) for h in range(2) for w in "ab"] \
            + [("y", t, k) for t in range(TT) for k in range(3)]
        ring = Ring(list(range(8)), names, full, free)

        with nc.Block() as block:
            @block.sync
            def _(sp):
                wo_rows = A["L0_xattn_W_o"].rearrange("(j a d) n -> a j d n", a=2, d=HD0)
                for a in range(2):
                    for j in range(NJ):
                        sp.dma_start(wo[HD0 * j:HD0 * (j + 1), a, :], wo_rows[a, j]).then_inc(small_in, 16)
                sp.dma_start(bo[:], A["L0_xattn_b_o"].rearrange("(a n) -> a n", a=1).broadcast_to((128, D))).then_inc(small_in, 16)
                sp.dma_start(rb[:], A["L0_ffn_router_b"].rearrange("(a n) -> a n", a=1).broadcast_to((128, E0))).then_inc(small_in, 16)
                sp.dma_start(rw[:], A["L0_ffn_router_w"]).then_inc(small_in, 16)
                for w, name in ((w1, "w1"), (w3, "w3")):
                    sp.dma_start(w[:, 0:E0, :], A["L0_ffn_routed_" + name].rearrange("e d h -> d e h")).then_inc(w_in, 16)
                    sp.dma_start(w[:, E0:, :], A["L0_ffn_shared_" + name].rearrange("e d h -> d e h")).then_inc(w_in, 16)
                sp.dma_start(w2[:, 0:EP - 1, :], A["L0_ffn_routed_w2"].rearrange("(k e) h d -> (e h) k d", e=2)).then_inc(w_in, 16)
                sp.dma_start(w2[:, EP - 1, :], A["L0_ffn_shared_w2"].rearrange("e h d -> (e h) d")).then_inc(w_in, 16)

            @block.vector
            def _(v):
                chain = Chain(v, own)
                v.wait_ge(small_in, 16 * (2 * NJ + 3))
                for t in range(TT):
                    bank, fu, fr, u = ring(("o", t))
                    v.wait_ge(fu, u + 1)
                    last = nc.vector.tensor_tensor(x_nat[:, t, :], x_nat[:, t, :], ps[:, bank, 0:D], ALU.add)
                    last.then_inc(fr, 1)
                    v.wait_ge(fr, u + 1)
                    last = nc.vector.tensor_tensor(x_nat[:, t, :], x_nat[:, t, :], bo[:], ALU.add)
                chain.link(last)
                layer_norm(v, chain, var_ready, root_done, 1, x_nat, h_nat, T["stats"], T["mv"], T["rstd"])
                v.sem_inc(norm_ready, 1)
                for h in range(2):
                    bank, fu, fr, u = ring(("T", h))
                    v.wait_ge(fu, u + 1)
                    n = 128 * len(transposed_tiles(h))
                    nc.vector.tensor_copy(hT[:, 512 * h:512 * h + n], ps[:, bank, 0:n]).then_inc(fr, 1)
                bank, fu, fr, u = ring(("lg",))
                v.wait_ge(fu, u + 1)
                nc.vector.tensor_tensor(lg[:], ps[:, bank, 0:TT * E0].rearrange("p (t e) -> p t e", t=TT),
                                        rb[:].unsqueeze(1).broadcast_to((128, TT, E0)), ALU.add).then_inc(fr, 1)
                v.wait_ge(fr, u + 1)
                top2(nc, chain, T["iota8"], lg, top, idx, idxf, hit)
                chain.link(nc.vector.tensor_tensor(lg[:], lg[:], top[:, :, 0:1].broadcast_to((128, TT, E0)), ALU.subtract))
                v.sem_inc(exp_ready, 1)
                v.wait_ge(exp_done, 1)
                chain.link(nc.vector.tensor_tensor(gate[:], lg[:], hit[:, :, 0, :], ALU.mult))
                chain.link(nc.vector.tensor_reduce(gsum[:], gate[:], AX.X, ALU.add))
                chain.link(nc.vector.reciprocal(gsum[:], gsum[:]))
                chain.link(nc.vector.tensor_tensor(gate[:], gate[:], gsum[:].unsqueeze(2).broadcast_to((128, TT, E0)), ALU.mult))
                for e in range(EP):
                    for h in range(2):
                        bank, fu, fr, u = ring(("b", e, h))
                        v.wait_ge(act_ready, 2 * e + h + 1)
                        v.wait_ge(fu, u + 1)
                        nc.vector.tensor_tensor(H[:, e, h * HALF:(h + 1) * HALF], act_sb[:, h, :], ps[:, bank, 0:HALF],
                                                ALU.mult).then_inc(fr, 1)
                        v.wait_ge(fr, u + 1)
                        v.sem_inc(H_ready, 1)
                for t in range(TT):
                    bank, fu, fr, u = ring(("y", t, 2))
                    v.wait_ge(fu, u + 1)
                    nc.vector.tensor_tensor(x_nat[:, t, :], x_nat[:, t, :], ps[:, bank, 0:D], ALU.add).then_inc(fr, 1)
                    v.wait_ge(fr, u + 1)
                    for k in range(2):
                        bank, fu, fr, u = ring(("y", t, k))
                        v.wait_ge(fu, u + 1)
                        for e in range(4):
                            i = nc.vector.scalar_tensor_tensor(x_nat[:, t, :], ps[:, bank, D * e:D * (e + 1)],
                                                               gate[:, t, 2 * e + k:2 * e + k + 1], x_nat[:, t, :],
                                                               ALU.mult, ALU.add)
                            if e < 3:
                                chain.link(i)
                        i.then_inc(fr, 1)
                        v.wait_ge(fr, u + 1)

            @block.scalar
            def _(act):
                act.wait_ge(var_ready, 1)
                nc.scalar.activation(T["rstd"][:], T["rstd"][:], ACT.Sqrt).then_inc(root_done, 1)
                act.wait_ge(exp_ready, 1)
                nc.scalar.activation(lg[:], lg[:], ACT.Exp).then_inc(exp_done, 1)
                for e in range(EP):
                    for h in range(2):
                        bank, fu, fr, u = ring(("a", e, h))
                        act.wait_ge(fu, u + 1)
                        at_least(act, H_ready, 2 * e + h - 1)
                        nc.scalar.activation(act_sb[:, h, :], ps[:, bank, 0:HALF], ACT.Silu).then_inc(fr, 1)
                        act.wait_ge(fr, u + 1)
                        act.sem_inc(act_ready, 1)

            @block.tensor
            def _(pe):
                def claim(name):
                    bank, fu, fr, u = ring(name)
                    at_least(pe, fr, u)
                    return bank, fu
                pe.wait_ge(small_in, 16 * (2 * NJ + 3))
                for t in range(TT):
                    bank, fu = claim(("o", t))
                    for a in range(2):
                        last = nc.tensor.matmul(ps[:, bank, 0:D], AT0[:, a, 128 * t:128 * (t + 1)], wo[:, a, :],
                                                start=(a == 0), stop=(a == 1))
                    last.then_inc(fu, 1)
                pe.wait_ge(norm_ready, 1)
                for h in range(2):
                    bank, fu = claim(("T", h))
                    for k, t in enumerate(transposed_tiles(h)):
                        last = nc.tensor.transpose(ps[:, bank, 128 * k:128 * (k + 1)], h_nat[:, t, :], ident)
                    last.then_inc(fu, 1)
                for h in range(2):
                    _, _, fr, u = ring(("T", h))
                    pe.wait_ge(fr, u + 1)
                bank, fu = claim(("lg",))
                for t in range(TT):
                    last = nc.tensor.matmul(ps[:, bank, E0 * t:E0 * (t + 1)], hT[:, 128 * t:128 * (t + 1)], rw[:],
                                            start=True, stop=True)
                last.then_inc(fu, 1)
                pe.wait_ge(w_in, 16 * 6)
                for e in range(EP):
                    for h in range(2):
                        for w, wt in (("a", w1), ("b", w3)):
                            bank, fu = claim((w, e, h))
                            nc.tensor.matmul(ps[:, bank, 0:HALF], wt[:, 2 * e:2 * e + 2, :].rearrange("p e h -> p (e h)"),
                                             hT[:, h * HALF:(h + 1) * HALF], start=True, stop=True).then_inc(fu, 1)
                pe.wait_ge(H_ready, 2 * EP)
                for t in range(TT):
                    tok = slice(128 * t, 128 * (t + 1))
                    for k in range(3):
                        bank, fu = claim(("y", t, k))
                        if k < 2:
                            for e in range(4):
                                last = nc.tensor.matmul(ps[:, bank, D * e:D * (e + 1)], H[64 * k:64 * k + 64, e, tok],
                                                        w2[64 * k:64 * k + 64, e, :], start=True, stop=True)
                        else:
                            last = nc.tensor.matmul(ps[:, bank, 0:D], H[:, EP - 1, tok], w2[:, EP - 1, :],
                                                    start=True, stop=True)
                        last.then_inc(fu, 1)


def phase_attention1(nc, A, sem, sems, ps, T, ctx_rows):
    ident, ident_bf, x_nat, h_nat, ctx_mv, AT1 = (T[k] for k in "ident ident_bf x_nat h_nat ctx_mv AT1".split())
    SCALE = float(HD1) ** -0.5
    INNER = HEADS * HD1
    NT = KT + 1
    with ExitStack() as st:
        def sb(name, shape, dt=F32, stack=st):
            return stack.enter_context(nc.sbuf_tensor(name, shape, dt))
        wkT = [sb(f"b_wkT{i}", [128, NJ, 128]) for i in range(2)]
        wv = [sb(f"b_wv{i}", [128, HEADS, HD1 + 1]) for i in range(2)]
        wq = sb("b_wq", [128, INNER])
        lT = sb("b_lT", [128, NTOK])
        ctx_r = sb("b_ctx_r", [KP, B * KT])

        with ExitStack() as pre:
            wq_raw = sb("b_wq_raw", [128, INNER], stack=pre)
            wkv_raw = sb("b_wkv_raw", [128, 2 * INNER], stack=pre)
            gb = sb("b_gb", [128, 4], stack=pre)
            M = [sb(f"b_M{i}", [128, 128], stack=pre) for i in range(2)]
            ones = sb("b_ones", [1, 128], stack=pre)
            w_in, gb_in, own = sem("w_w_in"), sem("w_gb_in"), sem("w_own")
            var_ready, root_done, M_ready, l_ready = (sem("w_" + n) for n in "var_ready root_done M_ready l_ready".split())
            full, free = sems("w_full", 8), sems("w_free", 8)
            names = [("wkT", i, h) for i in range(2) for h in range(2)] + [("wv", i, h) for i in range(2) for h in range(2)] \
                + [("wq", h) for h in range(2)] + [("T", h) for h in range(2)]
            ring = Ring(list(range(8)), names, full, free)
            with nc.Block() as block:
                @block.sync
                def _(sp):
                    for k, n in enumerate(("ln_m_g", "ln_m_b", "ln_l_g", "ln_l_b")):
                        sp.dma_start(gb[:, k:k + 1], A["L1_xattn_" + n].rearrange("(p a) -> p a", a=1)).then_inc(gb_in, 16)
                    sp.dma_start(wkv_raw[:], A["L1_xattn_Wkv"]).then_inc(w_in, 16)
                    sp.dma_start(wq_raw[:], A["L1_xattn_Wq"]).then_inc(w_in, 16)

                @block.vector
                def _(v):
                    chain = Chain(v, own)
                    nc.vector.memset(ones[:], 1.0)
                    for i in range(2):
                        last = nc.vector.memset(wv[i][:, :, HD1:], 0.0)
                    chain.link(last)
                    for i in range(2):
                        last = nc.vector.memset(wv[i][0:1, :, HD1:], 1.0)
                    v.wait_ge(gb_in, 64)
                    for i in range(2):
                        last = nc.vector.tensor_scalar(M[i][:], ident, gb[:, 2 * i:2 * i + 1], None, ALU.mult)
                    chain.link(last)
                    for i in range(2):
                        nc.vector.tensor_scalar(M[i][0:1, 1:128], ones[:, 1:128], gb[0:1, 2 * i:2 * i + 1], -1.0,
                                                ALU.mult, ALU.mult)
                        last = nc.vector.tensor_copy(M[i][:, 0:1], gb[:, 2 * i + 1:2 * i + 2])
                    last.then_inc(M_ready, 1)
                    chain.link(nc.vector.tensor_scalar(ctx_r[:], ctx_mv[:, :, 1], LN_EPS, None, ALU.add))
                    layer_norm(v, chain, var_ready, root_done, 1, x_nat, h_nat, T["stats"], T["mv"], T["rstd"])
                    layer_norm(v, chain, var_ready, root_done, 2, h_nat, h_nat, T["stats"], T["mv"], T["rstd"])
                    nc.vector.memset(h_nat[:, :, 0:1], 1.0).then_inc(l_ready, 1)
                    v.wait_ge(root_done, 3)
                    nc.vector.reciprocal(ctx_r[:], ctx_r[:])
                    for h in range(2):
                        bank, fu, fr, u = ring(("T", h))
                        v.wait_ge(fu, u + 1)
                        n = 128 * len(transposed_tiles(h))
                        nc.vector.tensor_copy(lT[:, 512 * h:512 * h + n], ps[:, bank, 0:n]).then_inc(fr, 1)

                @block.scalar
                def _(act):
                    for r in range(2):
                        act.wait_ge(var_ready, r + 1)
                        nc.scalar.activation(T["rstd"][:], T["rstd"][:], ACT.Sqrt).then_inc(root_done, 1)
                    nc.scalar.activation(ctx_r[:], ctx_r[:], ACT.Sqrt).then_inc(root_done, 1)
                    for name in names:
                        bank, fu, fr, u = ring(name)
                        if name[0] == "T":
                            continue
                        act.wait_ge(fu, u + 1)
                        h = name[-1]
                        if name[0] == "wkT":
                            dst = wkT[name[1]][:, 4 * h:4 * h + 4, :].rearrange("p j f -> p (j f)")
                            src = ps[:, bank, :]
                        elif name[0] == "wv":
                            dst = wv[name[1]][:, 8 * h:8 * h + 8, 0:HD1]
                            src = ps[:, bank, :].rearrange("p (j d) -> p j d", j=8)
                        else:
                            dst, src = wq[:, 512 * h:512 * (h + 1)], ps[:, bank, :]
                        nc.scalar.activation(dst, src, ACT.Copy).then_inc(fr, 1)

                @block.tensor
                def _(pe):
                    pe.wait_ge(w_in, 32)
                    pe.wait_ge(M_ready, 1)
                    for name in names:
                        bank, fu, fr, u = ring(name)
                        at_least(pe, fr, u)
                        h = name[-1]
                        if name[0] == "wkT":
                            for k in range(4):
                                j = 4 * h + k
                                last = nc.tensor.matmul(ps[:, bank, 128 * k:128 * (k + 1)],
                                                        wkv_raw[:, 128 * j:128 * (j + 1)], M[name[1]][:], start=True, stop=True)
                        elif name[0] == "wv":
                            last = nc.tensor.matmul(ps[:, bank, :], M[name[1]][:],
                                                    wkv_raw[:, INNER + 512 * h:INNER + 512 * (h + 1)], start=True, stop=True)
                        elif name[0] == "wq":
                            last = nc.tensor.matmul(ps[:, bank, :], M[1][:], wq_raw[:, 512 * h:512 * (h + 1)],
                                                    start=True, stop=True)
                        else:
                            if h == 0:
                                pe.wait_ge(l_ready, 1)
                            for k, t in enumerate(transposed_tiles(h)):
                                last = nc.tensor.transpose(ps[:, bank, 128 * k:128 * (k + 1)], h_nat[:, t, :], ident)
                        last.then_inc(fu, 1)

        ctx = [sb(f"b_ctx{s}", [KP, KT, D]) for s in range(2)]
        c_mv = sb("b_c_mv", [KP, KT, 2])
        y = [sb(f"b_y{s}", [KP, KT, D]) for s in range(2)]
        yT_hi = [sb(f"b_yT_hi{s}", [128, NCTX], F32R) for s in range(2)]
        yT_lo = [sb(f"b_yT_lo{s}", [128, NCTX], F32R) for s in range(2)]
        yT_bf = sb("b_yT_bf", [128, NCTX], BF16)
        l_f = sb("b_l_f", [128, NQ])
        l_hi = [sb(f"b_l_hi{s}", [128, 128], F32R) for s in range(2)]
        l_lo = [sb(f"b_l_lo{s}", [128, 128], F32R) for s in range(2)]
        l_bf = sb("b_l_bf", [128, NQ], BF16)
        l_nat = [sb(f"b_l_nat{s}", [NQ, D]) for s in range(2)]
        q_bd = sb("b_q_bd", [128, NJ, 2, NQ])
        Q_f = [sb(f"b_Q_f{i}", [128, NJ, 2, NQ]) for i in range(2)]
        Q_bf = [sb(f"b_Q_bf{i}", [128, HQ], BF16) for i in range(2)]
        Q_hi = [[sb(f"b_Q_hi{s}{i}", [128, HQ], F32R) for i in range(2)] for s in range(2)]
        Q_lo = [[sb(f"b_Q_lo{s}{i}", [128, HQ], F32R) for i in range(2)] for s in range(2)]
        mx = sb("b_mx", [PAIR, NC + 1, NJ])
        negm = sb("b_negm", [PAIR, NJ], BF16)
        P = [sb(f"b_P{k}", [KP, 2, HALF]) for k in range(2)]
        U = [sb(f"b_U{i}", [128, HEADS, NQ]) for i in range(2)]
        rden = sb("b_rden", [NQ, HEADS])
        o_nat = sb("b_o_nat", [NQ, HEADS, HD1])

        ctx_in = sems("b_ctx_in", 2)
        aux_full, aux_free = sems("b_aux_full", 2), sems("b_aux_free", 2)
        s_full, exp_done, p_used = sems("b_s_full", 2), sems("b_exp_done", 2), sems("b_p_used", 2)
        (y_ready, hi_ready, bf_ready, l_ready, Q_bf_ready, mx_ready, Q_ready, u_free, own_v, own_p, pool_turn,
         pe_turn) = (sem("b_" + n) for n in
            "y_ready hi_ready bf_ready l_ready Q_bf_ready mx_ready Q_ready u_free own_v own_p pool_turn pe_turn".split())

        prep = [("l_nat",), ("q",)] + [("Q", i, a) for i in range(2) for a in range(2)] + [("T", c) for c in range(NC)] \
            + [("max", c, j) for c in range(NC) for j in range(NJ)] + [("max_l",)] + [("row", h) for h in range(2)]
        fin = [("Ul", h) for h in range(2)] + [("out", k) for k in range(4)] + [("oT", h) for h in range(2)]
        ring = TwoStageRing([6, 7], prep, fin, aux_full, aux_free)
        aux_prep, aux_fin = ring.prep, ring.fin

        def order(b):
            first, last = isinstance(b, int) and b == 0, isinstance(b, int) and b == B - 1
            groups = []
            for t in range(NT):
                groups.append([("scores", t)])
                if t == 0 and not first:
                    groups.append([("fin", n) for n in fin if n[0] == "Ul"])
                if t:
                    groups += [[("weigh", (t - 1, h))] for h in range(2)]
            rest = [] if first else [("fin", n) for n in fin if n[0] != "Ul"]
            rest += [] if last else [("prepare", n) for n in prep]
            return sum(groups[:3], []) + spread(groups[3:-3], rest) + sum(groups[-3:], [])

        def s_use(b, t):
            return t % 2, b * (NT // 2 + 1 if t % 2 == 0 else NT // 2) + t // 2

        with nc.Block() as block:
            @block.sync
            def _(sp):
                def load(b, s):
                    if not (isinstance(b, int) and b < 2):
                        sp.wait_ge(y_ready, b - 1)
                    sp.dma_start(ctx[s][:], ctx_rows[b]).then_inc(ctx_in[s], 16)
                load(0, 0)
                load(1, 1)
                with sp.Fori(1, B // 2) as i:
                    load(2 * i, 0)
                    load(2 * i + 1, 1)

            @block.gpsimd
            def _(pool):
                def step(b, s):
                    if not (isinstance(b, int) and b < 2):
                        pool.wait_ge(p_used[1], 6 * (b - 1))
                        pool.sem_inc(pool_turn, 1)
                    nc.gpsimd.tensor_copy(c_mv[:, :, 0], ctx_mv[:, bass.ds(b * KT, KT), 0])
                    nc.gpsimd.tensor_copy(c_mv[:, :, 1], ctx_r[:, bass.ds(b * KT, KT)]).then_inc(own_p, 1)
                    pool.wait_ge(own_p, 2 * b + 1)
                    pool.sem_inc(pool_turn, 1)
                    pool.wait_ge(ctx_in[s], 8 * (b - s) + 16)
                    pool.sem_inc(pool_turn, 1)
                    for t in range(KT):
                        last = nc.gpsimd.tensor_scalar(y[s][:, t, :], ctx[s][:, t, :], c_mv[:, t, 0:1], c_mv[:, t, 1:2],
                                                       ALU.subtract, ALU.mult)
                    last.then_inc(own_p, 1)
                    pool.wait_ge(own_p, 2 * b + 2)
                    pool.sem_inc(pool_turn, 1)
                    nc.gpsimd.memset(y[s][:, :, 0:1], 1.0).then_inc(y_ready, 1)
                    for c in range(NC):
                        pool.wait_ge(hi_ready, b * NC + c + 1)
                        pool.sem_inc(pool_turn, 1)
                        nc.gpsimd.tensor_copy(yT_bf[:, c * CH:(c + 1) * CH],
                                              yT_hi[s][:, c * CH:(c + 1) * CH].bitcast(F32)).then_inc(bf_ready, 1)
                step(0, 0)
                step(1, 1)
                with pool.Fori(1, B // 2) as i:
                    step(2 * i, 0)
                    step(2 * i + 1, 1)

            @block.vector
            def _(v):
                chain = Chain(v, own_v)

                def prepare(b, s):
                    at_least(v, p_used[1], 6 * (b - 1))
                    chain.link(nc.vector.tensor_copy(l_f[:], lT[:, bass.ds(b * NQ, NQ)]))
                    nc.vector.tensor_copy(l_bf[:], l_f[:])
                    chain.link(nc.vector.tensor_copy(l_hi[s][:, 0:NQ], l_f[:]))
                    nc.vector.tensor_tensor(l_lo[s][:, 0:NQ], l_f[:], l_hi[s][:, 0:NQ].bitcast(F32), ALU.subtract).then_inc(l_ready, 1)
                    bank, fu, fr, u = aux_prep(("q",), b)
                    v.wait_ge(fu, u + 1)
                    for a in range(2):
                        rows = slice(64 * a, 64 * a + 64)
                        last = nc.vector.tensor_copy(q_bd[rows, :, a, :],
                                                     ps[rows, bank, 0:HALF].rearrange("p (j q) -> p j q", j=NJ))
                    last.then_inc(fr, 1)
                    for i in range(2):
                        for a in range(2):
                            bank, fu, fr, u = aux_prep(("Q", i, a), b)
                            v.wait_ge(fu, u + 1)
                            nc.vector.tensor_copy(Q_f[i][:, 4 * a:4 * a + 4].rearrange("p j a q -> p (j a q)"),
                                                  ps[:, bank, 0:HALF]).then_inc(fr, 1)
                            v.wait_ge(fr, u + 1)
                        nc.vector.tensor_copy(Q_bf[i][:], Q_f[i][:].rearrange("p j a q -> p (j a q)")).then_inc(Q_bf_ready, 1)
                    for c in range(NC):
                        bank, fu, fr, u = aux_prep(("T", c), b)
                        v.wait_ge(hi_ready, b * NC + c + 1)
                        nc.vector.tensor_tensor(yT_lo[s][:, c * CH:(c + 1) * CH], ps[:, bank, 0:CH],
                                                yT_hi[s][:, c * CH:(c + 1) * CH].bitcast(F32), ALU.subtract).then_inc(fr, 1)
                    for c in range(NC):
                        for j in range(NJ):
                            bank, fu, fr, u = aux_prep(("max", c, j), b)
                            v.wait_ge(fu, u + 1)
                            nc.vector.tensor_reduce(mx[:, c, j:j + 1], ps[0:PAIR, bank, 0:CH], AX.X, ALU.max).then_inc(fr, 1)
                    bank, fu, fr, u = aux_prep(("max_l",), b)
                    v.wait_ge(fu, u + 1)
                    nc.vector.tensor_reduce(mx[:, NC, :], ps[0:PAIR, bank, 0:HALF].rearrange("p (j k) -> p j k", j=NJ), AX.X,
                                            ALU.max).then_inc(fr, 1)
                    v.wait_ge(fr, u + 1)
                    nc.vector.tensor_reduce(negm[:], mx[:].rearrange("p c j -> p j c"), AX.X, ALU.max,
                                            negate=True).then_inc(mx_ready, 1)
                    for h in range(2):
                        bank, fu, fr, u = aux_prep(("row", h), b)
                        v.wait_ge(fu, u + 1)
                        for i in range(2):
                            row = Q_f[i][0:1].rearrange("p j a q -> p (j a q)")[:, h * HALF:(h + 1) * HALF]
                            last = nc.vector.tensor_tensor(row, row, ps[0:1, bank, 0:HALF], ALU.add)
                        last.then_inc(fr, 1)
                    v.wait_ge(fr, u + 1)
                    for i in range(2):
                        last = nc.vector.tensor_copy(Q_hi[s][i][:], Q_f[i][:].rearrange("p j a q -> p (j a q)"))
                    chain.link(last)
                    for i in range(2):
                        last = nc.vector.tensor_tensor(Q_lo[s][i][:], Q_f[i][:].rearrange("p j a q -> p (j a q)"),
                                                       Q_hi[s][i][:].bitcast(F32), ALU.subtract)
                    last.then_inc(Q_ready, 1)

                def finish(b):
                    for k in range(4):
                        bank, fu, fr, u = aux_fin(("out", k), b)
                        v.wait_ge(fu, u + 1)
                        o = ps[0:NQ, bank, 0:4 * (HD1 + 1)].rearrange("p (h w) -> p h w", h=4)
                        chain.link(nc.vector.reciprocal(rden[:, 4 * k:4 * k + 4], o[:, :, HD1]))
                        last = nc.vector.tensor_tensor(o_nat[:, 4 * k:4 * k + 4, :], o[:, :, 0:HD1],
                                                       rden[:, 4 * k:4 * k + 4].unsqueeze(2).broadcast_to((NQ, 4, HD1)), ALU.mult)
                        last.then_inc(fr, 1)

                def step(b, s):
                    if not (isinstance(b, int) and b == 0):
                        finish(b - 1)
                    if not (isinstance(b, int) and b == B - 1):
                        prepare(b + 1, 1 - s)
                for buf in l_hi + l_lo:
                    nc.vector.memset(buf[:, NQ:].bitcast(F32), 0.0)
                last = nc.vector.memset(q_bd[:], 0.0)
                chain.link(last)
                prepare(0, 0)
                batch_loop(v, chain, step)
                finish(B - 1)

            @block.scalar
            def _(act):
                def prepare(b, s, name):
                    kind = name[0]
                    if kind not in ("T", "l_nat"):
                        return
                    bank, fu, fr, u = aux_prep(name, b)
                    act.wait_ge(fu, u + 1)
                    if kind == "T":
                        c = name[1]
                        nc.scalar.activation(yT_hi[s][:, c * CH:(c + 1) * CH], ps[:, bank, 0:CH], ACT.Copy).then_inc(hi_ready, 1)
                    else:
                        nc.scalar.activation(l_nat[s][:], ps[0:NQ, bank, 0:D], ACT.Copy).then_inc(fr, 1)

                def finish(b, name):
                    kind, k = name
                    if kind == "out":
                        return
                    bank, fu, fr, u = aux_fin(name, b)
                    act.wait_ge(fu, u + 1)
                    if kind == "Ul":
                        nc.scalar.activation(U[1][:, 8 * k:8 * k + 8, :].rearrange("p h q -> p (h q)"), ps[:, bank, 0:HALF],
                                             ACT.Copy).then_inc(fr, 1)
                    else:
                        nc.scalar.activation(AT1[:, 4 * k:4 * k + 4, bass.ds(b * NQ, NQ)],
                                             ps[:, bank, 0:4 * NQ].rearrange("p (j q) -> p j q", j=4), ACT.Copy).then_inc(fr, 1)

                def step(b, s):
                    items = order(b)
                    if items[1][0] == "fin":
                        items = items[1:3] + items[0:1] + items[3:]
                    for kind, what in items:
                        if kind == "scores":
                            k, u = s_use(b, what)
                            rows = KP if what < KT else NQ
                            act.wait_ge(s_full[k], u + 1)
                            at_least(act, p_used[k], 6 * b + what // 2)
                            nc.scalar.activation(P[k][0:rows], ps[0:rows, 2 * k:2 * k + 2, 0:HALF], ACT.Exp,
                                                 scale=SCALE).then_inc(exp_done[k], 1)
                        elif kind == "weigh":
                            if what == (KT - 1, 1):
                                act.wait_ge(p_used[1], 6 * (b + 1))
                                nc.scalar.activation(U[0][:].rearrange("p (a h) q -> p a (h q)", a=2), ps[:, 4:6, 0:HALF],
                                                     ACT.Copy).then_inc(u_free, 1)
                        elif kind == "fin":
                            finish(b - 1, what)
                        else:
                            prepare(b + 1, 1 - s, what)
                for n in prep:
                    prepare(0, 0, n)
                batch_loop(act, Chain(act, None), step)
                for n in fin:
                    finish(B - 1, n)

            @block.tensor
            def _(pe):
                def prepare(b, s, name):
                    kind = name[0]
                    bank, fu, fr, u = aux_prep(name, b)
                    at_least(pe, fr, u)
                    if kind == "l_nat":
                        pe.wait_ge(l_ready, b + 1)
                        pe.sem_inc(pe_turn, 1)
                        last = nc.tensor.transpose(ps[0:NQ, bank, 0:D], l_f[:], ident)
                    elif kind == "q":
                        for j in range(NJ):
                            last = nc.tensor.matmul(ps[:, bank, NQ * j:NQ * (j + 1)], wq[:, 128 * j:128 * (j + 1)], l_f[:],
                                                    start=True, stop=True)
                    elif kind == "Q":
                        i, a = name[1:]
                        if (i, a) == (0, 0):
                            _, _, fq, uq = aux_prep(("q",), b)
                            pe.wait_ge(fq, uq + 1)
                        for k in range(4):
                            j = 4 * a + k
                            last = nc.tensor.matmul(ps[:, bank, PAIR * k:PAIR * (k + 1)], wkT[i][:, j, :],
                                                    q_bd[:, j].rearrange("p a q -> p (a q)"), start=True, stop=True)
                    elif kind == "T":
                        c = name[1]
                        if c == 0:
                            pe.wait_ge(y_ready, b + 1)
                        for k in range(4):
                            last = nc.tensor.transpose(ps[:, bank, KP * k:KP * (k + 1)], y[s][:, 4 * c + k, :],
                                                       ident[0:KP, 0:KP])
                    elif kind == "max":
                        c, j = name[1:]
                        if j == 0:
                            pe.wait_ge(bf_ready, b * NC + c + 1)
                            pe.wait_ge(Q_bf_ready, 2 * b + 2)
                        last = nc.tensor.matmul(ps[0:PAIR, bank, 0:CH], Q_bf[0][:, PAIR * j:PAIR * (j + 1)],
                                                yT_bf[:, c * CH:(c + 1) * CH], start=True, stop=True)
                    elif kind == "max_l":
                        for j in range(NJ):
                            last = nc.tensor.matmul(ps[0:PAIR, bank, NQ * j:NQ * (j + 1)], Q_bf[1][:, PAIR * j:PAIR * (j + 1)],
                                                    l_bf[:], start=True, stop=True)
                    else:
                        h = name[1]
                        if h == 0:
                            pe.wait_ge(mx_ready, b + 1)
                        for k in range(4):
                            last = nc.tensor.matmul(ps[0:1, bank, PAIR * k:PAIR * (k + 1)], negm[:, 4 * h + k:4 * h + k + 1],
                                                    ident_bf[0:PAIR, 0:PAIR], start=True, stop=True)
                    last.then_inc(fu, 1)

                def finish(b, s, name):
                    kind, k = name
                    bank, fu, fr, u = aux_fin(name, b)
                    at_least(pe, fr, u)
                    if kind == "Ul":
                        kk, us = s_use(b, KT)
                        if k == 0:
                            pe.wait_ge(exp_done[kk], us + 1)
                        last = nc.tensor.matmul(ps[:, bank, 0:HALF], l_nat[s][:], P[kk][0:NQ, k, :], start=True, stop=True)
                    elif kind == "out":
                        if k == 0:
                            pe.wait_ge(u_free, b + 1)
                            for h in range(2):
                                _, _, fl, ul = aux_fin(("Ul", h), b)
                                pe.wait_ge(fl, ul + 1)
                        pe.sem_inc(pe_turn, 1)
                        for n in range(4):
                            h = 4 * k + n
                            o = ps[0:NQ, bank, (HD1 + 1) * n:(HD1 + 1) * (n + 1)]
                            nc.tensor.matmul(o, U[0][:, h, :], wv[0][:, h, :], start=True, stop=False)
                            last = nc.tensor.matmul(o, U[1][:, h, :], wv[1][:, h, :], start=False, stop=True)
                    else:
                        if k == 0:
                            for m in (2, 3):
                                _, _, fo, uo = aux_fin(("out", m), b)
                                pe.wait_ge(fo, uo + 1)
                        pe.sem_inc(pe_turn, 1)
                        for n in range(4):
                            j = 4 * k + n
                            last = nc.tensor.transpose(ps[:, bank, NQ * n:NQ * (n + 1)],
                                                       o_nat[:, 2 * j:2 * j + 2, :].rearrange("p h d -> p (h d)"),
                                                       ident[0:NQ, 0:NQ])
                    last.then_inc(fu, 1)

                def step(b, s):
                    for kind, what in order(b):
                        if kind == "scores":
                            t = what
                            k, u = s_use(b, t)
                            if t == 0:
                                pe.wait_ge(Q_ready, b + 1)
                            at_least(pe, exp_done[k], u)
                            i = int(t == KT)
                            if i:
                                hi, lo, rows = l_hi[s][:], l_lo[s][:], 128
                            else:
                                hi, lo, rows = yT_hi[s][:, KP * t:KP * (t + 1)], yT_lo[s][:, KP * t:KP * (t + 1)], KP
                            for h in range(2):
                                o = ps[0:rows, 2 * k + h, 0:HALF]
                                cols = slice(HALF * h, HALF * (h + 1))
                                nc.tensor.matmul(o, hi, Q_hi[s][i][:, cols], start=True, stop=False)
                                nc.tensor.matmul(o, hi, Q_lo[s][i][:, cols], start=False, stop=False)
                                last = nc.tensor.matmul(o, lo, Q_hi[s][i][:, cols], start=False, stop=True)
                            last.then_inc(s_full[k], 1)
                        elif kind == "weigh":
                            t, h = what
                            k, u = s_use(b, t)
                            if t == 0 and h == 0:
                                at_least(pe, u_free, b)
                            if h == 0:
                                pe.wait_ge(exp_done[k], u + 1)
                            last = nc.tensor.matmul(ps[:, 4 + h, 0:HALF], y[s][:, t, :], P[k][:, h, :],
                                                    start=(t == 0), stop=(t == KT - 1))
                            if h:
                                last.then_inc(p_used[k], 1)
                        elif kind == "fin":
                            finish(b - 1, 1 - s, what)
                        else:
                            prepare(b + 1, 1 - s, what)

                for n in prep:
                    prepare(0, 0, n)
                batch_loop(pe, Chain(pe, None), step)
                for n in fin:
                    finish(B - 1, 1, n)


def top2(nc, chain, iota8, lg, top, idx, idxf, hit):
    for t in range(TT):
        last = nc.vector.max(top[:, t, :], lg[:, t, :])
    chain.link(last)
    for t in range(TT):
        last = nc.vector.max_index(idx[:, t, :], top[:, t, :], lg[:, t, :])
    chain.link(last)
    chain.link(nc.vector.tensor_copy(idxf[:], idx[:]))
    for k in range(2):
        last = nc.vector.tensor_tensor(hit[:, :, k, :], idxf[:, :, k:k + 1].broadcast_to((128, TT, 8)),
                                       iota8.unsqueeze(1).broadcast_to((128, TT, 8)), ALU.is_equal)
    chain.link(last)
    chain.link(nc.vector.tensor_tensor(hit[:, :, 0, :], hit[:, :, 0, :], hit[:, :, 1, :], ALU.add))


def phase_ffn1(nc, A, sem, sems, ps, T, out_tok):
    ident, x_nat, h_nat, hT, AT1 = (T[k] for k in "ident x_nat h_nat hT AT1".split())
    KI = I1 // 128
    with ExitStack() as st:
        def sb(name, shape, dt=F32):
            return st.enter_context(nc.sbuf_tensor(name, shape, dt))
        wout = sb("g_wout", [128, NJ, D])
        gw = sb("g_gw", [E1, D])
        gwT = sb("g_gwT", [128, E1])
        eb = sb("g_eb", [128, E1])
        up = sb("g_up", [128, E1, KI, D])
        down = sb("g_down", [128, E1, I1])
        upT = [sb(f"g_upT{k}", [128, I1]) for k in range(2)]
        downT = [sb(f"g_downT{k}", [128, I1]) for k in range(2)]
        H = [sb(f"g_H{k}", [128, KI, NTOK]) for k in range(2)]
        acc = sb("g_acc", [128, TT, D])
        lg = sb("g_lg", [128, TT, E1])
        top = sb("g_top", [128, TT, 8])
        idx = sb("g_idx", [128, TT, 8], U32)
        idxf = sb("g_idxf", [128, TT, 8])
        hit = sb("g_hit", [128, TT, 2, E1])
        gate = sb("g_gate", [128, TT, E1])
        gsum = sb("g_gsum", [128, TT])

        w_in, small_in, out_done = sem("g_w_in"), sem("g_small_in"), sem("g_out_done")
        var_ready, root_done, own, norm_ready, exp_ready, exp_done, result_ready = (
            sem("g_" + n) for n in "var_ready root_done own norm_ready exp_ready exp_done result_ready".split())
        full, free = sems("g_full", 8), sems("g_free", 8)
        names = [("gT",)] + [("o", t) for t in range(TT)] + [("T", h) for h in range(2)] + [("lg",)]
        for e in range(E1 + 1):
            if e < E1:
                names += [("upT", e), ("downT", e)] + [("h", e, k, h) for k in range(KI) for h in range(2)]
            if e:
                names += [("y", e - 1, h) for h in range(2)]
        ring = Ring(list(range(8)), names, full, free)

        with nc.Block() as block:
            @block.sync
            def _(sp):
                sp.dma_start(gw[:], A["L1_ffn_gate_w"]).then_inc(small_in, 16)
                sp.dma_start(eb[:], A["L1_ffn_expert_bias"].rearrange("(a n) -> a n", a=1).broadcast_to((128, E1))).then_inc(small_in, 16)
                sp.dma_start(wout[:], A["L1_xattn_Wout"].rearrange("(j p) n -> p j n", p=128)).then_inc(small_in, 16)
                sp.dma_start(up[:], A["L1_ffn_w_up"].rearrange("e (k p) d -> p e k d", p=128)).then_inc(w_in, 16)
                sp.dma_start(down[:], A["L1_ffn_w_down"].rearrange("e p i -> p e i")).then_inc(w_in, 16)
                sp.wait_ge(result_ready, 1)
                sp.dma_start(out_tok, acc[:]).then_inc(out_done, 16)
                sp.wait_ge(out_done, 16)

            @block.vector
            def _(v):
                chain = Chain(v, own)

                def take(name):
                    bank, fu, fr, u = ring(name)
                    v.wait_ge(fu, u + 1)
                    return bank, fr, u
                bank, fr, u = take(("gT",))
                nc.vector.tensor_copy(gwT[:], ps[:, bank, 0:E1]).then_inc(fr, 1)
                for t in range(TT):
                    bank, fr, u = take(("o", t))
                    nc.vector.tensor_tensor(x_nat[:, t, :], x_nat[:, t, :], ps[:, bank, 0:D], ALU.add).then_inc(fr, 1)
                v.wait_ge(fr, u + 1)
                layer_norm(v, chain, var_ready, root_done, 1, x_nat, h_nat, T["stats"], T["mv"], T["rstd"])
                v.sem_inc(norm_ready, 1)
                for h in range(2):
                    bank, fr, u = take(("T", h))
                    n = 128 * len(transposed_tiles(h))
                    nc.vector.tensor_copy(hT[:, 512 * h:512 * h + n], ps[:, bank, 0:n]).then_inc(fr, 1)
                bank, fr, u = take(("lg",))
                v.wait_ge(small_in, 48)
                nc.vector.tensor_tensor(lg[:], ps[:, bank, 0:TT * E1].rearrange("p (t e) -> p t e", t=TT),
                                        eb[:].unsqueeze(1).broadcast_to((128, TT, E1)), ALU.add).then_inc(fr, 1)
                v.wait_ge(fr, u + 1)
                top2(nc, chain, T["iota8"], lg, top, idx, idxf, hit)
                chain.link(nc.vector.tensor_tensor(lg[:], lg[:], top[:, :, 0:1].broadcast_to((128, TT, E1)), ALU.subtract))
                v.sem_inc(exp_ready, 1)
                v.wait_ge(exp_done, 1)

                def divide(a, s):
                    chain.link(nc.vector.reciprocal(s, s))
                    chain.link(nc.vector.tensor_tensor(a, a, s.unsqueeze(2).broadcast_to((128, TT, E1)), ALU.mult))
                chain.link(nc.vector.tensor_reduce(gsum[:], lg[:], AX.X, ALU.add))
                divide(lg[:], gsum[:])
                chain.link(nc.vector.tensor_tensor(gate[:], lg[:], hit[:, :, 0, :], ALU.mult))
                chain.link(nc.vector.tensor_reduce(gsum[:], gate[:], AX.X, ALU.add))
                chain.link(nc.vector.tensor_scalar(gsum[:], gsum[:], GATE_EPS, None, ALU.add))
                divide(gate[:], gsum[:])

                def weights(e):
                    bank, fr, u = take(("upT", e))
                    nc.vector.tensor_copy(upT[e % 2][:], ps[:, bank, :]).then_inc(fr, 1)
                    bank, fr, u = take(("downT", e))
                    nc.vector.tensor_copy(downT[e % 2][:], ps[:, bank, :]).then_inc(fr, 1)
                for e in range(E1 + 1):
                    if e < E1:
                        weights(e)
                    if e == 0:
                        continue
                    for h in range(2):
                        bank, fr, u = take(("y", e - 1, h))
                        for k, t in enumerate(transposed_tiles(h)):
                            y = ps[:, bank, D * k:D * (k + 1)]
                            g = gate[:, t, e - 1:e]
                            if e == 1:
                                last = nc.vector.tensor_scalar(acc[:, t, :], y, g, None, ALU.mult)
                            else:
                                last = nc.vector.scalar_tensor_tensor(acc[:, t, :], y, g, acc[:, t, :], ALU.mult, ALU.add)
                        last.then_inc(fr, 1)
                        v.wait_ge(fr, u + 1)
                chain.link(nc.vector.tensor_tensor(x_nat[:], x_nat[:], h_nat[:], ALU.add))
                layer_norm(v, chain, var_ready, root_done, 2, acc, acc, T["stats"], T["mv"], T["rstd"])
                nc.vector.tensor_tensor(acc[:], acc[:], x_nat[:], ALU.add).then_inc(result_ready, 1)

            @block.scalar
            def _(act):
                act.wait_ge(var_ready, 1)
                nc.scalar.activation(T["rstd"][:], T["rstd"][:], ACT.Sqrt).then_inc(root_done, 1)
                act.wait_ge(exp_ready, 1)
                nc.scalar.activation(lg[:], lg[:], ACT.Exp).then_inc(exp_done, 1)
                for e in range(E1):
                    for k in range(KI):
                        for h in range(2):
                            bank, fu, fr, u = ring(("h", e, k, h))
                            act.wait_ge(fu, u + 1)
                            nc.scalar.activation(H[e % 2][:, k, h * HALF:(h + 1) * HALF], ps[:, bank, 0:HALF],
                                                 ACT.Gelu).then_inc(fr, 1)
                act.wait_ge(var_ready, 2)
                nc.scalar.activation(T["rstd"][:], T["rstd"][:], ACT.Sqrt).then_inc(root_done, 1)

            @block.tensor
            def _(pe):
                def claim(name):
                    bank, fu, fr, u = ring(name)
                    at_least(pe, fr, u)
                    return bank, fu

                def copied(name):
                    bank, fu, fr, u = ring(name)
                    pe.wait_ge(fr, u + 1)
                pe.wait_ge(small_in, 48)
                bank, fu = claim(("gT",))
                nc.tensor.transpose(ps[:, bank, 0:E1], gw[:], ident[0:E1, 0:E1]).then_inc(fu, 1)
                for t in range(TT):
                    bank, fu = claim(("o", t))
                    for j in range(NJ):
                        last = nc.tensor.matmul(ps[:, bank, 0:D], AT1[:, j, 128 * t:128 * (t + 1)], wout[:, j, :],
                                                start=(j == 0), stop=(j == NJ - 1))
                    last.then_inc(fu, 1)
                pe.wait_ge(norm_ready, 1)
                for h in range(2):
                    bank, fu = claim(("T", h))
                    for k, t in enumerate(transposed_tiles(h)):
                        last = nc.tensor.transpose(ps[:, bank, 128 * k:128 * (k + 1)], h_nat[:, t, :], ident)
                    last.then_inc(fu, 1)
                for h in range(2):
                    copied(("T", h))
                bank, fu = claim(("lg",))
                for t in range(TT):
                    last = nc.tensor.matmul(ps[:, bank, E1 * t:E1 * (t + 1)], hT[:, 128 * t:128 * (t + 1)], gwT[:],
                                            start=True, stop=True)
                last.then_inc(fu, 1)
                pe.wait_ge(w_in, 32)

                def outputs(e):
                    for k in range(KI):
                        for h in range(2):
                            copied(("h", e, k, h))
                    for h in range(2):
                        bank, fu = claim(("y", e, h))
                        for n, t in enumerate(transposed_tiles(h)):
                            for k in range(KI):
                                last = nc.tensor.matmul(ps[:, bank, D * n:D * (n + 1)], H[e % 2][:, k, 128 * t:128 * (t + 1)],
                                                        downT[e % 2][:, 128 * k:128 * (k + 1)],
                                                        start=(k == 0), stop=(k == KI - 1))
                        last.then_inc(fu, 1)
                for e in range(E1):
                    bank, fu = claim(("upT", e))
                    for k in range(KI):
                        last = nc.tensor.transpose(ps[:, bank, 128 * k:128 * (k + 1)], up[:, e, k, :], ident)
                    last.then_inc(fu, 1)
                    bank, fu = claim(("downT", e))
                    for k in range(KI):
                        last = nc.tensor.transpose(ps[:, bank, 128 * k:128 * (k + 1)], down[:, e, 128 * k:128 * (k + 1)], ident)
                    last.then_inc(fu, 1)
                    copied(("upT", e))
                    copied(("downT", e))
                    for k in range(KI):
                        for h in range(2):
                            bank, fu = claim(("h", e, k, h))
                            nc.tensor.matmul(ps[:, bank, 0:HALF], upT[e % 2][:, 128 * k:128 * (k + 1)],
                                             hT[:, h * HALF:(h + 1) * HALF], start=True, stop=True).then_inc(fu, 1)
                    if e:
                        outputs(e - 1)
                outputs(E1 - 1)


_INS = ["x", "ctx_1024", "L0_xattn_W_v", "L0_xattn_W_k", "L0_xattn_W_q", "L0_xattn_W_o", "L0_xattn_b_o",
        "L0_ffn_router_w", "L0_ffn_router_b", "L0_ffn_routed_w1", "L0_ffn_routed_w3", "L0_ffn_routed_w2",
        "L0_ffn_shared_w1", "L0_ffn_shared_w3", "L0_ffn_shared_w2", "L1_xattn_ln_m_g", "L1_xattn_ln_m_b",
        "L1_xattn_ln_l_g", "L1_xattn_ln_l_b", "L1_xattn_Wq", "L1_xattn_Wkv", "L1_xattn_Wout",
        "L1_ffn_gate_w", "L1_ffn_expert_bias", "L1_ffn_w_up", "L1_ffn_w_down"]


def constants():
    import numpy as np
    p = np.arange(128)
    c = np.zeros((128, CONSTS), np.float32)
    c[:, 0:128] = np.eye(128)
    c[:, 128:132] = (p[:, None] % 32) // HD0 == np.arange(4)[None, :]
    c[:, 132] = p < NQ
    c[:, 133] = p >= NQ
    c[:, 134:142] = np.arange(8)
    c[:, 142:142 + HEADS] = p[:, None] // HD0 == np.arange(HEADS)[None, :]
    return c


def kernel(**inputs):
    import numpy as np
    import concourse.bacc as bacc
    from concourse.bass_utils import run_bass_kernel_spmd as run

    nc = bacc.Bacc("TRN2", target_bir_lowering=False, num_devices=1)
    arrays, aps = {}, {}
    for name, a in [(n, inputs[n]) for n in _INS] + [("consts", constants())]:
        a = np.ascontiguousarray(a)
        arrays[f"in_{name}_dram"] = a
        aps[name] = nc.dram_tensor(f"in_{name}_dram", a.shape, mybir.dt.from_np(a.dtype), kind="ExternalInput").ap()
    out = nc.dram_tensor("out_0_dram", (B, NQ, D), F32, kind="ExternalOutput").ap()
    build(nc, aps, out)
    r = run(nc, [arrays], core_ids=[0])
    return r.results[0]["out_0_dram"]
```

```python
from contextlib import ExitStack

import concourse.bass as bass
from concourse import mybir

F32 = mybir.dt.float32
F32R = mybir.dt.float32r
BF16 = mybir.dt.bfloat16
U32 = mybir.dt.uint32
ALU = mybir.AluOpType
ACT = mybir.ActivationFunctionType
AX = mybir.AxisListType

B, NQ, D = 16, 56, 128
NCTX = 1500
KT, KP = 12, 125
HEADS = 16
NTOK = B * NQ
TT = NTOK // 128
HALF = NTOK // 2
HQ = HEADS * NQ
PAIR = 2 * NQ
NJ = HEADS // 2
CH = 500
NC = NCTX // CH
HD0, HD1 = 8, 64
GQ = 4 * NQ
VW = 4 * HD0 + 1
VPARTS = 2 * 4 * HD0 + 1
VPAD = 66
MT = HQ // 128
E0, HID0 = 8, 64
E1, I1 = 8, 512
INNER = HEADS * HD1
LN_EPS = 1e-5
GATE_EPS = 1e-6
LAG = 2
PB = LAG + 1
SPLIT = 2
CONSTS = 128 + 4 + 2 + 8 + HEADS + VW


def at_least(eng, sem, count):
    if isinstance(count, int) and count <= 0:
        return
    eng.wait_ge(sem, count)


class Chain:

    def __init__(self, eng, sem):
        self.eng, self.sem, self.n, self.offset = eng, sem, 0, 0

    def link(self, ins):
        self.n += 1
        ins.then_inc(self.sem, 1)
        self.eng.wait_ge(self.sem, self.offset + self.n)


class Ring:

    def __init__(self, banks, names, full, free):
        self.banks, self.full, self.free = banks, full, free
        self.place = {name: k for k, name in enumerate(names)}

    def __call__(self, name):
        k = self.place[name]
        slot = k % len(self.banks)
        return self.banks[slot], self.full[slot], self.free[slot], k // len(self.banks)


class TwoStageRing:

    def __init__(self, banks, prep, fin, full, free):
        assert len(prep) % 2 == 0 and len(fin) % 2 == 0
        self.banks, self.full, self.free = banks, full, free
        self.prep_at = {n: k for k, n in enumerate(prep)}
        self.fin_at = {n: k for k, n in enumerate(fin)}
        self.p, self.f = len(prep) // 2, len(fin) // 2

    def use(self, k, before):
        return self.banks[k % 2], self.full[k % 2], self.free[k % 2], before + k // 2

    def prep(self, name, b):
        ends = max(b - 1, 0) if isinstance(b, int) else b - 1
        return self.use(self.prep_at[name], b * self.p + ends * self.f)

    def fin(self, name, b):
        prepared = min(b + 2, B) if isinstance(b, int) else b + 2
        return self.use(self.fin_at[name], prepared * self.p + b * self.f)


def batch_loop(eng, chain, step):
    step(0, 0)
    before = chain.n
    step(1, 1)
    start, stride = chain.n, 2 * (chain.n - before)
    with eng.Fori(1, B // 2 - 1) as i:
        chain.n, chain.offset = start, (i - 1) * stride
        step(2 * i, 0)
        step(2 * i + 1, 1)
    chain.n, chain.offset = start + (B // 2 - 2) * stride, 0
    step(B - 2, 0)
    step(B - 1, 1)


def spread(groups, pieces, weight):
    out, total, n = [], sum(weight(p) for p in pieces), len(groups)
    done, k = 0, 0
    for p in pieces:
        done += weight(p)
        while k < n and (k + 1) * total <= done * n:
            out += groups[k]
            k += 1
        out.append(p)
    return out + sum(groups[k:], [])


def weight(piece):
    kind, name = piece
    if name == ("row", 0):
        return 2
    return {"k": 1.5, "T": 1.5, "q": 1.5, "Q": 1.5, "max": 1.6, "row": .7}.get(name[0], 1)


def build(nc, A, out):
    x_tok = A["x"].rearrange("b q d -> (b q) d").rearrange("(t p) d -> p t d", p=128)
    out_tok = out.rearrange("b q d -> (b q) d").rearrange("(t p) d -> p t d", p=128)
    ctx_rows = A["ctx_1024"].rearrange("b (p t) d -> b p t d", p=KP)

    with ExitStack() as outer:
        def tensor(stack, name, shape, dt=F32):
            return stack.enter_context(nc.sbuf_tensor(name, shape, dt))

        def sem(name):
            return outer.enter_context(nc.semaphore(name))

        def sems(name, n):
            return [sem(f"{name}{i}") for i in range(n)]

        ps = outer.enter_context(nc.psum_tensor("ps", [128, 8, 512], F32))

        cst = tensor(outer, "cst", [128, CONSTS])
        ident = cst[:, 0:128]
        group_mask = cst[:, 128:132]
        pair_mask = cst[:, 132:134]
        iota8 = cst[:, 134:142]
        head_mask = cst[:, 142:142 + HEADS]
        fold = cst[:, 142 + HEADS:CONSTS]
        ident_bf = tensor(outer, "ident_bf", [128, 128], BF16)
        x_nat = tensor(outer, "x_nat", [128, TT, D])
        h_nat = tensor(outer, "h_nat", [128, TT, D])
        hT = tensor(outer, "hT", [128, NTOK])
        stats = tensor(outer, "stats", [128, TT, 6])
        mv = tensor(outer, "mv", [128, TT, 2])
        rstd = tensor(outer, "rstd", [128, TT])
        ctx_mv = tensor(outer, "ctx_mv", [KP, B * KT, 2])

        wkT = [tensor(outer, f"b_wkT{i}", [128, NJ, 128]) for i in range(2)]
        wv = [tensor(outer, f"b_wv{i}", [128, HEADS, HD1 + 1]) for i in range(2)]
        wq = tensor(outer, "b_wq", [128, INNER])

        with ExitStack() as l0:
            wq0 = tensor(l0, "wq0", [128, 128])
            qT = tensor(l0, "qT", [128, NTOK])
            wk0 = tensor(l0, "wk0", [128, 128])
            wv0 = tensor(l0, "wv0", [128, 128])
            q_parts = tensor(l0, "q_parts", [96, 4, NTOK], F32R)
            AT0 = tensor(l0, "AT0", [64, 2, NTOK])
            EP = E0 // 2 + 1
            f_weights = (tensor(l0, "f_wo", [64, 2, D]), tensor(l0, "f_bo", [128, D]), tensor(l0, "f_rw", [128, E0]),
                         tensor(l0, "f_rb", [128, E0]), tensor(l0, "f_w1", [128, 2 * EP, HID0]),
                         tensor(l0, "f_w3", [128, 2 * EP, HID0]),
                         tensor(l0, "f_w2", [128, EP, 2, D]))
            f_w_in, f_small_in = sem("f_w_in"), sem("f_small_in")
            phase_queries(nc, A, sem, sems, ps, locals())
            phase_attention0(nc, A, sem, sems, ps, locals(), ctx_rows)
            wq_raw = tensor(l0, "wq_raw", [128, INNER])
            wkv_raw = tensor(l0, "wkv_raw", [128, 2 * INNER])
            gb = tensor(l0, "gb", [128, 4])
            M = [tensor(l0, f"M{i}", [128, 128]) for i in range(2)]
            ones = tensor(l0, "ones", [1, 128])
            w_in, gb_in = sem("w_w_in"), sem("w_gb_in")
            phase_ffn0(nc, A, sem, sems, ps, locals())
            phase_weights1(nc, A, sem, sems, ps, locals())
        with ExitStack() as l1:
            AT1 = tensor(l1, "AT1", [128, NJ, NTOK])
            phase_attention1(nc, A, sem, sems, ps, locals(), ctx_rows)
            phase_ffn1(nc, A, sem, sems, ps, locals(), out_tok)


def layer_norm(v, chain, act_ready, act_done, round_, src, dst, stats, mv, rstd):
    for t in range(TT):
        last = v.bn_stats(stats[:, t, :], src[:, t, :])
    chain.link(last)
    for t in range(TT):
        last = v.bn_aggr(mv[:, t, :], stats[:, t, :])
    chain.link(last)
    v.tensor_scalar(rstd[:], mv[:, :, 1], LN_EPS, None, ALU.add).then_inc(act_ready, 1)
    v.wait_ge(act_done, round_)
    chain.link(v.reciprocal(rstd[:], rstd[:]))
    for t in range(TT):
        last = v.tensor_scalar(dst[:, t, :], src[:, t, :], mv[:, t, 0:1], rstd[:, t:t + 1], ALU.subtract, ALU.mult)
    chain.link(last)


def row_tiles(k):
    return range(0, 3) if k == 0 else range(2 * k + 1, 2 * k + 3)


def row_columns(k):
    return slice(128 * row_tiles(k).start, 128 * row_tiles(k).stop)


def transposed_tiles(h):
    return range(0, 4) if h == 0 else range(4, TT)


def phase_queries(nc, A, sem, sems, ps, T):
    cst, ident, ident_bf, x_nat, h_nat, hT, q_parts = (
        T[k] for k in "cst ident ident_bf x_nat h_nat hT q_parts".split())
    const_in, x_in, w0_in = sem("const_in"), sem("x_in"), sem("w0_in")
    var_ready, root_done, norm_ready = sem("q_var_ready"), sem("q_root_done"), sem("q_norm_ready")
    hT_ready, own = sem("q_hT_ready"), sem("q_own")
    q_full, w_ready, q_hi_ready, q_lo_ready = (sem("q_" + n) for n in "full w_ready hi_ready lo_ready".split())
    wo, bo, rw, rb, w1, w3, w2 = T["f_weights"]
    w_in, small_in, zero_ready, EP = T["f_w_in"], T["f_small_in"], sem("f_zero_ready"), T["EP"]
    wq3 = T["l0"].enter_context(nc.sbuf_tensor("wq3", [128, 4, 3, 32], F32))
    with nc.Block() as block:
        @block.gpsimd
        def _(pool):
            nc.gpsimd.memset(w2[:], 0.0).then_inc(zero_ready, 1)

        @block.sync
        def _(sp):
            sp.dma_start(cst[:], A["consts"]).then_inc(const_in, 16)
            sp.dma_start(x_nat[:], T["x_tok"]).then_inc(x_in, 16)
            sp.dma_start(T["wq0"][:], A["L0_xattn_W_q"]).then_inc(w0_in, 16)
            sp.dma_start(T["wk0"][:], A["L0_xattn_W_k"]).then_inc(w0_in, 16)
            sp.dma_start(T["wv0"][:], A["L0_xattn_W_v"]).then_inc(w0_in, 16)
            wo_rows = A["L0_xattn_W_o"].rearrange("(j a d) n -> a j d n", a=2, d=HD0)
            for a in range(2):
                for j in range(NJ):
                    sp.dma_start(wo[HD0 * j:HD0 * (j + 1), a, :], wo_rows[a, j]).then_inc(small_in, 16)
            sp.dma_start(bo[:], A["L0_xattn_b_o"].rearrange("(a n) -> a n", a=1).broadcast_to((128, D))).then_inc(small_in, 16)
            sp.dma_start(rb[:], A["L0_ffn_router_b"].rearrange("(a n) -> a n", a=1).broadcast_to((128, E0))).then_inc(small_in, 16)
            sp.dma_start(rw[:], A["L0_ffn_router_w"]).then_inc(small_in, 16)
            for w, name in ((w1, "w1"), (w3, "w3")):
                sp.dma_start(w[:, 0:E0, :], A["L0_ffn_routed_" + name].rearrange("e d h -> d e h")).then_inc(w_in, 16)
                sp.dma_start(w[:, E0:, :], A["L0_ffn_shared_" + name].rearrange("e d h -> d e h")).then_inc(w_in, 16)
            routed = A["L0_ffn_routed_w2"].rearrange("(k e) h d -> e h k d", e=2)
            sp.wait_ge(zero_ready, 1)
            for e in range(2):
                sp.dma_start(w2[HID0 * e:HID0 * (e + 1), 0:EP - 1, e, :], routed[e]).then_inc(w_in, 16)
            sp.dma_start(w2[:, EP - 1, 0, :], A["L0_ffn_shared_w2"].rearrange("e h d -> (e h) d")).then_inc(w_in, 16)

        @block.vector
        def _(v):
            chain = Chain(v, own)
            v.wait_ge(const_in, 16)
            v.wait_ge(x_in, 16)
            nc.vector.tensor_copy(ident_bf[:], ident)
            layer_norm(v, chain, var_ready, root_done, 1, x_nat, h_nat, T["stats"], T["mv"], T["rstd"])
            v.sem_inc(norm_ready, 1)
            v.wait_ge(w0_in, 48)
            nc.vector.tensor_copy(wq3[:], T["wq0"][:].rearrange("p (g c) -> p g c", g=4).unsqueeze(2)
                                  .broadcast_to((128, 4, 3, 32))).then_inc(w_ready, 1)
            for h in range(2):
                v.wait_ge(q_full, h + 1)
                n = 128 * len(transposed_tiles(h))
                nc.vector.tensor_copy(hT[:, 512 * h:512 * h + n], ps[:, h, 0:n]).then_inc(hT_ready, 1)
            for k in range(8):
                g, h = k // 2, k % 2
                lo = q_parts[32:64, g, HALF * h:HALF * (h + 1)]
                v.wait_ge(q_hi_ready, k + 1)
                nc.vector.tensor_tensor(lo, ps[32:64, (2 + k) % 8, 0:HALF], lo.bitcast(F32),
                                        ALU.subtract).then_inc(q_lo_ready, 1)

        @block.scalar
        def _(act):
            act.wait_ge(var_ready, 1)
            nc.scalar.activation(T["rstd"][:], T["rstd"][:], ACT.Sqrt).then_inc(root_done, 1)
            for k in range(8):
                g, h = k // 2, k % 2
                act.wait_ge(q_full, k + 3)
                nc.scalar.activation(q_parts[:, g, HALF * h:HALF * (h + 1)], ps[0:96, (2 + k) % 8, 0:HALF],
                                     ACT.Copy).then_inc(q_hi_ready, 1)
            for h in range(2):
                act.wait_ge(q_full, h + 11)
                nc.scalar.activation(T["qT"][:, HALF * h:HALF * (h + 1)], ps[:, 2 + h, 0:HALF], ACT.Copy)

        @block.tensor
        def _(pe):
            pe.wait_ge(const_in, 16)
            pe.wait_ge(norm_ready, 1)
            for h in range(2):
                for k, t in enumerate(transposed_tiles(h)):
                    last = nc.tensor.transpose(ps[:, h, 128 * k:128 * (k + 1)], h_nat[:, t, :], ident)
                last.then_inc(q_full, 1)
            pe.wait_ge(w_ready, 1)
            pe.wait_ge(hT_ready, 2)
            for k in range(8):
                g, h = k // 2, k % 2
                nc.tensor.matmul(ps[0:96, (2 + k) % 8, 0:HALF], wq3[:, g, :, :].rearrange("p r c -> p (r c)"),
                                 hT[:, HALF * h:HALF * (h + 1)], start=True, stop=True).then_inc(q_full, 1)
            for h in range(2):
                pe.wait_ge(q_lo_ready, h + 1)
                nc.tensor.matmul(ps[:, 2 + h, 0:HALF], T["wq0"][:], hT[:, HALF * h:HALF * (h + 1)],
                                 start=True, stop=True).then_inc(q_full, 1)


def phase_attention0(nc, A, sem, sems, ps, T, ctx_rows):
    ident, ident_bf, q_parts, AT0, ctx_mv = (T[k] for k in "ident ident_bf q_parts AT0 ctx_mv".split())
    SCALE = 1.0 / float(D) ** 0.5
    STACK = 12 * 16
    with ExitStack() as st:
        def sb(name, shape, dt=F32):
            return st.enter_context(nc.sbuf_tensor(name, shape, dt))
        ctx = [sb(f"a_ctx{s}", [KP, KT, D]) for s in range(2)]
        ctxT = sb("a_ctxT", [128, NCTX])
        k_hi = sb("a_k_hi", [128, NCTX], F32R)
        k_lo = sb("a_k_lo", [128, NCTX], F32R)
        k_bf = sb("a_k_bf", [128, NCTX], BF16)
        k_parts = [sb(f"a_k_parts{s}", [97, 4, NCTX], F32R) for s in range(2)]
        vals = [[sb(f"a_vals{s}{c}", [KP, KT // 4, 4, VPAD], F32R if c == SPLIT else F32) for c in range(4)]
                for s in range(2)]
        q_rows = [sb(f"a_q_rows{s}", [97, 4, 4, NQ], F32R) for s in range(2)]
        q_bf = sb("a_q_bf", [128, HQ], BF16)
        qT = T["qT"]
        mx = sb("a_mx", [128, MT, NC])
        negm = sb("a_negm", [128, MT], BF16)
        P = [sb(f"a_P{k}", [KP, 4, GQ]) for k in range(PB)]
        P_hi, P_lo = sb("a_P_hi", [KP, 4, GQ], F32R), sb("a_P_lo", [KP, 4, GQ], F32R)
        c_st = sb("a_c_st", [KP, KT, 6])
        c_mv = sb("a_c_mv", [KP, KT, 2])
        rden = sb("a_rden", [PAIR, NJ])
        o_T = sb("a_o_T", [VPARTS, HQ])
        o_sel = sb("a_o_sel", [PAIR, 4, 2, HD0])
        o_nat = sb("a_o_nat", [PAIR, 2 * NJ, HD0])

        ctx_in, k_stacked = sems("a_ctx_in", 2), sems("a_k_stacked", 2)
        ctx_measured = sem("a_ctx_measured")
        sp_turn = sem("a_sp_turn")
        aux_full, aux_free = sems("a_aux_full", 2), sems("a_aux_free", 2)
        k_bf_ready, q_ready, negm_ready, const_ready = (sem("a_" + n) for n in
                                                        "k_bf_ready q_ready negm_ready const_ready".split())
        s_full, exp_done = sems("a_s_full", 2), sems("a_exp_done", 2)
        lo_ready, v_hi_ready, pv_done, o_ready, o_free = (
            sem("a_" + n) for n in "lo_ready v_hi_ready pv_done o_ready o_free".split())
        own_v = sem("a_own_v")

        names = [("ctxT", c) for c in range(NC)] + [("k", c) for c in range(NC)] + [("v", c) for c in range(4)] \
            + [("max", c, j) for c in range(NC) for j in range(MT)] + [("row", k) for k in range(3)]
        fin = [("o_nat",), ("oT",)]
        aux = TwoStageRing([6, 7], names, fin, aux_full, aux_free)
        ring = aux.prep

        def order(b):
            first, last = isinstance(b, int) and b == 0, isinstance(b, int) and b == B - 1
            groups = []
            for t in range(KT):
                groups.append([("scores", t)])
                if t >= LAG:
                    groups += [[("weigh", (t - LAG, h))] for h in range(2)]
                elif not first:
                    groups += [[("late", (t + KT - LAG, h))] for h in range(2)]
            if not first:
                groups[3 * LAG - 1].append(("copy", None))
            rest = [] if first else [("fin", n) for n in fin]
            rest += [] if last else [("prepare", n) for n in names]
            return sum(groups[:3 * LAG + 1], []) + spread(groups[3 * LAG + 1:-2], rest, weight) + sum(groups[-2:], [])

        with nc.Block() as block:
            @block.sync
            def _(sp):
                def load(b, s):
                    if not (isinstance(b, int) and b < 2):
                        bank, full, free, u = ring(("ctxT", NC - 1), b - 2)
                        sp.wait_ge(free, u + 1)
                        sp.sem_inc(sp_turn, 1)
                        sp.wait_ge(ctx_measured, b - 1)
                    sp.dma_start(ctx[s][:], ctx_rows[b]).then_inc(ctx_in[s], 16)

                def stack(b, s):
                    if not (isinstance(b, int) and b < 2):
                        sp.wait_ge(pv_done, KT * (b - 1))
                        sp.sem_inc(sp_turn, 1)
                    bank, full, free, u = ring(("k", NC - 1), b)
                    sp.wait_ge(free, u + 1)
                    for g in range(4):
                        for r, part in enumerate((k_hi, k_hi, k_lo)):
                            sp.dma_start(k_parts[s][32 * r:32 * r + 32, g, :].bitcast(F32),
                                         part[32 * g:32 * g + 32, :].bitcast(F32)).then_inc(k_stacked[s], 16)
                load(0, 0)
                load(1, 1)
                for b in range(2):
                    stack(b, b)
                    load(b + 2, b)
                with sp.Fori(1, B // 2 - 1) as i:
                    for s in range(2):
                        stack(2 * i + s, s)
                        load(2 * i + s + 2, s)
                for b in (B - 2, B - 1):
                    stack(b, b % 2)

            @block.gpsimd
            def _(pool):
                for s in range(2):
                    for c in range(4):
                        if c != SPLIT:
                            nc.gpsimd.memset(vals[s][c][:, :, :, 4 * HD0:VPARTS - 1], 0.0)
                        ones = vals[s][c][:, :, :, VPARTS - 1:]
                        nc.gpsimd.memset(ones.bitcast(F32) if c == SPLIT else ones, 1.0)
                nc.gpsimd.memset(o_nat[:, NJ:, :], 0.0).then_inc(const_ready, 1)

                def queries(b, s):
                    at_least(pool, negm_ready, b)
                    nc.gpsimd.tensor_tensor(
                        q_bf[:].rearrange("p (h q) -> p h q", h=HEADS),
                        T["head_mask"].unsqueeze(2).broadcast_to((128, HEADS, NQ)),
                        qT[:, bass.ds(b * NQ, NQ)].unsqueeze(1).broadcast_to((128, HEADS, NQ)), ALU.mult)
                    at_least(pool, exp_done[1], KT // 2 * (b - 1))
                    for g in range(4):
                        last = nc.gpsimd.tensor_tensor(
                            q_rows[s][0:96, g], T["group_mask"][0:96].unsqueeze(2).broadcast_to((96, 4, NQ)),
                            q_parts[:, g, bass.ds(b * NQ, NQ)].bitcast(F32).unsqueeze(1).broadcast_to((96, 4, NQ)), ALU.mult)
                    last.then_inc(q_ready, 1)

                def step(b, s):
                    if not (isinstance(b, int) and b == B - 1):
                        queries(b + 1, 1 - s)
                    for t in range(SPLIT, KT, 4):
                        pool.wait_ge(exp_done[t % 2], KT // 2 * b + t // 2 + 1)
                        nc.gpsimd.tensor_tensor(P_lo[:], P[t % PB][:], P_hi[:].bitcast(F32),
                                                ALU.subtract).then_inc(lo_ready, 1)
                queries(0, 0)
                pool.wait_ge(q_ready, 1)
                for s in range(2):
                    nc.gpsimd.memset(k_parts[s][96:97].bitcast(F32), 1.0).then_inc(const_ready, 1)
                    pool.wait_ge(const_ready, s + 2)
                batch_loop(pool, Chain(pool, None), step)

            @block.vector
            def _(v):
                chain = Chain(v, own_v)

                def prepare(b, s, name):
                    kind, c = name[0:2]
                    bank, full, free, u = ring(name, b)
                    if kind == "ctxT":
                        if c == 0:
                            v.wait_ge(ctx_in[s], 8 * (b - s) + 16)
                        for t in range(4 * c, 4 * c + 4):
                            last = nc.vector.bn_stats(c_st[:, t, :], ctx[s][:, t, :])
                        if c == NC - 1:
                            last.then_inc(ctx_measured, 1)
                    elif kind == "k":
                        cols = slice(c * CH, (c + 1) * CH)
                        v.wait_ge(k_bf_ready, b * NC + c + 1)
                        nc.vector.tensor_tensor(k_lo[:, cols], ps[:, bank, 0:CH], k_hi[:, cols].bitcast(F32),
                                                ALU.subtract).then_inc(free, 1)
                    elif kind == "v":
                        if c == SPLIT:
                            v.wait_ge(ctx_measured, b + 1)
                            v.wait_ge(v_hi_ready, b + 1)
                            nc.vector.tensor_tensor(
                                vals[s][c][:, :, :, 4 * HD0:VPARTS - 1],
                                ps[0:KP, bank, 0:384].rearrange("p (t g w) -> p t g w", t=3, g=4),
                                vals[s][c][:, :, :, 0:4 * HD0].bitcast(F32), ALU.subtract).then_inc(free, 1)
                            for t in range(KT):
                                last = nc.vector.bn_aggr(c_mv[:, t, :], c_st[:, t, :])
                            chain.link(last)
                            nc.vector.tensor_copy(ctx_mv[:, bass.ds(b * KT, KT), :], c_mv[:])
                    elif kind == "max":
                        v.wait_ge(full, u + 1)
                        nc.vector.tensor_reduce(mx[:, name[2], c:c + 1], ps[:, bank, 0:CH], AX.X, ALU.max).then_inc(free, 1)
                        if name == ("max", NC - 1, MT - 1):
                            v.wait_ge(free, u + 1)
                            nc.vector.tensor_reduce(negm[:], mx[:], AX.X, ALU.max, negate=True).then_inc(negm_ready, 1)
                    else:
                        v.wait_ge(full, u + 1)
                        cols = row_columns(c)
                        nc.vector.tensor_copy(q_rows[s][96:97].rearrange("p g h q -> p (g h q)")[:, cols],
                                              ps[96:97, bank, 0:cols.stop - cols.start]).then_inc(free, 1)

                def finish(b, s):
                    bank, full, free, u = aux.fin(("o_nat",), b)
                    v.wait_ge(full, u + 1)
                    o = ps[0:PAIR, bank, 0:NJ * VW].rearrange("p (g a w) -> p g a w", g=4, a=2)
                    for a in range(2):
                        nc.vector.tensor_scalar(o_sel[:, :, a, :], o[:, :, a, 16 * a:16 * a + 8],
                                                T["pair_mask"][0:PAIR, 0:1], None, ALU.mult)
                    chain.link(nc.vector.reciprocal(rden[:].rearrange("p (g a) -> p g a", g=4), o[:, :, :, VW - 1]))
                    for a in range(2):
                        last = nc.vector.scalar_tensor_tensor(o_sel[:, :, a, :], o[:, :, a, 16 * a + 8:16 * a + 16],
                                                              T["pair_mask"][0:PAIR, 1:2], o_sel[:, :, a, :], ALU.mult, ALU.add)
                    last.then_inc(free, 1)
                    v.wait_ge(free, u + 1)
                    nc.vector.tensor_tensor(o_nat[:, 0:NJ, :], o_sel[:].rearrange("p g a d -> p (g a) d"),
                                            rden[:].unsqueeze(2).broadcast_to((PAIR, NJ, HD0)), ALU.mult).then_inc(o_ready, 1)

                def step(b, s):
                    for kind, what in order(b):
                        if kind == "fin":
                            if what == ("o_nat",):
                                finish(b - 1, 1 - s)
                        elif kind == "prepare":
                            prepare(b + 1, 1 - s, what)
                for n in names:
                    prepare(0, 0, n)
                batch_loop(v, chain, step)
                finish(B - 1, 1)

            @block.scalar
            def _(act):
                def prepare(b, s, name):
                    kind = name[0]
                    if kind not in ("ctxT", "k", "v"):
                        return
                    c = name[1]
                    bank, full, free, u = ring(name, b)
                    act.wait_ge(full, u + 1)
                    cols = slice(c * CH, (c + 1) * CH)
                    if kind == "ctxT":
                        nc.scalar.activation(ctxT[:, cols], ps[:, bank, 0:CH], ACT.Copy).then_inc(free, 1)
                    elif kind == "k":
                        if c == 0 and not (isinstance(b, int) and b == 0):
                            act.wait_ge(k_stacked[1 - s], STACK // 2 * (b - 2 + s) + STACK)
                        nc.scalar.activation(k_hi[:, cols], ps[:, bank, 0:CH], ACT.Copy)
                        nc.scalar.activation(k_bf[:, cols], ps[:, bank, 0:CH], ACT.Copy).then_inc(k_bf_ready, 1)
                    else:
                        nc.scalar.activation(
                            vals[s][c][:, :, :, 0:4 * HD0],
                            ps[0:KP, bank, 0:384].rearrange("p (t g w) -> p t g w", t=3, g=4),
                            ACT.Copy).then_inc(v_hi_ready if c == SPLIT else free, 1)

                def copy_out(b):
                    act.wait_ge(pv_done, KT * (b + 1))
                    nc.scalar.activation(o_T[:].rearrange("p (h c) -> p h c", h=2), ps[0:VPARTS, 4:6, 0:HALF],
                                         ACT.Copy).then_inc(o_free, 1)

                def finish(b):
                    bank, full, free, u = aux.fin(("oT",), b)
                    act.wait_ge(full, u + 1)
                    nc.scalar.activation(AT0[:, :, bass.ds(b * NQ, NQ)],
                                         ps[0:64, bank, 0:PAIR].rearrange("p (a q) -> p a q", a=2), ACT.Copy).then_inc(free, 1)

                def step(b, s):
                    for kind, what in order(b):
                        if kind == "scores":
                            t = what
                            scores = ps[0:KP, 2 * (t % 2):2 * (t % 2) + 2, 0:HALF]
                            at_least(act, pv_done, KT * b + t + 1 - PB)
                            act.wait_ge(s_full[t % 2], KT // 2 * b + t // 2 + 1)
                            if t % 4 == SPLIT:
                                nc.scalar.activation(P_hi[:].rearrange("p (a g) c -> p a (g c)", a=2), scores,
                                                     ACT.Exp, scale=SCALE)
                            nc.scalar.activation(P[t % PB][:].rearrange("p (a g) c -> p a (g c)", a=2), scores,
                                                 ACT.Exp, scale=SCALE).then_inc(exp_done[t % 2], 1)
                        elif kind == "copy":
                            copy_out(b - 1)
                        elif kind == "fin":
                            if what == ("oT",):
                                finish(b - 1)
                        elif kind == "prepare":
                            prepare(b + 1, 1 - s, what)
                for n in names:
                    prepare(0, 0, n)
                batch_loop(act, Chain(act, None), step)
                copy_out(B - 1)
                finish(B - 1)

            @block.tensor
            def _(pe):
                def prepare(b, s, name):
                    kind = name[0]
                    bank, full, free, u = ring(name, b)
                    at_least(pe, free, u)
                    if kind == "ctxT":
                        c = name[1]
                        if c == 0:
                            pe.wait_ge(ctx_in[s], 8 * (b - s) + 16)
                        for k in range(4):
                            last = nc.tensor.transpose(ps[:, bank, KP * k:KP * (k + 1)], ctx[s][:, 4 * c + k, :],
                                                       ident[0:KP, 0:KP])
                    elif kind == "k":
                        c = name[1]
                        _, _, free_t, ut = ring(("ctxT", c), b)
                        pe.wait_ge(free_t, ut + 1)
                        last = nc.tensor.matmul(ps[:, bank, 0:CH], T["wk0"][:], ctxT[:, c * CH:(c + 1) * CH],
                                                start=True, stop=True)
                    elif kind == "v":
                        c = name[1]
                        for k in range(3):
                            last = nc.tensor.matmul(ps[0:KP, bank, 128 * k:128 * (k + 1)],
                                                    ctxT[:, (c + 4 * k) * KP:(c + 4 * k + 1) * KP], T["wv0"][:],
                                                    start=True, stop=True)
                    elif kind == "max":
                        c, j = name[1:]
                        if j == 0:
                            pe.wait_ge(k_bf_ready, b * NC + c + 1)
                            pe.wait_ge(q_ready, b + 1)
                        last = nc.tensor.matmul(ps[:, bank, 0:CH], q_bf[:, 128 * j:128 * (j + 1)],
                                                k_bf[:, c * CH:(c + 1) * CH], start=True, stop=True)
                    else:
                        if name[1] == 0:
                            pe.wait_ge(negm_ready, b + 1)
                        for k, j in enumerate(row_tiles(name[1])):
                            last = nc.tensor.matmul(ps[96:97, bank, 128 * k:128 * (k + 1)], negm[:, j:j + 1],
                                                    ident_bf[:], start=True, stop=True)
                    last.then_inc(full, 1)

                def finish(b, name):
                    bank, full, free, u = aux.fin(name, b)
                    pe.wait_ge(free, u)
                    if name == ("o_nat",):
                        pe.wait_ge(o_free, b + 1)
                        for j in range(NJ):
                            last = nc.tensor.matmul(ps[0:PAIR, bank, VW * j:VW * (j + 1)], o_T[:, PAIR * j:PAIR * (j + 1)],
                                                    T["fold"][0:VPARTS], start=True, stop=True)
                    else:
                        pe.wait_ge(o_ready, b + 1)
                        last = nc.tensor.transpose(ps[:, bank, 0:PAIR], o_nat[:].rearrange("p j d -> p (j d)"),
                                                   ident[0:PAIR, 0:PAIR])
                    last.then_inc(full, 1)

                def weigh(b, s, t, h):
                    if t == 0 and h == 0:
                        at_least(pe, o_free, b)
                    split = t % 4 == SPLIT
                    if h == 0 and split:
                        pe.wait_ge(lo_ready, KT // 4 * b + t // 4 + 1)
                    elif h == 0:
                        pe.wait_ge(exp_done[t % 2], KT // 2 * b + t // 2 + 1)
                    for a in range(2):
                        g = 2 * h + a
                        for n, probs in enumerate((P_hi, P_lo) if split else (P[t % PB],)):
                            last = nc.tensor.matmul(ps[0:VPAD, 4 + h, GQ * a:GQ * (a + 1)], vals[s][t % 4][:, t // 4, g, :],
                                                    probs[:, g, :], start=(t == 0 and a == 0 and n == 0),
                                                    stop=(t == KT - 1 and (n == 1 or not split)), skip_group_check=True)
                    if h:
                        last.then_inc(pv_done, 1)

                def step(b, s):
                    for kind, what in order(b):
                        if kind == "scores":
                            t = what
                            if t == 0:
                                _, _, free, ur = ring(("row", 2), b)
                                pe.wait_ge(free, ur + 1)
                                pe.wait_ge(k_stacked[s], STACK // 2 * (b - s) + STACK)
                            at_least(pe, exp_done[t % 2], KT // 2 * b + t // 2)
                            for g in range(4):
                                last = nc.tensor.matmul(ps[0:KP, 2 * (t % 2) + g // 2, (g % 2) * GQ:(g % 2 + 1) * GQ],
                                                        k_parts[s][:, g, KP * t:KP * (t + 1)],
                                                        q_rows[s][:, g].rearrange("p h q -> p (h q)"), start=True, stop=True)
                            last.then_inc(s_full[t % 2], 1)
                        elif kind == "weigh":
                            weigh(b, s, *what)
                        elif kind == "late":
                            weigh(b - 1, 1 - s, *what)
                        elif kind == "fin":
                            finish(b - 1, what)
                        elif kind == "prepare":
                            prepare(b + 1, 1 - s, what)

                for n in names:
                    prepare(0, 0, n)
                pe.wait_ge(const_ready, 3)
                batch_loop(pe, Chain(pe, None), step)
                for t in range(KT - LAG, KT):
                    for h in range(2):
                        weigh(B - 1, 1, t, h)
                for n in fin:
                    finish(B - 1, n)


def phase_ffn0(nc, A, sem, sems, ps, T):
    ident, x_nat, h_nat, hT, AT0 = (T[k] for k in "ident x_nat h_nat hT AT0".split())
    EP = E0 // 2 + 1
    with ExitStack() as st:
        def sb(name, shape, dt=F32):
            return st.enter_context(nc.sbuf_tensor(name, shape, dt))
        wo, bo, rw, rb, w1, w3, w2 = T["f_weights"]
        act_sb = sb("f_act", [128, 2, HALF])
        H = sb("f_H", [128, EP, NTOK])
        lg = sb("f_lg", [128, TT, E0])
        top = sb("f_top", [128, TT, 8])
        idx = sb("f_idx", [128, TT, 8], U32)
        idxf = sb("f_idxf", [128, TT, 8])
        hit = sb("f_hit", [128, TT, 2, E0])
        gate = sb("f_gate", [128, TT, E0])
        gsum = sb("f_gsum", [128, TT])

        w_in, small_in, M_step = T["f_w_in"], T["f_small_in"], sem("f_M_step")
        var_ready, root_done, own = sem("f_var_ready"), sem("f_root_done"), sem("f_own")
        norm_ready, hT_ready, exp_ready, exp_done, act_ready, H_ready = (
            sem("f_" + n) for n in "norm_ready hT_ready exp_ready exp_done act_ready H_ready".split())
        full, free = sems("f_full", 8), sems("f_free", 8)
        names = [("o", t) for t in range(TT)] + [("T", h) for h in range(2)] + [("lg",)] \
            + [(w, e, h) for e in range(EP) for h in range(2) for w in "ab"] \
            + [("y", t, k) for first in range(0, TT, 2) for k in (2, 0, 1) for t in range(first, min(first + 2, TT))]
        ring = Ring(list(range(8)), names, full, free)

        with nc.Block() as block:
            @block.gpsimd
            def _(pool):
                chain = Chain(pool, M_step)
                wv, gb, M, ones = (T[k] for k in "wv gb M ones".split())
                chain.link(nc.gpsimd.memset(ones[:], 1.0))
                for i in range(2):
                    chain.link(nc.gpsimd.memset(wv[i][:, :, HD1:], 0.0))
                    chain.link(nc.gpsimd.memset(wv[i][0:1, :, HD1:], 1.0))
                pool.wait_ge(T["gb_in"], 64)
                for i in range(2):
                    chain.link(nc.gpsimd.tensor_scalar(M[i][:], ident, gb[:, 2 * i:2 * i + 1], None, ALU.mult))
                    chain.link(nc.gpsimd.tensor_scalar(M[i][0:1, 1:128], ones[:, 1:128], gb[0:1, 2 * i:2 * i + 1], -1.0,
                                                       ALU.mult, ALU.mult))
                    chain.link(nc.gpsimd.tensor_copy(M[i][:, 0:1], gb[:, 2 * i + 1:2 * i + 2]))

            @block.sync
            def _(sp):
                for k, n in enumerate(("ln_m_g", "ln_m_b", "ln_l_g", "ln_l_b")):
                    sp.dma_start(T["gb"][:, k:k + 1], A["L1_xattn_" + n].rearrange("(p a) -> p a", a=1)).then_inc(T["gb_in"], 16)
                sp.dma_start(T["wkv_raw"][:], A["L1_xattn_Wkv"]).then_inc(T["w_in"], 16)
                sp.dma_start(T["wq_raw"][:], A["L1_xattn_Wq"]).then_inc(T["w_in"], 16)

            @block.vector
            def _(v):
                chain = Chain(v, own)
                v.wait_ge(small_in, 16 * (2 * NJ + 3))
                for t in range(TT):
                    bank, fu, fr, u = ring(("o", t))
                    v.wait_ge(fu, u + 1)
                    last = nc.vector.tensor_tensor(x_nat[:, t, :], x_nat[:, t, :], ps[:, bank, 0:D], ALU.add)
                    last.then_inc(fr, 1)
                    v.wait_ge(fr, u + 1)
                    last = nc.vector.tensor_tensor(x_nat[:, t, :], x_nat[:, t, :], bo[:], ALU.add)
                chain.link(last)
                layer_norm(v, chain, var_ready, root_done, 1, x_nat, h_nat, T["stats"], T["mv"], T["rstd"])
                v.sem_inc(norm_ready, 1)
                for h in range(2):
                    bank, fu, fr, u = ring(("T", h))
                    v.wait_ge(fu, u + 1)
                    n = 128 * len(transposed_tiles(h))
                    nc.vector.tensor_copy(hT[:, 512 * h:512 * h + n], ps[:, bank, 0:n]).then_inc(fr, 1)
                bank, fu, fr, u = ring(("lg",))
                v.wait_ge(fu, u + 1)
                nc.vector.tensor_tensor(lg[:], ps[:, bank, 0:TT * E0].rearrange("p (t e) -> p t e", t=TT),
                                        rb[:].unsqueeze(1).broadcast_to((128, TT, E0)), ALU.add).then_inc(fr, 1)
                v.wait_ge(fr, u + 1)
                top2(nc, chain, T["iota8"], lg, top, idx, idxf, hit)
                chain.link(nc.vector.tensor_tensor(lg[:], lg[:], top[:, :, 0:1].broadcast_to((128, TT, E0)), ALU.subtract))
                v.sem_inc(exp_ready, 1)
                v.wait_ge(exp_done, 1)
                chain.link(nc.vector.tensor_tensor(gate[:], lg[:], hit[:, :, 0, :], ALU.mult))
                chain.link(nc.vector.tensor_reduce(gsum[:], gate[:], AX.X, ALU.add))
                chain.link(nc.vector.reciprocal(gsum[:], gsum[:]))
                chain.link(nc.vector.tensor_tensor(gate[:], gate[:], gsum[:].unsqueeze(2).broadcast_to((128, TT, E0)), ALU.mult))
                for e in range(EP):
                    for h in range(2):
                        bank, fu, fr, u = ring(("b", e, h))
                        v.wait_ge(act_ready, 2 * e + h + 1)
                        v.wait_ge(fu, u + 1)
                        nc.vector.tensor_tensor(H[:, e, h * HALF:(h + 1) * HALF], act_sb[:, h, :], ps[:, bank, 0:HALF],
                                                ALU.mult).then_inc(fr, 1)
                        v.wait_ge(fr, u + 1)
                        v.sem_inc(H_ready, 1)
                for first in range(0, TT, 2):
                    tiles = range(first, min(first + 2, TT))
                    for k in (2, 0, 1):
                        uses = [ring(("y", t, k)) for t in tiles]
                        for _, fu, _, u in uses:
                            v.wait_ge(fu, u + 1)
                        for e in range(4 if k < 2 else 1):
                            for t, (bank, _, fr, u) in zip(tiles, uses):
                                y = ps[:, bank, D * e:D * (e + 1)]
                                if k == 2:
                                    i = nc.vector.tensor_tensor(x_nat[:, t, :], x_nat[:, t, :], y, ALU.add)
                                else:
                                    i = nc.vector.scalar_tensor_tensor(x_nat[:, t, :], y, gate[:, t, 4 * k + e:4 * k + e + 1],
                                                                       x_nat[:, t, :], ALU.mult, ALU.add)
                                if e == 3 or k == 2:
                                    i.then_inc(fr, 1)
                            if e < 3 and k < 2:
                                chain.link(i)
                        for _, _, fr, u in uses:
                            v.wait_ge(fr, u + 1)

            @block.scalar
            def _(act):
                act.wait_ge(var_ready, 1)
                nc.scalar.activation(T["rstd"][:], T["rstd"][:], ACT.Sqrt).then_inc(root_done, 1)
                act.wait_ge(exp_ready, 1)
                nc.scalar.activation(lg[:], lg[:], ACT.Exp).then_inc(exp_done, 1)
                for e in range(EP):
                    for h in range(2):
                        bank, fu, fr, u = ring(("a", e, h))
                        act.wait_ge(fu, u + 1)
                        at_least(act, H_ready, 2 * e + h - 1)
                        nc.scalar.activation(act_sb[:, h, :], ps[:, bank, 0:HALF], ACT.Silu).then_inc(fr, 1)
                        act.wait_ge(fr, u + 1)
                        act.sem_inc(act_ready, 1)

            @block.tensor
            def _(pe):
                def claim(name):
                    bank, fu, fr, u = ring(name)
                    at_least(pe, fr, u)
                    return bank, fu
                pe.wait_ge(small_in, 16 * (2 * NJ + 3))
                for t in range(TT):
                    bank, fu = claim(("o", t))
                    for a in range(2):
                        last = nc.tensor.matmul(ps[:, bank, 0:D], AT0[:, a, 128 * t:128 * (t + 1)], wo[:, a, :],
                                                start=(a == 0), stop=(a == 1))
                    last.then_inc(fu, 1)
                pe.wait_ge(norm_ready, 1)
                for h in range(2):
                    bank, fu = claim(("T", h))
                    for k, t in enumerate(transposed_tiles(h)):
                        last = nc.tensor.transpose(ps[:, bank, 128 * k:128 * (k + 1)], h_nat[:, t, :], ident)
                    last.then_inc(fu, 1)
                for h in range(2):
                    _, _, fr, u = ring(("T", h))
                    pe.wait_ge(fr, u + 1)
                bank, fu = claim(("lg",))
                for t in range(TT):
                    last = nc.tensor.matmul(ps[:, bank, E0 * t:E0 * (t + 1)], hT[:, 128 * t:128 * (t + 1)], rw[:],
                                            start=True, stop=True)
                last.then_inc(fu, 1)
                pe.wait_ge(w_in, 16 * 7)
                for e in range(EP):
                    for h in range(2):
                        for w, wt in (("a", w1), ("b", w3)):
                            bank, fu = claim((w, e, h))
                            nc.tensor.matmul(ps[:, bank, 0:HALF], wt[:, 2 * e:2 * e + 2, :].rearrange("p e h -> p (e h)"),
                                             hT[:, h * HALF:(h + 1) * HALF], start=True, stop=True).then_inc(fu, 1)
                pe.wait_ge(H_ready, 2 * EP)
                for _, t, k in [n for n in names if n[0] == "y"]:
                    tok = slice(128 * t, 128 * (t + 1))
                    bank, fu = claim(("y", t, k))
                    if k < 2:
                        for e in range(2):
                            last = nc.tensor.matmul(ps[:, bank, 2 * D * e:2 * D * (e + 1)], H[:, 2 * k + e, tok],
                                                    w2[:, 2 * k + e, :, :].rearrange("p a d -> p (a d)"),
                                                    start=True, stop=True)
                    else:
                        last = nc.tensor.matmul(ps[:, bank, 0:D], H[:, EP - 1, tok], w2[:, EP - 1, 0, :],
                                                start=True, stop=True)
                    last.then_inc(fu, 1)


def phase_weights1(nc, A, sem, sems, ps, T):
    ident, x_nat, h_nat, ctx_mv, lT = (T[k] for k in "ident x_nat h_nat ctx_mv hT".split())
    wkT, wv, wq, wq_raw, wkv_raw, M = (T[k] for k in "wkT wv wq wq_raw wkv_raw M".split())
    ctx_r = ctx_mv[:, :, 1]
    w_in, own = T["w_in"], sem("w_own")
    var_ready, root_done, l_ready = (sem("w_" + n) for n in "var_ready root_done l_ready".split())
    full, free = sems("w_full", 8), sems("w_free", 8)
    names = [("wkT", i, h) for i in range(2) for h in range(2)] + [("wv", i, h) for i in range(2) for h in range(2)] \
        + [("wq", h) for h in range(2)] + [("T", h) for h in range(2)]
    ring = Ring(list(range(8)), names, full, free)
    with nc.Block() as block:
        @block.vector
        def _(v):
            chain = Chain(v, own)
            chain.link(nc.vector.tensor_scalar(ctx_r, ctx_mv[:, :, 1], LN_EPS, None, ALU.add))
            layer_norm(v, chain, var_ready, root_done, 1, x_nat, h_nat, T["stats"], T["mv"], T["rstd"])
            layer_norm(v, chain, var_ready, root_done, 2, h_nat, h_nat, T["stats"], T["mv"], T["rstd"])
            nc.vector.memset(h_nat[:, :, 0:1], 1.0).then_inc(l_ready, 1)
            v.wait_ge(root_done, 3)
            nc.vector.reciprocal(ctx_r, ctx_r)
            for h in range(2):
                bank, fu, fr, u = ring(("T", h))
                v.wait_ge(fu, u + 1)
                n = 128 * len(transposed_tiles(h))
                nc.vector.tensor_copy(lT[:, 512 * h:512 * h + n], ps[:, bank, 0:n]).then_inc(fr, 1)

        @block.scalar
        def _(act):
            for r in range(2):
                act.wait_ge(var_ready, r + 1)
                nc.scalar.activation(T["rstd"][:], T["rstd"][:], ACT.Sqrt).then_inc(root_done, 1)
            nc.scalar.activation(ctx_r, ctx_r, ACT.Sqrt).then_inc(root_done, 1)
            for name in names:
                bank, fu, fr, u = ring(name)
                if name[0] == "T":
                    continue
                act.wait_ge(fu, u + 1)
                h = name[-1]
                if name[0] == "wkT":
                    dst = wkT[name[1]][:, 4 * h:4 * h + 4, :].rearrange("p j f -> p (j f)")
                    src = ps[:, bank, :]
                elif name[0] == "wv":
                    dst = wv[name[1]][:, 8 * h:8 * h + 8, 0:HD1]
                    src = ps[:, bank, :].rearrange("p (j d) -> p j d", j=8)
                else:
                    dst, src = wq[:, 512 * h:512 * (h + 1)], ps[:, bank, :]
                nc.scalar.activation(dst, src, ACT.Copy).then_inc(fr, 1)

        @block.tensor
        def _(pe):
            pe.wait_ge(w_in, 32)
            for name in names:
                bank, fu, fr, u = ring(name)
                at_least(pe, fr, u)
                h = name[-1]
                if name[0] == "wkT":
                    for k in range(4):
                        j = 4 * h + k
                        last = nc.tensor.matmul(ps[:, bank, 128 * k:128 * (k + 1)],
                                                wkv_raw[:, 128 * j:128 * (j + 1)], M[name[1]][:], start=True, stop=True)
                elif name[0] == "wv":
                    last = nc.tensor.matmul(ps[:, bank, :], M[name[1]][:],
                                            wkv_raw[:, INNER + 512 * h:INNER + 512 * (h + 1)], start=True, stop=True)
                elif name[0] == "wq":
                    last = nc.tensor.matmul(ps[:, bank, :], M[1][:], wq_raw[:, 512 * h:512 * (h + 1)],
                                            start=True, stop=True)
                else:
                    if h == 0:
                        pe.wait_ge(l_ready, 1)
                    for k, t in enumerate(transposed_tiles(h)):
                        last = nc.tensor.transpose(ps[:, bank, 128 * k:128 * (k + 1)], h_nat[:, t, :], ident)
                last.then_inc(fu, 1)


def phase_attention1(nc, A, sem, sems, ps, T, ctx_rows):
    ident, ident_bf, x_nat, h_nat, ctx_mv, AT1 = (T[k] for k in "ident ident_bf x_nat h_nat ctx_mv AT1".split())
    SCALE = float(HD1) ** -0.5
    NT = KT + 1
    with ExitStack() as st:
        def sb(name, shape, dt=F32, stack=st):
            return stack.enter_context(nc.sbuf_tensor(name, shape, dt))
        wkT, wv, wq = T["wkT"], T["wv"], T["wq"]
        lT = T["hT"]
        ctx = sb("b_ctx", [KP, KT, D])
        c_mv = sb("b_c_mv", [KP, KT, 2])
        y = sb("b_y", [KP, KT, D])
        y_hi = [sb(f"b_y_hi{s}", [KP, KT, D], F32R) for s in range(2)]
        y_lo = [sb(f"b_y_lo{s}", [KP, KT, D], F32R) for s in range(2)]
        yT_hi = [sb(f"b_yT_hi{s}", [128, NCTX], F32R) for s in range(2)]
        yT_lo = [sb(f"b_yT_lo{s}", [128, NCTX], F32R) for s in range(2)]
        yT_bf = sb("b_yT_bf", [128, NCTX], BF16)
        l_f = sb("b_l_f", [128, NQ])
        l_hi = [sb(f"b_l_hi{s}", [128, 128], F32R) for s in range(2)]
        l_lo = [sb(f"b_l_lo{s}", [128, 128], F32R) for s in range(2)]
        l_bf = sb("b_l_bf", [128, NQ], BF16)
        l_nat = [sb(f"b_l_nat{s}", [128, D]) for s in range(2)]
        q_bd = h_nat[:].rearrange("p t d -> p (t d)").rearrange("p (j a q) -> p j a q", j=NJ, a=2)
        Q_f = [sb(f"b_Q_f{i}", [128, HQ]) for i in range(2)]
        Q_bf = [sb(f"b_Q_bf{i}", [128, HQ], BF16) for i in range(2)]
        Q_hi = [[sb(f"b_Q_hi{s}{i}", [128, HQ], F32R) for i in range(2)] for s in range(2)]
        Q_lo = [[sb(f"b_Q_lo{s}{i}", [128, HQ], F32R) for i in range(2)] for s in range(2)]
        mx = sb("b_mx", [128, NC + 1, MT])
        negm = sb("b_negm", [128, MT], BF16)
        P_hi = [sb(f"b_P_hi{k}", [KP, 2, HALF], F32R) for k in range(PB)]
        P_lo = [sb(f"b_P_lo{k}", [KP, 2, HALF], F32R) for k in range(PB)]
        P_l = sb("b_P_l", [128, 2, HALF])
        U = [sb(f"b_U{i}", [128, HEADS, NQ]) for i in range(2)]
        rden = sb("b_rden", [NQ, HEADS])
        o_nat = sb("b_o_nat", [NQ, HEADS, HD1])

        ctx_in = sem("b_ctx_in")
        aux_full, aux_free = sems("b_aux_full", 2), sems("b_aux_free", 2)
        s_full, exp_done = sems("b_s_full", 2), sems("b_exp_done", 2)
        (zero_ready, lo_ready, pv_done, y_ready, parts_ready, hi_ready, l_ready, Q_bf_ready, mx_ready, Q_ready, u_free,
         own_v, own_p, pool_turn, pe_turn) = (sem("b_" + n) for n in (
            "zero_ready lo_ready pv_done y_ready parts_ready hi_ready l_ready Q_bf_ready mx_ready Q_ready u_free "
            "own_v own_p pool_turn pe_turn").split())

        prep = [("l_nat",), ("q",), ("T", 0), ("Q", 0, 0), ("T", 1), ("Q", 0, 1), ("T", 2), ("Q", 1, 0), ("Q", 1, 1)] \
            + [("max", c, j) for c in range(NC) for j in range(MT)] + [("max_l",)] + [("row", k) for k in range(3)]
        fin = [("Ul", h) for h in range(2)] + [("out", k) for k in range(4)] + [("oT", h) for h in range(2)]
        ring = TwoStageRing([6, 7], prep, fin, aux_full, aux_free)
        aux_prep, aux_fin = ring.prep, ring.fin

        def order(b):
            first, last = isinstance(b, int) and b == 0, isinstance(b, int) and b == B - 1
            groups = []
            for t in range(NT):
                groups.append([("scores", t)])
                if t >= LAG:
                    groups += [[("weigh", (t - LAG, h))] for h in range(2)]
                elif t + NT - LAG < KT and not first:
                    groups += [[("late", (t + NT - LAG, h))] for h in range(2)]
                if t < KT:
                    groups[-1].append(("part", t))
                if t == LAG - 2 and not first:
                    groups.append([("copy", None)] + [("fin", n) for n in fin if n[0] == "Ul"])
            rest = [] if first else [("fin", n) for n in fin if n[0] != "Ul"]
            rest += [] if last else [("prepare", n) for n in prep]
            return sum(groups[:5], []) + spread(groups[5:-5], rest, weight) + sum(groups[-5:], [])

        def s_use(b, t):
            return t % 2, b * (NT // 2 + 1 if t % 2 == 0 else NT // 2) + t // 2

        with nc.Block() as block:
            @block.sync
            def _(sp):
                sp.dma_start(ctx[:], ctx_rows[0]).then_inc(ctx_in, 16)
                with sp.Fori(1, B) as b:
                    sp.wait_ge(y_ready, b)
                    sp.dma_start(ctx[:], ctx_rows[b]).then_inc(ctx_in, 16)

            @block.gpsimd
            def _(pool):
                def step(b, s):
                    if not (isinstance(b, int) and b == 0):
                        _, _, fr, u = aux_prep(("T", NC - 1), b - 1)
                        pool.wait_ge(fr, u + 1)
                        pool.sem_inc(pool_turn, 1)
                    nc.gpsimd.tensor_copy(c_mv[:], ctx_mv[:, bass.ds(b * KT, KT), :]).then_inc(own_p, 1)
                    pool.wait_ge(own_p, 3 * b + 1)
                    pool.sem_inc(pool_turn, 1)
                    pool.wait_ge(ctx_in, 16 * b + 16)
                    pool.sem_inc(pool_turn, 1)
                    if not (isinstance(b, int) and b == 0):
                        pool.wait_ge(parts_ready, b)
                        pool.sem_inc(pool_turn, 1)
                    for t in range(KT):
                        last = nc.gpsimd.tensor_scalar(y[:, t, :], ctx[:, t, :], c_mv[:, t, 0:1], c_mv[:, t, 1:2],
                                                       ALU.subtract, ALU.mult)
                    last.then_inc(own_p, 1)
                    pool.wait_ge(own_p, 3 * b + 2)
                    pool.sem_inc(pool_turn, 1)
                    nc.gpsimd.memset(y[:, :, 0:1], 1.0).then_inc(y_ready, 1)
                    pool.wait_ge(y_ready, b + 1)
                    pool.sem_inc(pool_turn, 1)
                    if not (isinstance(b, int) and b < 2):
                        pool.wait_ge(pv_done, KT * (b - 1))
                        pool.sem_inc(pool_turn, 1)
                    nc.gpsimd.tensor_copy(y_hi[s][:], y[:]).then_inc(own_p, 1)
                    pool.wait_ge(own_p, 3 * b + 3)
                    pool.sem_inc(pool_turn, 1)
                    nc.gpsimd.tensor_tensor(y_lo[s][:], y[:], y_hi[s][:].bitcast(F32), ALU.subtract).then_inc(parts_ready, 1)
                step(0, 0)
                step(1, 1)
                with pool.Fori(1, B // 2) as i:
                    step(2 * i, 0)
                    step(2 * i + 1, 1)

            @block.vector
            def _(v):
                chain = Chain(v, own_v)

                def prepare(b, s, name):
                    kind = name[0]
                    bank, fu, fr, u = aux_prep(name, b)
                    if kind == "l_nat":
                        at_least(v, pv_done, KT * (b - 1))
                        chain.link(nc.vector.tensor_copy(l_f[:], lT[:, bass.ds(b * NQ, NQ)]))
                        nc.vector.tensor_copy(l_bf[:], l_f[:])
                        chain.link(nc.vector.tensor_copy(l_hi[s][:, 0:NQ], l_f[:]))
                        nc.vector.tensor_tensor(l_lo[s][:, 0:NQ], l_f[:], l_hi[s][:, 0:NQ].bitcast(F32),
                                                ALU.subtract).then_inc(l_ready, 1)
                    elif kind == "q":
                        v.wait_ge(fu, u + 1)
                        for a in range(2):
                            rows = slice(64 * a, 64 * a + 64)
                            last = nc.vector.tensor_copy(q_bd[rows, :, a, :],
                                                         ps[rows, bank, 0:HALF].rearrange("p (j q) -> p j q", j=NJ))
                        last.then_inc(fr, 1)
                    elif kind == "Q":
                        i, a = name[1:]
                        v.wait_ge(fu, u + 1)
                        nc.vector.tensor_copy(Q_f[i][:, HALF * a:HALF * (a + 1)], ps[:, bank, 0:HALF]).then_inc(fr, 1)
                        if a:
                            v.wait_ge(fr, u + 1)
                            nc.vector.tensor_copy(Q_bf[i][:], Q_f[i][:]).then_inc(Q_bf_ready, 1)
                    elif kind == "T":
                        c = name[1]
                        v.wait_ge(hi_ready, b * NC + c + 1)
                        nc.vector.tensor_tensor(yT_lo[s][:, c * CH:(c + 1) * CH], ps[:, bank, 0:CH],
                                                yT_hi[s][:, c * CH:(c + 1) * CH].bitcast(F32), ALU.subtract).then_inc(fr, 1)
                    elif kind == "max":
                        c, j = name[1:]
                        v.wait_ge(fu, u + 1)
                        nc.vector.tensor_reduce(mx[:, c, j:j + 1], ps[:, bank, 0:CH], AX.X, ALU.max).then_inc(fr, 1)
                    elif kind == "max_l":
                        v.wait_ge(fu, u + 1)
                        nc.vector.tensor_reduce(mx[:, NC, :], ps[:, bank, 0:MT * NQ].rearrange("p (j k) -> p j k", j=MT), AX.X,
                                                ALU.max).then_inc(fr, 1)
                        v.wait_ge(fr, u + 1)
                        nc.vector.tensor_reduce(negm[:], mx[:].rearrange("p c j -> p j c"), AX.X, ALU.max,
                                                negate=True).then_inc(mx_ready, 1)
                    else:
                        v.wait_ge(fu, u + 1)
                        cols = row_columns(name[1])
                        for i in range(2):
                            row = Q_f[i][0:1, cols]
                            last = nc.vector.tensor_tensor(row, row, ps[0:1, bank, 0:cols.stop - cols.start], ALU.add)
                        last.then_inc(fr, 1)
                        v.wait_ge(fr, u + 1)
                        for i in range(2):
                            last = nc.vector.tensor_copy(Q_hi[s][i][:, cols], Q_f[i][:, cols])
                        chain.link(last)
                        for i in range(2):
                            last = nc.vector.tensor_tensor(Q_lo[s][i][:, cols], Q_f[i][:, cols],
                                                           Q_hi[s][i][:, cols].bitcast(F32), ALU.subtract)
                        last.then_inc(Q_ready, 1)

                def finish(b, name):
                    kind, k = name
                    if kind != "out":
                        return
                    bank, fu, fr, u = aux_fin(name, b)
                    v.wait_ge(fu, u + 1)
                    o = ps[0:NQ, bank, 0:4 * (HD1 + 1)].rearrange("p (h w) -> p h w", h=4)
                    chain.link(nc.vector.reciprocal(rden[:, 4 * k:4 * k + 4], o[:, :, HD1]))
                    nc.vector.tensor_tensor(o_nat[:, 4 * k:4 * k + 4, :], o[:, :, 0:HD1],
                                            rden[:, 4 * k:4 * k + 4].unsqueeze(2).broadcast_to((NQ, 4, HD1)),
                                            ALU.mult).then_inc(fr, 1)

                def step(b, s):
                    for kind, what in order(b):
                        if kind == "part":
                            k, u = s_use(b, what)
                            v.wait_ge(exp_done[k], u + 1)
                            nc.vector.tensor_tensor(P_lo[what % PB][:], ps[0:KP, 2 * k:2 * k + 2, 0:HALF],
                                                    P_hi[what % PB][:].bitcast(F32), ALU.subtract).then_inc(lo_ready, 1)
                        elif kind == "fin":
                            finish(b - 1, what)
                        elif kind == "prepare":
                            prepare(b + 1, 1 - s, what)
                for buf in l_hi + l_lo:
                    nc.vector.memset(buf[:, NQ:].bitcast(F32), 0.0)
                for buf in l_nat + [P_l]:
                    nc.vector.memset(buf[:], 0.0)
                last = nc.vector.memset(q_bd, 0.0)
                chain.link(last)
                v.sem_inc(zero_ready, 1)
                for n in prep:
                    prepare(0, 0, n)
                batch_loop(v, chain, step)
                for n in fin:
                    finish(B - 1, n)

            @block.scalar
            def _(act):
                def prepare(b, s, name):
                    kind = name[0]
                    if kind not in ("T", "l_nat"):
                        return
                    bank, fu, fr, u = aux_prep(name, b)
                    act.wait_ge(fu, u + 1)
                    if kind == "T":
                        c = name[1]
                        cols = slice(c * CH, (c + 1) * CH)
                        if c == 0:
                            at_least(act, mx_ready, b)
                        nc.scalar.activation(yT_hi[s][:, cols], ps[:, bank, 0:CH], ACT.Copy)
                        nc.scalar.activation(yT_bf[:, cols], ps[:, bank, 0:CH], ACT.Copy).then_inc(hi_ready, 1)
                    else:
                        nc.scalar.activation(l_nat[s][0:NQ], ps[0:NQ, bank, 0:D], ACT.Copy).then_inc(fr, 1)

                def copy_out(b):
                    act.wait_ge(pv_done, KT * (b + 1))
                    nc.scalar.activation(U[0][:].rearrange("p (a h) q -> p a (h q)", a=2), ps[:, 4:6, 0:HALF],
                                         ACT.Copy).then_inc(u_free, 1)

                def finish(b, name):
                    kind, k = name
                    if kind == "out":
                        return
                    bank, fu, fr, u = aux_fin(name, b)
                    act.wait_ge(fu, u + 1)
                    if kind == "Ul":
                        nc.scalar.activation(U[1][:, 8 * k:8 * k + 8, :].rearrange("p h q -> p (h q)"), ps[:, bank, 0:HALF],
                                             ACT.Copy).then_inc(fr, 1)
                    else:
                        nc.scalar.activation(AT1[:, 4 * k:4 * k + 4, bass.ds(b * NQ, NQ)],
                                             ps[:, bank, 0:4 * NQ].rearrange("p (j q) -> p j q", j=4), ACT.Copy).then_inc(fr, 1)

                def step(b, s):
                    for kind, what in order(b):
                        if kind == "scores":
                            t = what
                            k, u = s_use(b, t)
                            act.wait_ge(s_full[k], u + 1)
                            if t == KT:
                                nc.scalar.activation(P_l[0:NQ], ps[0:NQ, 2 * k:2 * k + 2, 0:HALF], ACT.Exp,
                                                     scale=SCALE).then_inc(exp_done[k], 1)
                                continue
                            at_least(act, pv_done, KT * b + t + 1 - PB)
                            nc.scalar.activation(P_hi[t % PB][:], ps[0:KP, 2 * k:2 * k + 2, 0:HALF], ACT.Exp, scale=SCALE)
                            nc.scalar.activation(ps[0:KP, 2 * k:2 * k + 2, 0:HALF], ps[0:KP, 2 * k:2 * k + 2, 0:HALF], ACT.Exp,
                                                 scale=SCALE).then_inc(exp_done[k], 1)
                        elif kind == "copy":
                            copy_out(b - 1)
                        elif kind == "fin":
                            finish(b - 1, what)
                        elif kind == "prepare":
                            prepare(b + 1, 1 - s, what)
                act.wait_ge(zero_ready, 1)
                for n in prep:
                    prepare(0, 0, n)
                batch_loop(act, Chain(act, None), step)
                copy_out(B - 1)
                for n in fin:
                    finish(B - 1, n)

            @block.tensor
            def _(pe):
                def prepare(b, s, name):
                    kind = name[0]
                    bank, fu, fr, u = aux_prep(name, b)
                    at_least(pe, fr, u)
                    if kind == "l_nat":
                        pe.wait_ge(l_ready, b + 1)
                        pe.sem_inc(pe_turn, 1)
                        last = nc.tensor.transpose(ps[0:NQ, bank, 0:D], l_f[:], ident)
                    elif kind == "q":
                        for j in range(NJ):
                            last = nc.tensor.matmul(ps[:, bank, NQ * j:NQ * (j + 1)], wq[:, 128 * j:128 * (j + 1)], l_f[:],
                                                    start=True, stop=True)
                    elif kind == "Q":
                        i, a = name[1:]
                        if (i, a) == (0, 0):
                            _, _, fq, uq = aux_prep(("q",), b)
                            pe.wait_ge(fq, uq + 1)
                        for k in range(4):
                            j = 4 * a + k
                            last = nc.tensor.matmul(ps[:, bank, PAIR * k:PAIR * (k + 1)], wkT[i][:, j, :],
                                                    q_bd[:, j].rearrange("p a q -> p (a q)"), start=True, stop=True)
                    elif kind == "T":
                        c = name[1]
                        if c == 0:
                            pe.wait_ge(y_ready, b + 1)
                        for k in range(4):
                            last = nc.tensor.transpose(ps[:, bank, KP * k:KP * (k + 1)], y[:, 4 * c + k, :],
                                                       ident[0:KP, 0:KP])
                    elif kind == "max":
                        c, j = name[1:]
                        if j == 0:
                            pe.wait_ge(hi_ready, b * NC + c + 1)
                            pe.wait_ge(Q_bf_ready, 2 * b + 2)
                        last = nc.tensor.matmul(ps[:, bank, 0:CH], Q_bf[0][:, 128 * j:128 * (j + 1)],
                                                yT_bf[:, c * CH:(c + 1) * CH], start=True, stop=True)
                    elif kind == "max_l":
                        for j in range(MT):
                            last = nc.tensor.matmul(ps[:, bank, NQ * j:NQ * (j + 1)], Q_bf[1][:, 128 * j:128 * (j + 1)],
                                                    l_bf[:], start=True, stop=True)
                    else:
                        if name[1] == 0:
                            pe.wait_ge(mx_ready, b + 1)
                        for k, j in enumerate(row_tiles(name[1])):
                            last = nc.tensor.matmul(ps[0:1, bank, 128 * k:128 * (k + 1)], negm[:, j:j + 1],
                                                    ident_bf[:], start=True, stop=True)
                    last.then_inc(fu, 1)

                def finish(b, s, name):
                    kind, k = name
                    bank, fu, fr, u = aux_fin(name, b)
                    at_least(pe, fr, u)
                    if kind == "Ul":
                        kk, us = s_use(b, KT)
                        if k == 0:
                            pe.wait_ge(exp_done[kk], us + 1)
                        last = nc.tensor.matmul(ps[:, bank, 0:HALF], l_nat[s][:], P_l[:, k, :], start=True, stop=True)
                    elif kind == "out":
                        if k == 0:
                            pe.wait_ge(u_free, b + 1)
                            for h in range(2):
                                _, _, fl, ul = aux_fin(("Ul", h), b)
                                pe.wait_ge(fl, ul + 1)
                        pe.sem_inc(pe_turn, 1)
                        for n in range(4):
                            h = 4 * k + n
                            o = ps[0:NQ, bank, (HD1 + 1) * n:(HD1 + 1) * (n + 1)]
                            nc.tensor.matmul(o, U[0][:, h, :], wv[0][:, h, :], start=True, stop=False)
                            last = nc.tensor.matmul(o, U[1][:, h, :], wv[1][:, h, :], start=False, stop=True)
                    else:
                        if k == 0:
                            for m in (2, 3):
                                _, _, fo, uo = aux_fin(("out", m), b)
                                pe.wait_ge(fo, uo + 1)
                        pe.sem_inc(pe_turn, 1)
                        for n in range(4):
                            j = 4 * k + n
                            last = nc.tensor.transpose(ps[:, bank, NQ * n:NQ * (n + 1)],
                                                       o_nat[:, 2 * j:2 * j + 2, :].rearrange("p h d -> p (h d)"),
                                                       ident[0:NQ, 0:NQ])
                    last.then_inc(fu, 1)

                def weigh(b, s, t, h):
                    if t == 0 and h == 0:
                        at_least(pe, u_free, b)
                        pe.wait_ge(parts_ready, b + 1)
                    if h == 0:
                        pe.wait_ge(lo_ready, KT * b + t + 1)
                    o = ps[:, 4 + h, 0:HALF]
                    nc.tensor.matmul(o, y_hi[s][:, t, :], P_hi[t % PB][:, h, :], start=(t == 0), stop=False)
                    nc.tensor.matmul(o, y_hi[s][:, t, :], P_lo[t % PB][:, h, :], start=False, stop=False)
                    last = nc.tensor.matmul(o, y_lo[s][:, t, :], P_hi[t % PB][:, h, :], start=False, stop=(t == KT - 1))
                    if h:
                        last.then_inc(pv_done, 1)

                def step(b, s):
                    for kind, what in order(b):
                        if kind == "scores":
                            t = what
                            k, u = s_use(b, t)
                            if t == 0:
                                pe.wait_ge(Q_ready, 3 * (b + 1))
                            if t == 0:
                                at_least(pe, exp_done[k], u)
                            else:
                                at_least(pe, lo_ready, KT * b + t - 1)
                            i = int(t == KT)
                            if i:
                                hi, lo, rows = l_hi[s][:], l_lo[s][:], 128
                            else:
                                hi, lo, rows = yT_hi[s][:, KP * t:KP * (t + 1)], yT_lo[s][:, KP * t:KP * (t + 1)], KP
                            for h in range(2):
                                o = ps[0:rows, 2 * k + h, 0:HALF]
                                cols = slice(HALF * h, HALF * (h + 1))
                                nc.tensor.matmul(o, hi, Q_hi[s][i][:, cols], start=True, stop=False)
                                nc.tensor.matmul(o, hi, Q_lo[s][i][:, cols], start=False, stop=False)
                                last = nc.tensor.matmul(o, lo, Q_hi[s][i][:, cols], start=False, stop=True)
                            last.then_inc(s_full[k], 1)
                        elif kind == "weigh":
                            weigh(b, s, *what)
                        elif kind == "late":
                            weigh(b - 1, 1 - s, *what)
                        elif kind == "fin":
                            finish(b - 1, 1 - s, what)
                        elif kind == "prepare":
                            prepare(b + 1, 1 - s, what)

                for n in prep:
                    prepare(0, 0, n)
                batch_loop(pe, Chain(pe, None), step)
                for t in range(NT - LAG, KT):
                    for h in range(2):
                        weigh(B - 1, 1, t, h)
                for n in fin:
                    finish(B - 1, 1, n)


def top2(nc, chain, iota8, lg, top, idx, idxf, hit):
    for t in range(TT):
        last = nc.vector.max(top[:, t, :], lg[:, t, :])
    chain.link(last)
    for t in range(TT):
        last = nc.vector.max_index(idx[:, t, :], top[:, t, :], lg[:, t, :])
    chain.link(last)
    chain.link(nc.vector.tensor_copy(idxf[:], idx[:]))
    for k in range(2):
        last = nc.vector.tensor_tensor(hit[:, :, k, :], idxf[:, :, k:k + 1].broadcast_to((128, TT, 8)),
                                       iota8.unsqueeze(1).broadcast_to((128, TT, 8)), ALU.is_equal)
    chain.link(last)
    chain.link(nc.vector.tensor_tensor(hit[:, :, 0, :], hit[:, :, 0, :], hit[:, :, 1, :], ALU.add))


def phase_ffn1(nc, A, sem, sems, ps, T, out_tok):
    ident, x_nat, h_nat, hT, AT1 = (T[k] for k in "ident x_nat h_nat hT AT1".split())
    KI = I1 // 128
    with ExitStack() as st:
        def sb(name, shape, dt=F32):
            return st.enter_context(nc.sbuf_tensor(name, shape, dt))
        wout = sb("g_wout", [128, NJ, D])
        gw = sb("g_gw", [E1, D])
        gwT = sb("g_gwT", [128, E1])
        eb = sb("g_eb", [128, E1])
        up = sb("g_up", [128, E1, KI, D])
        down = sb("g_down", [128, E1, I1])
        upT = [sb(f"g_upT{k}", [128, I1]) for k in range(2)]
        downT = [sb(f"g_downT{k}", [128, I1]) for k in range(3)]
        H = [sb(f"g_H{k}", [128, KI, NTOK]) for k in range(2)]
        acc = sb("g_acc", [128, TT, D])
        lg = sb("g_lg", [128, TT, E1])
        top = sb("g_top", [128, TT, 8])
        idx = sb("g_idx", [128, TT, 8], U32)
        idxf = sb("g_idxf", [128, TT, 8])
        hit = sb("g_hit", [128, TT, 2, E1])
        gate = sb("g_gate", [128, TT, E1])
        gsum = sb("g_gsum", [128, TT])

        w_in, small_in, out_done = sem("g_w_in"), sem("g_small_in"), sem("g_out_done")
        var_ready, root_done, own, norm_ready, exp_ready, exp_done, result_ready = (
            sem("g_" + n) for n in "var_ready root_done own norm_ready exp_ready exp_done result_ready".split())
        full, free = sems("g_full", 8), sems("g_free", 8)
        names = [("gT",)] + [("o", t) for t in range(TT)] + [("T", h) for h in range(2)] + [("lg",)]
        names += [("upT", 0), ("downT", 0)]
        for e in range(E1 + 1):
            if e + 1 < E1:
                names += [("upT", e + 1), ("downT", e + 1)]
            if e < E1:
                names += [("h", e, k, h) for k in range(KI) for h in range(2)]
            if e:
                names += [("y", e - 1, h) for h in range(2)]
        ring = Ring(list(range(8)), names, full, free)

        with nc.Block() as block:
            @block.sync
            def _(sp):
                sp.dma_start(gw[:], A["L1_ffn_gate_w"]).then_inc(small_in, 16)
                sp.dma_start(eb[:], A["L1_ffn_expert_bias"].rearrange("(a n) -> a n", a=1).broadcast_to((128, E1))).then_inc(small_in, 16)
                sp.dma_start(wout[:], A["L1_xattn_Wout"].rearrange("(j p) n -> p j n", p=128)).then_inc(small_in, 16)
                sp.dma_start(up[:], A["L1_ffn_w_up"].rearrange("e (k p) d -> p e k d", p=128)).then_inc(w_in, 16)
                sp.dma_start(down[:], A["L1_ffn_w_down"].rearrange("e p i -> p e i")).then_inc(w_in, 16)
                sp.wait_ge(result_ready, 1)
                sp.dma_start(out_tok, acc[:]).then_inc(out_done, 16)
                sp.wait_ge(out_done, 16)

            @block.vector
            def _(v):
                chain = Chain(v, own)

                def take(name):
                    bank, fu, fr, u = ring(name)
                    v.wait_ge(fu, u + 1)
                    return bank, fr, u
                bank, fr, u = take(("gT",))
                nc.vector.tensor_copy(gwT[:], ps[:, bank, 0:E1]).then_inc(fr, 1)
                for t in range(TT):
                    bank, fr, u = take(("o", t))
                    nc.vector.tensor_tensor(x_nat[:, t, :], x_nat[:, t, :], ps[:, bank, 0:D], ALU.add).then_inc(fr, 1)
                v.wait_ge(fr, u + 1)
                layer_norm(v, chain, var_ready, root_done, 1, x_nat, h_nat, T["stats"], T["mv"], T["rstd"])
                v.sem_inc(norm_ready, 1)
                for h in range(2):
                    bank, fr, u = take(("T", h))
                    n = 128 * len(transposed_tiles(h))
                    nc.vector.tensor_copy(hT[:, 512 * h:512 * h + n], ps[:, bank, 0:n]).then_inc(fr, 1)
                bank, fr, u = take(("lg",))
                v.wait_ge(small_in, 48)
                nc.vector.tensor_tensor(lg[:], ps[:, bank, 0:TT * E1].rearrange("p (t e) -> p t e", t=TT),
                                        eb[:].unsqueeze(1).broadcast_to((128, TT, E1)), ALU.add).then_inc(fr, 1)
                v.wait_ge(fr, u + 1)
                top2(nc, chain, T["iota8"], lg, top, idx, idxf, hit)
                chain.link(nc.vector.tensor_tensor(lg[:], lg[:], top[:, :, 0:1].broadcast_to((128, TT, E1)), ALU.subtract))
                v.sem_inc(exp_ready, 1)
                v.wait_ge(exp_done, 1)

                def divide(a, s):
                    chain.link(nc.vector.reciprocal(s, s))
                    chain.link(nc.vector.tensor_tensor(a, a, s.unsqueeze(2).broadcast_to((128, TT, E1)), ALU.mult))
                chain.link(nc.vector.tensor_reduce(gsum[:], lg[:], AX.X, ALU.add))
                divide(lg[:], gsum[:])
                chain.link(nc.vector.tensor_tensor(gate[:], lg[:], hit[:, :, 0, :], ALU.mult))
                chain.link(nc.vector.tensor_reduce(gsum[:], gate[:], AX.X, ALU.add))
                chain.link(nc.vector.tensor_scalar(gsum[:], gsum[:], GATE_EPS, None, ALU.add))
                divide(gate[:], gsum[:])

                def weights(e):
                    bank, fr, u = take(("upT", e))
                    nc.vector.tensor_copy(upT[e % 2][:], ps[:, bank, :]).then_inc(fr, 1)
                    bank, fr, u = take(("downT", e))
                    nc.vector.tensor_copy(downT[e % 3][:], ps[:, bank, :]).then_inc(fr, 1)
                weights(0)
                for e in range(E1 + 1):
                    if e + 1 < E1:
                        weights(e + 1)
                    if e == 0:
                        continue
                    for h in range(2):
                        bank, fr, u = take(("y", e - 1, h))
                        for k, t in enumerate(transposed_tiles(h)):
                            y = ps[:, bank, D * k:D * (k + 1)]
                            g = gate[:, t, e - 1:e]
                            if e == 1:
                                last = nc.vector.tensor_scalar(acc[:, t, :], y, g, None, ALU.mult)
                            else:
                                last = nc.vector.scalar_tensor_tensor(acc[:, t, :], y, g, acc[:, t, :], ALU.mult, ALU.add)
                        last.then_inc(fr, 1)
                        v.wait_ge(fr, u + 1)
                chain.link(nc.vector.tensor_tensor(x_nat[:], x_nat[:], h_nat[:], ALU.add))
                layer_norm(v, chain, var_ready, root_done, 2, acc, acc, T["stats"], T["mv"], T["rstd"])
                nc.vector.tensor_tensor(acc[:], acc[:], x_nat[:], ALU.add).then_inc(result_ready, 1)

            @block.scalar
            def _(act):
                act.wait_ge(var_ready, 1)
                nc.scalar.activation(T["rstd"][:], T["rstd"][:], ACT.Sqrt).then_inc(root_done, 1)
                act.wait_ge(exp_ready, 1)
                nc.scalar.activation(lg[:], lg[:], ACT.Exp).then_inc(exp_done, 1)
                for e in range(E1):
                    for k in range(KI):
                        for h in range(2):
                            bank, fu, fr, u = ring(("h", e, k, h))
                            act.wait_ge(fu, u + 1)
                            nc.scalar.activation(H[e % 2][:, k, h * HALF:(h + 1) * HALF], ps[:, bank, 0:HALF],
                                                 ACT.Gelu).then_inc(fr, 1)
                act.wait_ge(var_ready, 2)
                nc.scalar.activation(T["rstd"][:], T["rstd"][:], ACT.Sqrt).then_inc(root_done, 1)

            @block.tensor
            def _(pe):
                def claim(name):
                    bank, fu, fr, u = ring(name)
                    at_least(pe, fr, u)
                    return bank, fu

                def copied(name):
                    bank, fu, fr, u = ring(name)
                    pe.wait_ge(fr, u + 1)
                pe.wait_ge(small_in, 48)
                bank, fu = claim(("gT",))
                nc.tensor.transpose(ps[:, bank, 0:E1], gw[:], ident[0:E1, 0:E1]).then_inc(fu, 1)
                for t in range(TT):
                    bank, fu = claim(("o", t))
                    for j in range(NJ):
                        last = nc.tensor.matmul(ps[:, bank, 0:D], AT1[:, j, 128 * t:128 * (t + 1)], wout[:, j, :],
                                                start=(j == 0), stop=(j == NJ - 1))
                    last.then_inc(fu, 1)
                pe.wait_ge(norm_ready, 1)
                for h in range(2):
                    bank, fu = claim(("T", h))
                    for k, t in enumerate(transposed_tiles(h)):
                        last = nc.tensor.transpose(ps[:, bank, 128 * k:128 * (k + 1)], h_nat[:, t, :], ident)
                    last.then_inc(fu, 1)
                for h in range(2):
                    copied(("T", h))
                bank, fu = claim(("lg",))
                for t in range(TT):
                    last = nc.tensor.matmul(ps[:, bank, E1 * t:E1 * (t + 1)], hT[:, 128 * t:128 * (t + 1)], gwT[:],
                                            start=True, stop=True)
                last.then_inc(fu, 1)
                pe.wait_ge(w_in, 32)

                def outputs(e):
                    for k in range(KI):
                        for h in range(2):
                            copied(("h", e, k, h))
                    for h in range(2):
                        bank, fu = claim(("y", e, h))
                        for n, t in enumerate(transposed_tiles(h)):
                            for k in range(KI):
                                last = nc.tensor.matmul(ps[:, bank, D * n:D * (n + 1)], H[e % 2][:, k, 128 * t:128 * (t + 1)],
                                                        downT[e % 3][:, 128 * k:128 * (k + 1)],
                                                        start=(k == 0), stop=(k == KI - 1))
                        last.then_inc(fu, 1)

                def weights(e):
                    bank, fu = claim(("upT", e))
                    for k in range(KI):
                        last = nc.tensor.transpose(ps[:, bank, 128 * k:128 * (k + 1)], up[:, e, k, :], ident)
                    last.then_inc(fu, 1)
                    bank, fu = claim(("downT", e))
                    for k in range(KI):
                        last = nc.tensor.transpose(ps[:, bank, 128 * k:128 * (k + 1)], down[:, e, 128 * k:128 * (k + 1)], ident)
                    last.then_inc(fu, 1)
                weights(0)
                for e in range(E1):
                    if e + 1 < E1:
                        weights(e + 1)
                    copied(("upT", e))
                    copied(("downT", e))
                    for k in range(KI):
                        for h in range(2):
                            bank, fu = claim(("h", e, k, h))
                            nc.tensor.matmul(ps[:, bank, 0:HALF], upT[e % 2][:, 128 * k:128 * (k + 1)],
                                             hT[:, h * HALF:(h + 1) * HALF], start=True, stop=True).then_inc(fu, 1)
                    if e:
                        outputs(e - 1)
                outputs(E1 - 1)


_INS = ["x", "ctx_1024", "L0_xattn_W_v", "L0_xattn_W_k", "L0_xattn_W_q", "L0_xattn_W_o", "L0_xattn_b_o",
        "L0_ffn_router_w", "L0_ffn_router_b", "L0_ffn_routed_w1", "L0_ffn_routed_w3", "L0_ffn_routed_w2",
        "L0_ffn_shared_w1", "L0_ffn_shared_w3", "L0_ffn_shared_w2", "L1_xattn_ln_m_g", "L1_xattn_ln_m_b",
        "L1_xattn_ln_l_g", "L1_xattn_ln_l_b", "L1_xattn_Wq", "L1_xattn_Wkv", "L1_xattn_Wout",
        "L1_ffn_gate_w", "L1_ffn_expert_bias", "L1_ffn_w_up", "L1_ffn_w_down"]


def constants():
    import numpy as np
    p = np.arange(128)
    c = np.zeros((128, CONSTS), np.float32)
    c[:, 0:128] = np.eye(128)
    c[:, 128:132] = (p[:, None] % 32) // HD0 == np.arange(4)[None, :]
    c[:, 132] = p < NQ
    c[:, 133] = p >= NQ
    c[:, 134:142] = np.arange(8)
    c[:, 142:142 + HEADS] = p[:, None] // HD0 == np.arange(HEADS)[None, :]
    for part in range(2):
        c[4 * HD0 * part:4 * HD0 * (part + 1), 142 + HEADS:CONSTS - 1] = np.eye(4 * HD0)
    c[VPARTS - 1, CONSTS - 1] = 1
    return c


def kernel(**inputs):
    import numpy as np
    import concourse.bacc as bacc
    from concourse.bass_utils import run_bass_kernel_spmd as run

    nc = bacc.Bacc("TRN2", target_bir_lowering=False, num_devices=1)
    arrays, aps = {}, {}
    for name, a in [(n, inputs[n]) for n in _INS] + [("consts", constants())]:
        a = np.ascontiguousarray(a)
        arrays[f"in_{name}_dram"] = a
        aps[name] = nc.dram_tensor(f"in_{name}_dram", a.shape, mybir.dt.from_np(a.dtype), kind="ExternalInput").ap()
    out = nc.dram_tensor("out_0_dram", (B, NQ, D), F32, kind="ExternalOutput").ap()
    build(nc, aps, out)
    r = run(nc, [arrays], core_ids=[0])
    return r.results[0]["out_0_dram"]
```
